# Optimizing a Trainium2 kernel written in Bass

```python
import numpy as np
import jax
import jax.numpy as jnp

def _softmax(x, axis=-1):
    return jax.nn.softmax(x, axis=axis)

def _gelu(x):
    return jax.nn.gelu(x, approximate=True)

def _silu(x):
    return jax.nn.silu(x)

def _sigmoid(x):
    return jax.nn.sigmoid(x)

def _layernorm(x, axis=-1, eps=1e-05):
    m = jnp.mean(x, axis=axis, keepdims=True)
    v = jnp.var(x, axis=axis, keepdims=True)
    return (x - m) / jnp.sqrt(v + eps)

def _scatter_add(tgt, idx, src, axis=0):
    return tgt.at[idx].add(src)

def _segment_sum(src, seg, n):
    return jax.ops.segment_sum(src, seg, n)
kernel_name = 'mk_gnn_preln_d4_gnn_r64_5777ef'

def setup_inputs(seed: int=0):
    np.random.seed(seed)
    _w = jnp.asarray

    def _rec_inputs():
        import jax
        import jax.numpy as jnp
        _gk = jax.random.key(seed)
        x = -0.000202 + 1 * jax.random.normal(jax.random.fold_in(_gk, 1), (100000, 64), jnp.float32)
        src = jax.random.randint(jax.random.fold_in(_gk, 2), (50000,), 0, 100000, jnp.int32)
        dst = jnp.minimum((100000 * jax.random.uniform(jax.random.fold_in(_gk, 3), (50000,)) ** 2.0).astype(jnp.int32), 99999)
        _o = jnp.argsort(dst, stable=True)
        src = src[_o]
        dst = dst[_o]
        edge_type_8 = jax.random.randint(jax.random.fold_in(_gk, 13), (50000,), 0, 8, jnp.int32)
        node_type_4 = jax.random.randint(jax.random.fold_in(_gk, 14), (100000,), 0, 4, jnp.int32)
        return (x, src, dst, edge_type_8, node_type_4)
    x, src, dst, edge_type_8, node_type_4 = _rec_inputs()

    def _L0_gnn_setup():
        import jax, jax.numpy as jnp
        import numpy as np
        N_TYPES = 4
        N_RELS = 8
        N, E, IN_DIM, OUT_DIM = (100000, 25000, 64, 64)
        SQRT_DK = float(np.sqrt(OUT_DIM))

        def _typed_matmul(x, W, node_type):
            out = jnp.zeros((x.shape[0], W.shape[-1]), x.dtype)
            for t in range(W.shape[0]):
                out = out + jnp.where((node_type == t)[:, None], x @ W[t], 0.0)
            return out
        key = jax.random.key(seed)
        ks = jax.random.split(key, 12)
        s = 0.05
        h = jax.random.normal(ks[0], (N, IN_DIM), jnp.float32)
        node_type = jax.random.randint(ks[1], (N,), 0, N_TYPES, jnp.int32)
        src = jax.random.randint(ks[2], (E,), 0, N, jnp.int32)
        dst = jax.random.randint(ks[3], (E,), 0, N, jnp.int32)
        etype = jax.random.randint(ks[4], (E,), 0, N_RELS, jnp.int32)
        k_lin = jax.random.normal(ks[5], (N_TYPES, IN_DIM, OUT_DIM), jnp.float32) * s
        q_lin = jax.random.normal(ks[6], (N_TYPES, IN_DIM, OUT_DIM), jnp.float32) * s
        v_lin = jax.random.normal(ks[7], (N_TYPES, IN_DIM, OUT_DIM), jnp.float32) * s
        a_lin = jax.random.normal(ks[8], (N_TYPES, OUT_DIM, OUT_DIM), jnp.float32) * s
        rel_att = jax.random.normal(ks[9], (N_RELS, OUT_DIM, OUT_DIM), jnp.float32) * s
        rel_msg = jax.random.normal(ks[10], (N_RELS, OUT_DIM, OUT_DIM), jnp.float32) * s
        rel_pri = jnp.ones((N_RELS,), jnp.float32)
        skip = jnp.ones((N_TYPES,), jnp.float32)
        return dict(h=h, node_type=node_type, src=src, dst=dst, etype=etype, k_lin=k_lin, q_lin=q_lin, v_lin=v_lin, a_lin=a_lin, rel_att=rel_att, rel_msg=rel_msg, rel_pri=rel_pri, skip=skip)
    _L0_gnn_all = _L0_gnn_setup()
    _L0_gnn_in = {k: v for k, v in _L0_gnn_all.items() if k in ('k_lin', 'q_lin', 'v_lin', 'a_lin', 'rel_att', 'rel_msg', 'rel_pri', 'skip')}
    del _L0_gnn_all

    def _L1_gnn_setup():
        import jax, jax.numpy as jnp
        import numpy as np
        N_NODES = 100000
        N_EDGES = 15625
        DIM = 64
        key = jax.random.key(seed)
        k1, k2, k3, k4, k5, k6 = jax.random.split(key, 6)
        h = jax.random.normal(k1, (N_NODES, DIM), dtype=jnp.float32)
        proj_cosim = jax.random.normal(k2, (DIM, DIM), dtype=jnp.float32) * np.sqrt(2.0 / DIM)
        W_ffn = jax.random.normal(k3, (DIM, DIM), dtype=jnp.float32) * np.sqrt(1.0 / DIM)
        b_ffn = jax.random.normal(k4, (DIM,), dtype=jnp.float32) * 0.01
        src = jax.random.randint(k5, (N_EDGES,), 0, N_NODES, dtype=jnp.int32)
        dst = jax.random.randint(k6, (N_EDGES,), 0, N_NODES, dtype=jnp.int32)
        return {'h': h, 'proj_cosim': proj_cosim, 'W_ffn': W_ffn, 'b_ffn': b_ffn, 'src': src, 'dst': dst}
    _L1_gnn_all = _L1_gnn_setup()
    _L1_gnn_in = {k: v for k, v in _L1_gnn_all.items() if k in ('proj_cosim', 'W_ffn', 'b_ffn')}
    del _L1_gnn_all

    def _L2_gnn_setup():
        import jax, jax.numpy as jnp
        import numpy as np
        N_NODES = 100000
        N_EDGES = 25000
        IN_DIM = 64
        HIDDEN_DIM = 128
        OUT_DIM = 64
        EPS = 0.0
        key = jax.random.key(seed)
        k_x, k_ei, k_w0, k_b0, k_w1, k_b1 = jax.random.split(key, 6)
        x = jax.random.normal(k_x, (N_NODES, IN_DIM), dtype=jnp.float32)
        edge_index = jax.random.randint(k_ei, (2, N_EDGES), 0, N_NODES, dtype=jnp.int64)
        lim0 = 1.0 / np.sqrt(IN_DIM)
        lim1 = 1.0 / np.sqrt(HIDDEN_DIM)
        W0 = jax.random.uniform(k_w0, (IN_DIM, HIDDEN_DIM), jnp.float32, -lim0, lim0)
        b0 = jax.random.uniform(k_b0, (HIDDEN_DIM,), jnp.float32, -lim0, lim0)
        W1 = jax.random.uniform(k_w1, (HIDDEN_DIM, OUT_DIM), jnp.float32, -lim1, lim1)
        b1 = jax.random.uniform(k_b1, (OUT_DIM,), jnp.float32, -lim1, lim1)
        return {'x': x, 'edge_index': edge_index, 'W0': W0, 'b0': b0, 'W1': W1, 'b1': b1}
    _L2_gnn_all = _L2_gnn_setup()
    _L2_gnn_in = {k: v for k, v in _L2_gnn_all.items() if k in ('W0', 'b0', 'W1', 'b1')}
    del _L2_gnn_all

    def _L3_gnn_setup():
        import jax, jax.numpy as jnp
        import numpy as np
        N = 50000
        E = 12500
        IN = 64
        H = 4
        D = 16
        OH = H * D
        SCALE = float(np.sqrt(IN))
        LN_EPS = 1e-05
        key = jax.random.key(seed)
        ks = jax.random.split(key, 16)
        w = 0.05
        return {'feats': jax.random.normal(ks[0], (N, IN), jnp.float32), 'Wq': jax.random.normal(ks[1], (IN, OH), jnp.float32) * w, 'bq': jnp.zeros((OH,), jnp.float32), 'Wk': jax.random.normal(ks[2], (IN, OH), jnp.float32) * w, 'bk': jnp.zeros((OH,), jnp.float32), 'Wv': jax.random.normal(ks[3], (IN, OH), jnp.float32) * w, 'bv': jnp.zeros((OH,), jnp.float32), 'Wo': jax.random.normal(ks[4], (OH, OH), jnp.float32) * w, 'bo': jnp.zeros((OH,), jnp.float32), 'Wf': jax.random.normal(ks[5], (IN, OH), jnp.float32) * w, 'bf': jnp.zeros((OH,), jnp.float32), 'gamma': jnp.ones((OH,), jnp.float32), 'beta': jnp.zeros((OH,), jnp.float32), 'src': jax.random.randint(ks[6], (E,), 0, N, jnp.int32), 'dst': jax.random.randint(ks[7], (E,), 0, N, jnp.int32)}
    _L3_gnn_all = _L3_gnn_setup()
    _L3_gnn_in = {k: v for k, v in _L3_gnn_all.items() if k in ('Wq', 'bq', 'Wk', 'bk', 'Wv', 'bv', 'Wo', 'bo', 'Wf', 'bf', 'gamma', 'beta')}
    del _L3_gnn_all
    return {'x': x, 'src': src, 'dst': dst, 'edge_type_8': edge_type_8, 'node_type_4': node_type_4, 'L0_gnn_k_lin': _L0_gnn_in['k_lin'], 'L0_gnn_q_lin': _L0_gnn_in['q_lin'], 'L0_gnn_v_lin': _L0_gnn_in['v_lin'], 'L0_gnn_a_lin': _L0_gnn_in['a_lin'], 'L0_gnn_rel_att': _L0_gnn_in['rel_att'], 'L0_gnn_rel_msg': _L0_gnn_in['rel_msg'], 'L0_gnn_rel_pri': _L0_gnn_in['rel_pri'], 'L0_gnn_skip': _L0_gnn_in['skip'], 'L1_gnn_proj_cosim': _L1_gnn_in['proj_cosim'], 'L1_gnn_W_ffn': _L1_gnn_in['W_ffn'], 'L1_gnn_b_ffn': _L1_gnn_in['b_ffn'], 'L2_gnn_W0': _L2_gnn_in['W0'], 'L2_gnn_b0': _L2_gnn_in['b0'], 'L2_gnn_W1': _L2_gnn_in['W1'], 'L2_gnn_b1': _L2_gnn_in['b1'], 'L3_gnn_Wq': _L3_gnn_in['Wq'], 'L3_gnn_bq': _L3_gnn_in['bq'], 'L3_gnn_Wk': _L3_gnn_in['Wk'], 'L3_gnn_bk': _L3_gnn_in['bk'], 'L3_gnn_Wv': _L3_gnn_in['Wv'], 'L3_gnn_bv': _L3_gnn_in['bv'], 'L3_gnn_Wo': _L3_gnn_in['Wo'], 'L3_gnn_bo': _L3_gnn_in['bo'], 'L3_gnn_Wf': _L3_gnn_in['Wf'], 'L3_gnn_bf': _L3_gnn_in['bf'], 'L3_gnn_gamma': _L3_gnn_in['gamma'], 'L3_gnn_beta': _L3_gnn_in['beta']}

def reference(x, src, dst, edge_type_8, node_type_4, L0_gnn_k_lin, L0_gnn_q_lin, L0_gnn_v_lin, L0_gnn_a_lin, L0_gnn_rel_att, L0_gnn_rel_msg, L0_gnn_rel_pri, L0_gnn_skip, L1_gnn_proj_cosim, L1_gnn_W_ffn, L1_gnn_b_ffn, L2_gnn_W0, L2_gnn_b0, L2_gnn_W1, L2_gnn_b1, L3_gnn_Wq, L3_gnn_bq, L3_gnn_Wk, L3_gnn_bk, L3_gnn_Wv, L3_gnn_bv, L3_gnn_Wo, L3_gnn_bo, L3_gnn_Wf, L3_gnn_bf, L3_gnn_gamma, L3_gnn_beta):
    import jax
    import jax.numpy as jnp

    def _L0_gnn_ref(h, node_type, src, dst, etype, k_lin, q_lin, v_lin, a_lin, rel_att, rel_msg, rel_pri, skip):
        import jax, jax.numpy as jnp
        import numpy as np
        N_TYPES = 4
        N_RELS = 8
        N, E, IN_DIM, OUT_DIM = (100000, 25000, 64, 64)
        SQRT_DK = float(np.sqrt(OUT_DIM))

        def _typed_matmul(x, W, node_type):
            out = jnp.zeros((x.shape[0], W.shape[-1]), x.dtype)
            for t in range(W.shape[0]):
                out = out + jnp.where((node_type == t)[:, None], x @ W[t], 0.0)
            return out
        k = _typed_matmul(h, k_lin, node_type)
        q = _typed_matmul(h, q_lin, node_type)
        v = _typed_matmul(h, v_lin, node_type)
        qW = jnp.einsum('nd,rde->rne', q, rel_att)
        t_edge = qW[etype, dst]
        score = jnp.sum(t_edge * k[src], axis=-1)
        logits = score * (rel_pri / SQRT_DK)[etype]
        m = jax.ops.segment_max(logits, dst, num_segments=N)
        ex = jnp.exp(logits - m[dst])
        den = jax.ops.segment_sum(ex, dst, num_segments=N)
        alpha = ex / jnp.where(den[dst] == 0, 1.0, den[dst])
        vW = jnp.einsum('nd,rde->rne', v, rel_msg)
        msg = vW[etype, src]
        agg = jax.ops.segment_sum(alpha[:, None] * msg, dst, num_segments=N)
        W_out = jax.nn.sigmoid(skip)[:, None, None] * a_lin
        return _typed_matmul(agg, W_out, node_type)

    def _L1_gnn_ref(h, proj_cosim, W_ffn, b_ffn, src, dst):
        import jax, jax.numpy as jnp
        import numpy as np
        N_NODES = 100000
        N_EDGES = 15625
        DIM = 64
        n_nodes = h.shape[0]
        h_src = h[src]
        h_dst = h[dst]
        scale = jnp.linalg.norm(h_src) * jnp.linalg.norm(h_dst) + 1e-06
        cosim = h_src * h_dst / scale
        cosim = jax.nn.relu(cosim @ proj_cosim)
        gate = jnp.exp(jnp.clip(cosim.sum(-1, keepdims=True), -5.0, 5.0))
        src_diff = jax.ops.segment_sum(h_src - h_dst, dst, num_segments=n_nodes)
        h_diff = jax.ops.segment_sum(src_diff[src] * gate, dst, num_segments=n_nodes)
        out = jax.nn.relu(h_diff @ W_ffn.T + b_ffn)
        return out

    def _L2_gnn_ref(x, edge_index, W0, b0, W1, b1):
        import jax, jax.numpy as jnp
        import numpy as np
        N_NODES = 100000
        N_EDGES = 25000
        IN_DIM = 64
        HIDDEN_DIM = 128
        OUT_DIM = 64
        EPS = 0.0
        src = edge_index[0]
        dst = edge_index[1]
        agg = jax.ops.segment_sum(x[src], dst, num_segments=x.shape[0])
        h = (1.0 + EPS) * x + agg
        h = jax.nn.relu(h @ W0 + b0)
        return h @ W1 + b1

    def _L3_gnn_ref(feats, Wq, bq, Wk, bk, Wv, bv, Wo, bo, Wf, bf, gamma, beta, src, dst):
        import jax, jax.numpy as jnp
        import numpy as np
        N = 50000
        E = 12500
        IN = 64
        H = 4
        D = 16
        OH = H * D
        SCALE = float(np.sqrt(IN))
        LN_EPS = 1e-05
        n = feats.shape[0]
        q = (feats @ Wq + bq).reshape(n, H, D)
        k = (feats @ Wk + bk).reshape(n, H, D)
        v = (feats @ Wv + bv).reshape(n, H, D)
        score = jnp.sum(k[src] * q[dst], axis=-1)
        score = jnp.exp(jnp.clip(score / SCALE, -5.0, 5.0))
        wv = jax.ops.segment_sum(v[src] * score[..., None], dst, num_segments=n)
        z = jax.ops.segment_sum(score, dst, num_segments=n)
        wv = wv / (z[..., None] + 1.0)
        o = wv.reshape(n, OH) @ Wo + bo
        h = feats @ Wf + bf + o
        mu = jnp.mean(h, axis=-1, keepdims=True)
        var = jnp.var(h, axis=-1, keepdims=True)
        ln = (h - mu) * jax.lax.rsqrt(var + LN_EPS) * gamma + beta
        return h + ln
    edge_index = jnp.stack([src, dst])
    h = jnp.maximum(_layernorm(x, axis=-1), 0.0)
    x = x + _L0_gnn_ref(h, node_type_4, src, dst, edge_type_8, L0_gnn_k_lin, L0_gnn_q_lin, L0_gnn_v_lin, L0_gnn_a_lin, L0_gnn_rel_att, L0_gnn_rel_msg, L0_gnn_rel_pri, L0_gnn_skip)
    h = jnp.maximum(_layernorm(x, axis=-1), 0.0)
    x = x + _L1_gnn_ref(h, L1_gnn_proj_cosim, L1_gnn_W_ffn, L1_gnn_b_ffn, src, dst)
    h = jnp.maximum(_layernorm(x, axis=-1), 0.0)
    x = x + _L2_gnn_ref(h, edge_index, L2_gnn_W0, L2_gnn_b0, L2_gnn_W1, L2_gnn_b1)
    h = jnp.maximum(_layernorm(x, axis=-1), 0.0)
    x = x + _L3_gnn_ref(h, L3_gnn_Wq, L3_gnn_bq, L3_gnn_Wk, L3_gnn_bk, L3_gnn_Wv, L3_gnn_bv, L3_gnn_Wo, L3_gnn_bo, L3_gnn_Wf, L3_gnn_bf, L3_gnn_gamma, L3_gnn_beta, src, dst)
    return x

_drawn_inputs = setup_inputs


def setup_inputs(seed=0):
    import zlib

    import numpy as np

    out = dict(_drawn_inputs(seed))
    spreads = {'L0_gnn_rel_pri': (1.0, 0.6),
     'L0_gnn_skip': (1.0, 0.6),
     'L3_gnn_bq': (0.0, 2.0),
     'L3_gnn_bk': (0.0, 2.0),
     'L3_gnn_bv': (0.0, 0.321),
     'L3_gnn_bo': (0.0, 0.1),
     'L3_gnn_bf': (0.0, 0.1),
     'L3_gnn_gamma': (1.0, 0.2),
     'L3_gnn_beta': (0.0, 0.1)}
    factors = {'L0_gnn_k_lin': 8.0,
     'L0_gnn_q_lin': 8.0,
     'L0_gnn_v_lin': 3.194,
     'L0_gnn_a_lin': 3.123,
     'L0_gnn_rel_att': 8.0,
     'L0_gnn_rel_msg': 3.153,
     'L1_gnn_proj_cosim': 64.0,
     'L1_gnn_b_ffn': 8.0,
     'L3_gnn_Wq': 8.0,
     'L3_gnn_Wk': 8.0}
    for name, (base, spread) in spreads.items():
        noise = np.random.default_rng([zlib.crc32(name.encode()), seed]).standard_normal(out[name].shape)
        drawn = base * np.exp(spread * noise) if base else spread * noise
        out[name] = jnp.asarray(drawn.astype(out[name].dtype))
    for name, factor in factors.items():
        out[name] = (out[name] * factor).astype(out[name].dtype)
    return out
```

```python
from contextlib import ExitStack

import numpy as np
import concourse.bass as bass
from concourse import mybir

P = 128
D = 64
NODES = 100000
EDGES = 50000
GE = 512
TU = GE // P
NG = -(-EDGES // GE)
EP = NG * GE
CH = EP // P
GN = 1024
RN = GN // P
NP = NG * GN
PADN = NODES
TW = 68
FAR = 8388608.0
BIG = 1.7e38
EPS = 1e-5
LAST = 2

F32 = mybir.dt.float32
I32 = mybir.dt.int32
ALU = mybir.AluOpType
ACT = mybir.ActivationFunctionType
AX = mybir.AxisListType.X

CONST_COLS = [("ident", 128), ("ones", 128), ("heads", 128), ("types", 4), ("rels", 4), ("eps", 1)]
WEIGHT_COLS = [
    ("q", 256), ("kv", 256), ("att", 256), ("msg", 256), ("pri", 4), ("a", 256), ("skip", 256),
    ("proj", 64), ("ffnT", 64), ("bffn", 1), ("bffn_row", 64),
    ("w0", 128), ("b0", 1), ("w1", 64), ("b1", 1), ("b1_top", 64),
    ("wq", 64), ("bq", 1), ("wk", 64), ("bk", 1), ("wv", 64), ("bv", 1),
    ("wo", 64), ("bo_top", 64), ("wf2", 128), ("bf_top", 64), ("gamma", 64), ("beta", 64),
]


def spans(cols):
    at, out = 0, {}
    for name, n in cols:
        out[name] = (at, at + n)
        at += n
    return out, at


CONST_AT, CONST_W = spans(CONST_COLS)
WEIGHT_AT, WEIGHT_W = spans(WEIGHT_COLS)


class Step:

    def __init__(self, n, k, s, u):
        self.n, self.k, self.s, self.u = n, k, s, u

    def back(self, lag):
        return Step(self.n - lag, self.k + (self.s - lag) // self.u, (self.s - lag) % self.u, self.u)

    def on(self):
        return not isinstance(self.n, int) or 0 <= self.n < NG

    def first(self):
        return isinstance(self.n, int) and self.n == 0


def run_groups(eng, body, u=2, tail=LAST):
    for n in range(2 * u):
        body(Step(n, n // u, n % u, u))
    with eng.Fori(2, NG // u) as i:
        for s in range(u):
            body(Step(i * u + s, i, s, u))
    for n in range(NG, NG + tail):
        body(Step(n, n // u, n % u, u))


def wait(eng, sem, value, passed=None):
    if isinstance(value, int) and value <= 0:
        return
    eng.wait_ge(sem, value)
    if passed is not None and not isinstance(value, int):
        eng.sem_inc(passed, 1)


class Chain:

    def __init__(self, eng, sem, step, per):
        self.eng, self.sem, self.base, self.per, self.i = eng, sem, step.n * per, per, 0

    def link(self, ins):
        self.i += 1
        assert self.i <= self.per
        ins.then_inc(self.sem, 1)
        self.eng.wait_ge(self.sem, self.base + self.i)

    def end(self):
        assert self.i == self.per, (self.i, self.per)


class Norm:

    def __init__(self, sb, sem, name, rows):
        self.rows = rows
        self.sum = sb(f"{name}_sum", [P, rows], F32)
        self.mean = sb(f"{name}_mean", [P, rows], F32)
        self.cent = sb(f"{name}_cent", [P, rows, D], F32)
        self.sq = sb(f"{name}_sq", [P, rows, D], F32)
        self.ss = sb(f"{name}_ss", [P, rows], F32)
        self.std = sb(f"{name}_std", [P, rows], F32)
        self.rstd = sb(f"{name}_rstd", [P, rows], F32)
        self.centered = sem(f"{name}_centered")
        self.squared = sem(f"{name}_squared")
        self.summed = sem(f"{name}_summed")
        self.rooted = sem(f"{name}_rooted")
        self.chain = sem(f"{name}_chain")

    def over(self, small):
        return small[:, :].unsqueeze(2).broadcast_to([P, self.rows, D])

    def center(self, v, c, x):
        c.link(v.tensor_reduce(self.sum[:, :], x, AX, ALU.add))
        c.link(v.tensor_scalar(self.mean[:, :], self.sum[:, :], 1.0 / D, None, ALU.mult))
        v.tensor_tensor(self.cent[:, :, :], x, self.over(self.mean), ALU.subtract).then_inc(self.centered, 1)

    def square(self, a, st):
        a.wait_ge(self.centered, st.n + 1)
        wait(a, self.summed, st.n)
        a.activation(self.sq[:, :, :], self.cent[:, :, :], ACT.Square).then_inc(self.squared, 1)

    def sumsq(self, v, st):
        v.wait_ge(self.squared, st.n + 1)
        v.tensor_reduce(self.ss[:, :], self.sq[:, :, :], AX, ALU.add).then_inc(self.summed, 1)

    def root(self, a, st, eps):
        a.wait_ge(self.summed, st.n + 1)
        a.activation(self.std[:, :], self.ss[:, :], ACT.Sqrt, bias=eps, scale=1.0 / D).then_inc(self.rooted, 1)

    def recip(self, v, c, st):
        v.wait_ge(self.rooted, st.n + 1)
        c.link(v.reciprocal(self.rstd[:, :], self.std[:, :]))

    def relu_to(self, v, out):
        return v.scalar_tensor_tensor(out=out, in0=self.cent[:, :, :], scalar=0.0, in1=self.over(self.rstd),
                                      op0=ALU.max, op1=ALU.mult)


class Scope:

    def __init__(self, nc, ctx, tag):
        self.nc, self.ctx, self.tag, self.used = nc, ctx, tag, []
        ctx.callback(self.clear)

    def clear(self):
        if self.used:
            self.nc.clear_and_free_semaphores(self.used)
            self.nc.all_engine_barrier()

    def sb(self, name, shape, dt=F32):
        return self.ctx.enter_context(self.nc.sbuf_tensor(f"{self.tag}_{name}", shape, dt))

    def ps(self, name, shape, dt=F32):
        return self.ctx.enter_context(self.nc.psum_tensor(f"{self.tag}_ps_{name}", shape, dt))

    def sem(self, name):
        self.used.append(self.nc.alloc_semaphore(f"{self.tag}_s_{name}"))
        return self.used[-1]

    def sems(self, name, n=2):
        return [self.sem(f"{name}{i}") for i in range(n)]

    def norm(self, name, rows):
        return Norm(self.sb, self.sem, f"{self.tag}_{name}", rows)


def edge_rows(table, at, width=D):
    return table[bass.ds(at, GE), :].rearrange("(u p) f -> p u f", p=P)


def node_rows(table, at):
    return table[bass.ds(at, GN), :].rearrange("(p j) f -> p j f", j=RN)


def over_parts(row, at, parts):
    return row[bass.ds(at, GE)].partition_broadcast(parts)


class Env:
    pass


def build(nc, x, node_type, src_idx, dst_idx, etype_row, dst_row, chunk_id, consts, weights, out):
    e = Env()
    e.x, e.out = x, out
    e.etype_row = etype_row

    def dram(name, shape, dt=F32):
        return nc.dram_tensor(name, shape, dt).ap()

    e.T0 = dram("t0", [NP, TW])
    e.XD = dram("xd", [EP, TW])
    e.VT = dram("vt", [D, EP])
    e.U1 = dram("u1", [2 * EP, D])
    e.SD = dram("sd", [EP, D])
    e.U2 = dram("u2", [EP + NP, D])
    e.U3 = dram("u3", [EP + NP, D])
    e.XH1 = dram("xh1", [P, EP])
    e.X2T = dram("x2t", [D, EP])
    e.XH3 = dram("xh3", [P, EP])
    e.same_prev = dram("same_prev", [EP])
    e.same_next = dram("same_next", [EP])
    e.logit = dram("logit", [EP])
    e.alpha = dram("alpha", [EP])
    e.cosim = dram("cosim", [EP])
    e.gate = dram("gate", [EP])
    e.meta_i = dram("meta_i", [2, EP], I32)
    e.meta_f = dram("meta_f", [2, EP])

    with ExitStack() as ctx:
        keep = Scope(nc, ctx, "keep")
        e.pe_passed, e.sp_passed, e.pool_passed = [keep.sem(f"{n}_passed") for n in ("pe", "sp", "pool")]
        e.cst = keep.sb("consts", [P, CONST_W])
        e.wts = keep.sb("weights", [P, WEIGHT_W])
        e.C = {n: e.cst[:, a:b] for n, (a, b) in CONST_AT.items()}
        e.W = {n: e.wts[:, a:b] for n, (a, b) in WEIGHT_AT.items()}
        e.relu_b = keep.sb("relu_b", [P, D])
        e.bfo = keep.sb("bfo", [P, D])
        e.gather0 = keep.sb("gather0", [P, NG, 2 * TU], I32)
        e.scat_ptr = keep.sb("scat_ptr", [P, CH], I32)
        e.scat_out = keep.sb("scat_out", [P, CH], I32)
        e.ptr_pay = keep.sb("ptr_pay", [P, CH, 2])
        e.ptrs = keep.sb("ptrs", [P, CH, 2])
        e.has = keep.sb("has", [P, CH])
        e.idx1 = keep.sb("idx1", [P, CH], I32)
        e.idxsd = keep.sb("idxsd", [P, CH], I32)
        e.idx2 = keep.sb("idx2", [P, CH], I32)
        e.segc = keep.sb("segc", [P, CH])
        e.segn = keep.sb("segn", [P, CH])
        meta(nc, e, dst_row, chunk_id, src_idx, dst_idx, consts, weights)
        node_table(nc, e, node_type)
        dense(nc, e)
        scores(nc, e)
        softmax(nc, e)
        attend(nc, e)
        difference(nc, e)
        propagate(nc, e)
        mlp(nc, e)
        heads(nc, e)


def meta(nc, e, dst_row, chunk_id, src_idx, dst_idx, consts, weights):
    with ExitStack() as ctx:
        s = Scope(nc, ctx, "meta")
        dst = s.sb("dst", [P, CH], I32)
        prv = s.sb("prev", [P, CH], I32)
        nxt = s.sb("next", [P, CH], I32)
        eid = s.sb("eid", [P, CH])
        dstf = s.sb("dstf", [P, CH])
        tmp = s.sb("tmp", [P, CH])
        start = s.sb("start", [P, CH])
        rows = s.sb("rows", [P, P + 1])
        ends = s.sb("ends", [P, P])
        carry = s.sb("carry", [P, 1])
        si = s.sb("si", [P, 2, CH], I32)
        sig = s.sb("sig", [P, 256])
        pt = s.ps("pt", [P, P])
        pc = s.ps("pc", [P, 1])
        loaded, chain, turned, carried, stored, back = [s.sem(n) for n in
                                                        ("loaded", "chain", "turned", "carried", "stored", "back")]
        sig_e, weights_in, row_done, meta_done = s.sem("sig_e"), s.sem("weights_in"), s.sem("row_done"), s.sem("meta_done")
        local_done = s.sem("local_done")

        with nc.Block() as block:
            @block.sync
            def _(sp):
                chunks = lambda off: dst_row[off:off + EP].rearrange("(p j) -> p j", j=CH)
                sp.dma_start(dst[:, :], chunks(1)).then_inc(loaded, 16)
                sp.dma_start(prv[:, :], chunks(0)).then_inc(loaded, 16)
                sp.dma_start(nxt[:, :], chunks(2)).then_inc(loaded, 16)
                sp.dma_start(eid[:, :], chunk_id).then_inc(loaded, 16)
                sp.dma_start(e.cst[:, :], consts).then_inc(loaded, 16)
                sp.dma_start(e.wts[:, :], weights).then_inc(weights_in, 16)
                sp.dma_start(e.gather0[:, :, 0:TU], src_idx).then_inc(back, 16)
                sp.dma_start(e.gather0[:, :, TU:2 * TU], dst_idx).then_inc(back, 16)
                wait(sp, meta_done, 1, e.sp_passed)
                rows_of = lambda t: t.rearrange("(p j) -> p j", j=CH)
                sp.dma_start(rows_of(e.same_prev), e.segc[:, :]).then_inc(stored, 16)
                sp.dma_start(rows_of(e.same_next), e.segn[:, :]).then_inc(stored, 16)
                sp.dma_start(rows_of(e.meta_f[0]), eid[:, :]).then_inc(stored, 16)
                sp.dma_start(rows_of(e.meta_f[1]), start[:, :]).then_inc(stored, 16)
                for i in range(2):
                    sp.dma_start(rows_of(e.meta_i[i]), si[:, i, :]).then_inc(stored, 16)
                wait(sp, stored, 96, e.sp_passed)
                major = lambda t: t.rearrange("(t p) -> p t", p=P)
                sp.dma_start(e.scat_ptr[:, :], major(e.meta_i[0]), allow_slow_non_contiguous=True).then_inc(back, 16)
                sp.dma_start(e.scat_out[:, :], major(e.meta_i[1]), allow_slow_non_contiguous=True).then_inc(back, 16)
                sp.dma_start(e.ptr_pay[:, :, 0], major(e.meta_f[0]), allow_slow_non_contiguous=True).then_inc(back, 16)
                sp.dma_start(e.ptr_pay[:, :, 1], major(e.meta_f[1]), allow_slow_non_contiguous=True).then_inc(back, 16)
                wait(sp, back, 96, e.sp_passed)

            @block.scalar
            def _(act):
                act.wait_ge(weights_in, 16)
                act.activation(sig[0:D, :], e.W["skip"][0:D, :], ACT.Sigmoid).then_inc(sig_e, 1)

            @block.vector
            def _(v):
                n = [0]

                def link(ins):
                    n[0] += 1
                    ins.then_inc(chain, 1)
                    v.wait_ge(chain, n[0])

                v.wait_ge(weights_in, 16)
                v.wait_ge(sig_e, 1)
                link(v.tensor_tensor(e.W["a"][0:D, :], e.W["a"][0:D, :], sig[0:D, :], ALU.mult))
                att = e.W["att"].rearrange("p (c m) -> p c m", c=4)
                pri = e.W["pri"].unsqueeze(2).broadcast_to([P, 4, D])
                link(v.tensor_tensor(att, att, pri, ALU.mult))
                link(v.tensor_scalar(e.W["att"], e.W["att"], 1.0 / 8.0, None, ALU.mult))
                link(v.tensor_scalar(e.relu_b[:, :], e.W["bffn_row"], 0.0, None, ALU.max))
                link(v.tensor_tensor(e.bfo[:, :], e.W["bf_top"], e.W["bo_top"], ALU.add))
                v.wait_ge(loaded, 80)
                link(v.tensor_tensor(e.segc[:, :], dst[:, :], prv[:, :], ALU.is_equal))
                link(v.tensor_tensor(e.segn[:, :], dst[:, :], nxt[:, :], ALU.is_equal))
                link(v.tensor_copy(dstf[:, :], dst[:, :]))
                link(v.tensor_scalar(tmp[:, :], dstf[:, :], TW / 2.0, TW / 2.0 - 1.0, ALU.mult, ALU.add))
                link(v.scalar_tensor_tensor(out=si[:, 0, :], in0=e.segn[:, :], scalar=FAR, in1=tmp[:, :],
                                            op0=ALU.mult, op1=ALU.add))
                link(v.scalar_tensor_tensor(out=si[:, 1, :], in0=e.segc[:, :], scalar=FAR, in1=dstf[:, :],
                                            op0=ALU.mult, op1=ALU.add))
                link(v.tensor_tensor(tmp[:, :], eid[:, :], e.segc[:, :], ALU.mult))
                link(v.tensor_tensor(tmp[:, :], eid[:, :], tmp[:, :], ALU.subtract))
                v.tensor_tensor_scan(start[:, :], tmp[:, :], tmp[:, :], 0.0, ALU.max, ALU.max).then_inc(local_done, 1)
                link(v.memset(rows[0:1, :], 0.0))
                v.wait_ge(turned, 1)
                link(v.tensor_copy(ends[0:1, :], pt[0:1, :]))
                v.tensor_tensor_scan(rows[0:1, 1:P + 1], ends[0:1, :], ends[0:1, :], 0.0,
                                     ALU.max, ALU.max).then_inc(row_done, 1)
                v.wait_ge(carried, 1)
                link(v.tensor_copy(carry[:, :], pc[:, :]))
                v.tensor_scalar(start[:, :], start[:, :], carry[:, 0:1], None, ALU.max).then_inc(meta_done, 1)

            @block.tensor
            def _(pe):
                wait(pe, loaded, 80, e.pe_passed)
                wait(pe, local_done, 1, e.pe_passed)
                pe.transpose(pt[0:1, :], start[:, CH - 1:CH], e.C["ident"]).then_inc(turned, 1)
                wait(pe, row_done, 1, e.pe_passed)
                pe.matmul(pc[:, :], rows[0:1, 0:P], e.C["ones"][0:1, 0:1], start=True, stop=True).then_inc(carried, 1)


def node_table(nc, e, node_type):
    U = 7
    with ExitStack() as ctx:
        s = Scope(nc, ctx, "tab")
        types = s.sb("types", [P, NG * RN], I32)
        row = [s.sb(f"row{i}", [P, RN, TW]) for i in range(U)]
        loaded, typed, stored = s.sems("loaded", U), s.sem("typed"), s.sems("stored", U)
        types_in, cleared = s.sem("types_in"), s.sem("cleared")
        with nc.Block() as block:
            @block.sync
            def _(sp):
                sp.dma_start(types[:, :], node_type).then_inc(types_in, 16)
                wait(sp, cleared, U, e.sp_passed)

                def body(st):
                    if st.on():
                        wait(sp, stored[st.s], 16 * st.k, e.sp_passed)
                        sp.dma_start(row[st.s][:, :, 0:D], node_rows(e.x, st.n * GN)).then_inc(loaded[st.s], 16)
                run_groups(sp, body, U, 0)

            @block.vector
            def _(v):
                for i in range(U):
                    v.memset(row[i][:, :, :], 0.0).then_inc(cleared, 1)
                v.wait_ge(types_in, 16)

                def body(st):
                    if st.on():
                        v.wait_ge(loaded[st.s], 16 * (st.k + 1))
                        v.tensor_copy(row[st.s][:, :, D], types[:, bass.ds(st.n * RN, RN)]).then_inc(typed, 1)
                run_groups(v, body, U, 0)

            @block.scalar
            def _(act):
                def body(st):
                    if st.on():
                        act.wait_ge(typed, st.n + 1)
                        act.dma_start(node_rows(e.T0, st.n * GN), row[st.s][:, :, :]).then_inc(stored[st.s], 16)
                run_groups(act, body, U, 0)
                for i in range(U):
                    act.wait_ge(stored[i], 16 * (NG // U))


def dense(nc, e):
    with ExitStack() as ctx:
        s = Scope(nc, ctx, "den")
        xin = [s.sb(f"x{i}", [P, RN, D]) for i in range(2)]
        x2 = [s.sb(f"x2{i}", [P, RN, D]) for i in range(2)]
        h2 = [s.sb(f"h2{i}", [P, RN, D]) for i in range(2)]
        x3 = [s.sb(f"x3{i}", [P, RN, D]) for i in range(2)]
        h3 = [s.sb(f"h3{i}", [P, RN, D]) for i in range(2)]
        x4 = [s.sb(f"x4{i}", [P, RN, D]) for i in range(2)]
        h2t = s.sb("h2t", [P, GE])
        h3t = s.sb("h3t", [P, GE])
        hid = s.sb("hid", [P, 2, GE])
        f1 = s.sb("f1", [P, RN, D])
        ps_t2, ps_t3 = s.ps("t2", [P, GE]), s.ps("t3", [P, GE])
        ps_hid = s.ps("hid", [P, 2, GE])
        ps_m, ps_h = [s.ps(f"m{i}", [P, RN, D]) for i in range(2)], s.ps("h", [P, RN, D])
        n2, n3, n4 = s.norm("n2", RN), s.norm("n3", RN), s.norm("n4", RN)
        x_in, h2_out, h3_out, x4_out = s.sems("x_in"), s.sems("h2_out"), s.sems("h3_out"), s.sems("x4_out")
        x2_done, h2_done, x3_done, h3_done, x4_done = [s.sem(n) for n in ("x2", "h2", "x3", "h3", "x4")]
        t2, t2_kept, hid_ready, hid_kept, m_ready = [s.sem(n) for n in ("t2", "t2k", "hidr", "hidk", "mr")]
        t3, t3_kept, h_ready = [s.sem(n) for n in ("t3", "t3k", "hr")]
        idx_c, ptr_out = s.sem("idx_c"), s.sems("ptr_out")
        sidx = [s.sb(f"sidx{i}", [P, TU], I32) for i in range(2)]
        spay = [s.sb(f"spay{i}", [P, TU, 2]) for i in range(2)]

        with nc.Block() as block:
            @block.gpsimd
            def _(pool):
                pairs = e.T0.rearrange("n (a b) -> (n a) b", b=2)

                def body(st):
                    if not st.on():
                        return
                    i = st.s
                    wait(pool, ptr_out[i], 16 * TU * st.k, e.pool_passed)
                    pool.tensor_copy(sidx[i][:, :], e.scat_ptr[:, bass.ds(st.n * TU, TU)]).then_inc(idx_c, 1)
                    pool.tensor_copy(spay[i][:, :, :], e.ptr_pay[:, bass.ds(st.n * TU, TU), :]).then_inc(idx_c, 1)
                    wait(pool, idx_c, (st.n + 1) * 2, e.pool_passed)
                    for u in range(TU):
                        pool.indirect_dma_start(pairs, bass.IndirectOffsetOnAxis(ap=sidx[i][:, u:u + 1], axis=0),
                                                spay[i][:, u, :], None, bounds_check=NP * TW // 2 - 1,
                                                oob_is_err=False).then_inc(ptr_out[i], 16)
                run_groups(pool, body, 2, 0)
                for i in range(2):
                    wait(pool, ptr_out[i], 16 * TU * (NG // 2), e.pool_passed)

            @block.sync
            def _(sp):
                def body(st):
                    if st.on():
                        wait(sp, x2_done, st.n - 1, e.sp_passed)
                        sp.dma_start(xin[st.s][:, :, :], node_rows(e.x, st.n * GN)).then_inc(x_in[st.s], 16)
                    b = st.back(1)
                    if b.on():
                        wait(sp, h2_done, b.n + 1, e.sp_passed)
                        sp.dma_start(node_rows(e.U2, b.n * GN + EP), h2[b.s][:, :, :]).then_inc(h2_out[b.s], 16)
                    b = st.back(3)
                    if b.on():
                        wait(sp, h3_done, b.n + 1, e.sp_passed)
                        sp.dma_start(node_rows(e.U3, b.n * GN + EP), h3[b.s][:, :, :]).then_inc(h3_out[b.s], 16)
                    b = st.back(4)
                    if b.on():
                        wait(sp, x4_done, b.n + 1, e.sp_passed)
                        sp.dma_start(node_rows(e.out, b.n * GN), x4[b.s][:, :, :]).then_inc(x4_out[b.s], 16)
                run_groups(sp, body, 2, 4)
                for sems in (h2_out, h3_out, x4_out):
                    for i in range(2):
                        wait(sp, sems[i], 16 * (NG // 2), e.sp_passed)

            @block.vector
            def _(v):
                def body(st):
                    d, f, g = st, st.back(2), st.back(3)
                    cd, cf, cg = (Chain(v, n.chain, b, k) for n, b, k in ((n2, d, 3), (n3, f, 3), (n4, g, 7)))
                    if f.on():
                        v.wait_ge(m_ready, f.n + 1)
                        v.tensor_tensor(x3[f.s][:, :, :], ps_m[f.s][:, :, :], x2[f.s][:, :, :], ALU.add).then_inc(x3_done, 1)
                        v.wait_ge(x3_done, f.n + 1)
                        n3.center(v, cf, x3[f.s][:, :, :])
                    if d.on():
                        v.wait_ge(x_in[d.s], 16 * (d.k + 1))
                        v.tensor_tensor(x2[d.s][:, :, :], xin[d.s][:, :, :],
                                        e.relu_b[:, :].unsqueeze(1).broadcast_to([P, RN, D]), ALU.add).then_inc(x2_done, 1)
                        v.wait_ge(x2_done, d.n + 1)
                        n2.center(v, cd, x2[d.s][:, :, :])
                    if g.on():
                        v.wait_ge(h_ready, g.n + 1)
                        n4.center(v, cg, ps_h[:, :, :])
                    if f.on():
                        n3.sumsq(v, f)
                    if d.on():
                        n2.sumsq(v, d)
                    if g.on():
                        n4.sumsq(v, g)
                    if f.on():
                        n3.recip(v, cf, f)
                        wait(v, h3_out[f.s], 16 * f.k)
                        n3.relu_to(v, h3[f.s][:, :, :]).then_inc(h3_done, 1)
                        cf.end()
                    if d.on():
                        n2.recip(v, cd, d)
                        wait(v, h2_out[d.s], 16 * d.k)
                        n2.relu_to(v, h2[d.s][:, :, :]).then_inc(h2_done, 1)
                        cd.end()
                    if g.on():
                        n4.recip(v, cg, g)
                        cg.link(v.tensor_tensor(f1[:, :, :], n4.cent[:, :, :], n4.over(n4.rstd), ALU.mult))
                        cg.link(v.tensor_tensor(f1[:, :, :], f1[:, :, :],
                                                e.W["gamma"].unsqueeze(1).broadcast_to([P, RN, D]), ALU.mult))
                        cg.link(v.tensor_tensor(f1[:, :, :], f1[:, :, :], ps_h[:, :, :], ALU.add))
                        cg.link(v.tensor_tensor(f1[:, :, :], f1[:, :, :], x3[g.s][:, :, :], ALU.add))
                        wait(v, x4_out[g.s], 16 * g.k)
                        v.tensor_tensor(x4[g.s][:, :, :], f1[:, :, :],
                                        e.W["beta"].unsqueeze(1).broadcast_to([P, RN, D]), ALU.add).then_inc(x4_done, 1)
                        cg.end()
                run_groups(v, body, 2, 3)

            @block.scalar
            def _(a):
                eps = e.C["eps"]

                def body(st):
                    d, f, g = st, st.back(2), st.back(3)
                    for norm, b in ((n3, f), (n2, d), (n4, g)):
                        if b.on():
                            norm.square(a, b)
                    for norm, b in ((n3, f), (n2, d), (n4, g)):
                        if b.on():
                            norm.root(a, b, eps)
                    if f.on():
                        a.wait_ge(t3, f.n + 1)
                        a.copy(h3t[:, :], ps_t3[:, :]).then_inc(t3_kept, 1)
                    if d.on():
                        a.wait_ge(t2, d.n + 1)
                        a.copy(h2t[:, :], ps_t2[:, :]).then_inc(t2_kept, 1)
                    if d.on():
                        a.wait_ge(hid_ready, d.n + 1)
                        a.activation(hid[:, :, :], ps_hid[:, :, :], ACT.Relu, bias=e.W["b0"]).then_inc(hid_kept, 1)
                run_groups(a, body, 2, 3)

            @block.tensor
            def _(pe):
                def body(st):
                    d, f = st, st.back(2)
                    if f.on():
                        wait(pe, h3_done, f.n + 1, e.pe_passed)
                        for c in range(4):
                            m = pe.transpose(ps_t3[:, c * P:(c + 1) * P],
                                             h3[f.s][:, 2 * c:2 * c + 2, :].rearrange("p a f -> p (a f)"), e.C["ident"])
                        m.then_inc(t3, 1)
                    if d.on():
                        wait(pe, h2_done, d.n + 1, e.pe_passed)
                        for c in range(4):
                            m = pe.transpose(ps_t2[:, c * P:(c + 1) * P],
                                             h2[d.s][:, 2 * c:2 * c + 2, :].rearrange("p a f -> p (a f)"), e.C["ident"])
                        m.then_inc(t2, 1)
                    if f.on():
                        wait(pe, t3_kept, f.n + 1, e.pe_passed)
                        wait(pe, x4_done, f.n, e.pe_passed)
                        for j in range(RN):
                            pe.matmul(ps_h[:, j, :], e.C["ones"], e.bfo[:, :], start=(j == 0), stop=False,
                                      skip_group_check=True)
                        for c in range(4):
                            m = pe.matmul(ps_h[:, 2 * c:2 * c + 2, :], h3t[:, c * P:(c + 1) * P],
                                          e.W["wf2"], start=False, stop=(c == 3), skip_group_check=True)
                        m.then_inc(h_ready, 1)
                    if d.on():
                        wait(pe, t2_kept, d.n + 1, e.pe_passed)
                        for a in range(2):
                            m = pe.matmul(ps_hid[:, a, :], e.W["w0"][64 * a:64 * a + 64, :], h2t[64 * a:64 * a + 64, :],
                                          start=True, stop=True)
                        m.then_inc(hid_ready, 1)
                        wait(pe, x3_done, d.n - 1, e.pe_passed)
                        for j in range(RN):
                            pe.matmul(ps_m[d.s][:, j, :], e.C["ones"], e.W["b1_top"], start=(j == 0), stop=False,
                                      skip_group_check=True)
                        wait(pe, hid_kept, d.n + 1, e.pe_passed)
                        for j in range(RN):
                            a, c = j % 2, j // 2
                            m = pe.matmul(ps_m[d.s][:, j, :], hid[:, a, c * P:(c + 1) * P], e.W["w1"],
                                          start=False, stop=(j == RN - 1), skip_group_check=True)
                        m.then_inc(m_ready, 1)
                run_groups(pe, body, 2, 3)


def scores(nc, e):
    with ExitStack() as ctx:
        s = Scope(nc, ctx, "sc")
        R = 2 * TU
        idx = [s.sb(f"idx{i}", [P, R], I32) for i in range(2)]
        xg = [s.sb(f"xg{i}", [P, R, TW]) for i in range(2)]
        hid = [s.sb(f"h{i}", [P, R, D]) for i in range(2)]
        onehot = s.sb("onehot", [P, R, 4])
        hx = [s.sb(f"hx{i}", [P, R, 4, D]) for i in range(2)]
        ht = s.sb("ht", [P, 4, GE])
        et = [s.sb(f"et{i}", [P, GE], I32) for i in range(2)]
        qx = s.sb("qx", [P, 4, GE])
        kt = s.sb("kt", [D, GE])
        vt = [s.sb(f"vt{i}", [P, GE]) for i in range(2)]
        prod = s.sb("prod", [D, GE])
        lrow = [s.sb(f"lrow{i}", [1, GE]) for i in range(2)]
        ps_t = s.ps("t", [P, 4, GE])
        ps_q, ps_kv, ps_r, ps_l = s.ps("q", [P, GE]), s.ps("kv", [P, GE]), s.ps("r", [D, GE]), s.ps("l", [1, GE])
        nrm = s.norm("n", R)
        hop = s.sem("hop")
        gathered, et_in, h_out, xd_out, v_out, l_out = [s.sems(n) for n in ("g", "et", "ho", "xd", "vo", "lo")]
        idx_c, h_done, hx_done, turned, ht_kept, qkv_ready = [s.sem(n) for n in ("ic", "h", "hx", "tu", "hk", "qkv")]
        q_used, r_ready, k_kept, v_kept, prod_done, l_ready, l_kept = [s.sem(n) for n in ("qu", "rr", "kk", "vk", "pd", "lr", "lk")]
        ptr_c = s.sem("ptr")

        with nc.Block() as block:
            @block.gpsimd
            def _(pool):
                def body(st):
                    if not st.on():
                        return
                    i = st.s
                    wait(pool, gathered[i], 16 * R * st.k, e.pool_passed)
                    pool.tensor_copy(idx[i][:, :], e.gather0[:, st.n, :] if isinstance(st.n, int) else
                                     e.gather0[:, bass.ds(st.n, 1), :].rearrange("p a r -> p (a r)")).then_inc(idx_c, 1)
                    wait(pool, idx_c, st.n + 1, e.pool_passed)
                    wait(pool, h_done, st.n - 1, e.pool_passed)
                    wait(pool, ptr_c, st.n - 1, e.pool_passed)
                    wait(pool, xd_out[i], 16 * st.k, e.pool_passed)
                    for u in range(R):
                        pool.indirect_dma_start(xg[i][:, u, :], None, e.T0,
                                                bass.IndirectOffsetOnAxis(ap=idx[i][:, u:u + 1], axis=0),
                                                bounds_check=NP - 1, oob_is_err=False).then_inc(gathered[i], 16)
                run_groups(pool, body, 2, 0)

            @block.sync
            def _(sp):
                def body(st):
                    if st.on():
                        wait(sp, r_ready, st.n - 1, e.sp_passed)
                        sp.dma_start(et[st.s][:, :], over_parts(e.etype_row, st.n * GE, P)).then_inc(et_in[st.s], 16)
                        wait(sp, gathered[st.s], 16 * R * (st.k + 1), e.sp_passed)
                        sp.dma_start(edge_rows(e.XD, st.n * GE, TW), xg[st.s][:, TU:R, :]).then_inc(xd_out[st.s], 16)
                        wait(sp, h_done, st.n + 1, e.sp_passed)
                        sp.dma_start(edge_rows(e.U1, st.n * GE + EP), hid[st.s][:, 0:TU, :]).then_inc(h_out[st.s], 16)
                    b = st.back(1)
                    if b.on():
                        wait(sp, v_kept, b.n + 1, e.sp_passed)
                        sp.dma_start(e.VT[:, bass.ds(b.n * GE, GE)], vt[b.s][D:P, :]).then_inc(v_out[b.s], 16)
                    b = st.back(2)
                    if b.on():
                        wait(sp, l_kept, b.n + 1, e.sp_passed)
                        sp.dma_start(e.logit[bass.ds(b.n * GE, GE)].unsqueeze(0), lrow[b.s][0:1, :]).then_inc(l_out[b.s], 16)
                run_groups(sp, body)
                for sems in (xd_out, h_out, v_out, l_out):
                    for i in range(2):
                        wait(sp, sems[i], 16 * (NG // 2), e.sp_passed)

            @block.vector
            def _(v):
                def body(st):
                    b = st.back(1)
                    c = Chain(v, nrm.chain, st, 4)
                    if st.on():
                        v.wait_ge(gathered[st.s], 16 * R * (st.k + 1))
                        x = xg[st.s][:, :, 0:D]
                        nrm.center(v, c, x)
                        v.tensor_copy(e.ptrs[:, bass.ds(st.n * TU, TU), :], xg[st.s][:, 0:TU, TW - 2:TW]).then_inc(ptr_c, 1)
                        wait(v, hx_done, st.n)
                        c.link(v.tensor_tensor(onehot[:, :, :], e.C["types"].unsqueeze(1).broadcast_to([P, R, 4]),
                                               xg[st.s][:, :, D:D + 1].broadcast_to([P, R, 4]), ALU.is_equal))
                    if b.on():
                        v.wait_ge(qkv_ready, b.n + 1)
                        v.wait_ge(et_in[b.s], 16 * (b.k + 1))
                        wait(v, r_ready, b.n)
                        for r in range(4):
                            m = v.scalar_tensor_tensor(out=qx[:, r, :], in0=et[b.s][:, :], scalar=e.C["rels"][:, r:r + 1],
                                                       in1=ps_q[:, :], op0=ALU.is_equal, op1=ALU.mult)
                        m.then_inc(q_used, 1)
                    if st.on():
                        nrm.sumsq(v, st)
                        nrm.recip(v, c, st)
                        wait(v, h_out[st.s], 16 * st.k)
                        nrm.relu_to(v, hid[st.s][:, :, :]).then_inc(h_done, 1)
                        v.wait_ge(h_done, st.n + 1)
                        wait(v, turned, 2 * st.n - 2)
                        for r in range(2):
                            v.tensor_tensor(hx[st.s][:, r * TU:(r + 1) * TU, :, :],
                                            hid[st.s][:, r * TU:(r + 1) * TU, :].unsqueeze(2).broadcast_to([P, TU, 4, D]),
                                            onehot[:, r * TU:(r + 1) * TU, :].unsqueeze(3).broadcast_to([P, TU, 4, D]),
                                            ALU.mult).then_inc(hx_done, 1) if r == 1 else \
                                v.tensor_tensor(hx[st.s][:, 0:TU, :, :],
                                                hid[st.s][:, 0:TU, :].unsqueeze(2).broadcast_to([P, TU, 4, D]),
                                                onehot[:, 0:TU, :].unsqueeze(3).broadcast_to([P, TU, 4, D]), ALU.mult)
                        c.end()
                    if b.on():
                        v.wait_ge(r_ready, b.n + 1)
                        v.wait_ge(k_kept, b.n + 1)
                        wait(v, l_ready, b.n)
                        v.tensor_tensor(prod[:, :], ps_r[:, :], kt[:, :], ALU.mult).then_inc(prod_done, 1)
                run_groups(v, body)

            @block.scalar
            def _(a):
                def body(st):
                    b = st.back(1)
                    if st.on():
                        nrm.square(a, st)
                        nrm.root(a, st, e.C["eps"])
                    if b.on():
                        a.wait_ge(qkv_ready, b.n + 1)
                        wait(a, prod_done, b.n)
                        a.copy(kt[:, :], ps_kv[0:D, :]).then_inc(k_kept, 1)
                        wait(a, v_out[b.s], 16 * b.k)
                        a.copy(vt[b.s][D:P, :], ps_kv[D:P, :]).then_inc(v_kept, 1)
                    if st.on():
                        for r in range(2):
                            a.wait_ge(turned, 2 * st.n + r + 1)
                            a.copy(ht[:, 2 * r:2 * r + 2, :], ps_t[:, 2 * r:2 * r + 2, :]).then_inc(ht_kept, 1)
                    if b.on():
                        a.wait_ge(l_ready, b.n + 1)
                        wait(a, l_out[b.s], 16 * b.k)
                        a.copy(lrow[b.s][0:1, :], ps_l[0:1, :]).then_inc(l_kept, 1)
                run_groups(a, body)

            @block.tensor
            def _(pe):
                def body(st):
                    b = st.back(1)
                    if b.on():
                        wait(pe, q_used, b.n + 1, e.pe_passed)
                        wait(pe, prod_done, b.n, e.pe_passed)
                        for r in range(4):
                            m = pe.matmul(ps_r[:, :], e.W["att"][:, r * D:(r + 1) * D], qx[:, r, :], start=(r == 0), stop=(r == 3))
                        m.then_inc(r_ready, 1)
                    if st.on():
                        wait(pe, hx_done, st.n + 1, e.pe_passed)
                        for side in range(2):
                            for u in range(TU):
                                for c in range(2):
                                    m = pe.transpose(ps_t[:, 2 * side + c, u * P:(u + 1) * P],
                                                     hx[st.s][:, (1 - side) * TU + u, 2 * c:2 * c + 2, :].rearrange("p a f -> p (a f)"),
                                                     e.C["ident"])
                            m.then_inc(turned, 1)
                    if b.on():
                        wait(pe, prod_done, b.n + 1, e.pe_passed)
                        wait(pe, l_kept, b.n, e.pe_passed)
                        pe.matmul(ps_l[:, :], e.C["ones"][0:D, 0:1], prod[:, :], start=True, stop=True).then_inc(l_ready, 1)
                    if st.on():
                        wait(pe, ht_kept, 2 * st.n + 1, e.pe_passed)
                        for c in range(2):
                            pe.matmul(ps_q[:, :], e.W["q"][:, c * P:(c + 1) * P], ht[:, c, :], start=(c == 0), stop=(c == 1))
                        wait(pe, ht_kept, 2 * st.n + 2, e.pe_passed)
                        wait(pe, v_kept, st.n, e.pe_passed)
                        for c in range(2):
                            m = pe.matmul(ps_kv[:, :], e.W["kv"][:, c * P:(c + 1) * P], ht[:, 2 + c, :], start=(c == 0), stop=(c == 1))
                        m.then_inc(qkv_ready, 1)
                run_groups(pe, body)


def softmax(nc, e):
    with ExitStack() as ctx:
        s = Scope(nc, ctx, "sm")
        lg, a1, a2, a3, a4, m = [s.sb(n, [P, CH]) for n in ("lg", "a1", "a2", "a3", "a4", "m")]
        ones = s.sb("ones", [P, CH])
        ends = s.sb("ends", [1, 2, P])
        srcs = s.sb("srcs", [P, NG, TU])
        carried = s.sb("carried", [1, P + 1])
        carry = s.sb("carry", [P, 1])
        eid = s.sb("eid", [P, CH], I32)
        eidf = s.sb("eidf", [P, CH])
        ps_a, ps_b, ps_c = s.ps("a", [1, P]), s.ps("b", [1, P]), s.ps("c", [P, 1])
        loaded, stored, chain, p_ready, iot = s.sem("loaded"), s.sem("stored"), s.sem("chain"), s.sem("pr"), s.sem("iot")
        local, turned, row_done, back, alpha_done = [s.sem(n) for n in ("local", "turned", "row", "back", "alpha")]
        max_done = s.sem("maxd")

        with nc.Block() as block:
            @block.sync
            def _(sp):
                sp.dma_start(lg[:, :], e.logit.rearrange("(p j) -> p j", j=CH)).then_inc(loaded, 16)
                wait(sp, alpha_done, 1, e.sp_passed)
                sp.dma_start(e.alpha.rearrange("(p j) -> p j", j=CH), a1[:, :]).then_inc(stored, 16)
                wait(sp, stored, 16, e.sp_passed)

            @block.gpsimd
            def _(pool):
                pool.iota(eid[:, :], [[P, CH]], base=0, channel_multiplier=1).then_inc(iot, 1)

            @block.scalar
            def _(a):
                a.wait_ge(max_done, 1)
                a.activation(m[:, :], lg[:, :], ACT.Exp).then_inc(p_ready, 1)

            @block.tensor
            def _(pe):
                for i in range(4):
                    wait(pe, local, i + 1, e.pe_passed)
                    col = CH - 1 if i % 2 == 0 else 0
                    val = a1 if i % 2 == 0 else a3
                    pre = a2 if i % 2 == 0 else a4
                    pe.transpose(ps_a[:, :], val[:, col:col + 1], e.C["ident"])
                    pe.transpose(ps_b[:, :], pre[:, col:col + 1], e.C["ident"]).then_inc(turned, 1)
                    wait(pe, row_done, i + 1, e.pe_passed)
                    row = carried[0:1, 0:P] if i % 2 == 0 else carried[0:1, 1:P + 1]
                    pe.matmul(ps_c[:, :], row, e.C["ones"][0:1, 0:1], start=True, stop=True).then_inc(back, 1)

            @block.vector
            def _(v):
                n = [0]

                def link(ins):
                    n[0] += 1
                    ins.then_inc(chain, 1)
                    v.wait_ge(chain, n[0])

                def seg_scan(i, val, pre, x, is_max):
                    rev = slice(None, None, -1 if i % 2 else 1)
                    same = e.segn if i % 2 else e.segc
                    link(v.tensor_tensor_scan(pre[:, rev], same[:, rev], ones[:, :], 1.0, ALU.mult, ALU.mult))
                    if is_max:
                        link(v.tensor_scalar(val[:, :], same[:, :], -1.0, BIG, ALU.add, ALU.mult))
                        v.tensor_tensor_scan(val[:, rev], val[:, rev], x[:, rev], -BIG, ALU.add, ALU.max).then_inc(local, 1)
                    else:
                        v.tensor_tensor_scan(val[:, rev], same[:, rev], x[:, rev], 0.0, ALU.mult, ALU.add).then_inc(local, 1)
                    v.wait_ge(turned, i + 1)
                    none = -BIG if is_max else 0.0
                    link(v.memset(carried[0:1, :], none))
                    link(v.tensor_copy(ends[0:1, 0, :], ps_a[:, :]))
                    out = carried[0:1, 1:P + 1] if i % 2 == 0 else carried[0:1, 0:P]
                    if is_max:
                        link(v.tensor_scalar(ends[0:1, 1, :], ps_b[:, :], -1.0, BIG, ALU.add, ALU.mult))
                    else:
                        link(v.tensor_copy(ends[0:1, 1, :], ps_b[:, :]))
                    v.tensor_tensor_scan(out[:, rev], ends[0:1, 1, rev], ends[0:1, 0, rev], none,
                                         ALU.add if is_max else ALU.mult, ALU.max if is_max else ALU.add).then_inc(row_done, 1)
                    v.wait_ge(back, i + 1)
                    link(v.tensor_copy(carry[:, :], ps_c[:, :]))
                    if is_max:
                        link(v.tensor_scalar(pre[:, :], pre[:, :], -1.0, BIG, ALU.add, ALU.mult))
                        link(v.scalar_tensor_tensor(out=val[:, :], in0=pre[:, :], scalar=carry[:, 0:1], in1=val[:, :],
                                                    op0=ALU.add, op1=ALU.max))
                    else:
                        link(v.scalar_tensor_tensor(out=val[:, :], in0=pre[:, :], scalar=carry[:, 0:1], in1=val[:, :],
                                                    op0=ALU.mult, op1=ALU.add))

                link(v.memset(ones[:, :], 1.0))
                v.wait_ge(loaded, 16)
                seg_scan(0, a1, a2, lg, True)
                seg_scan(1, a3, a4, lg, True)
                link(v.tensor_tensor(a1[:, :], a1[:, :], a3[:, :], ALU.max))
                v.tensor_tensor(lg[:, :], lg[:, :], a1[:, :], ALU.subtract).then_inc(max_done, 1)
                v.wait_ge(p_ready, 1)
                seg_scan(2, a1, a2, m, False)
                seg_scan(3, a3, a4, m, False)
                link(v.tensor_tensor(a1[:, :], a1[:, :], a3[:, :], ALU.add))
                link(v.tensor_tensor(a1[:, :], a1[:, :], m[:, :], ALU.subtract))
                link(v.tensor_scalar(a2[:, :], a1[:, :], 0.0, None, ALU.is_equal))
                link(v.tensor_tensor(a1[:, :], a1[:, :], a2[:, :], ALU.add))
                link(v.reciprocal(a1[:, :], a1[:, :]))
                v.tensor_tensor(a1[:, :], a1[:, :], m[:, :], ALU.mult).then_inc(alpha_done, 1)

                v.wait_ge(iot, 1)
                link(v.tensor_copy(eidf[:, :], eid[:, :]))
                last, frst = e.ptrs[:, :, 0], e.ptrs[:, :, 1]
                link(v.tensor_scalar(e.has[:, :], last, 1.0, None, ALU.min))

                def choose(out, ptr, base, off):
                    link(v.tensor_scalar(a4[:, :], base, float(off), None, ALU.add))
                    link(v.tensor_tensor(a3[:, :], ptr, a4[:, :], ALU.subtract))
                    link(v.scalar_tensor_tensor(out=a3[:, :], in0=a3[:, :], scalar=-1.0, in1=e.has[:, :],
                                                op0=ALU.add, op1=ALU.mult))
                    link(v.tensor_tensor(out[:, :], a3[:, :], a4[:, :], ALU.add))

                choose(e.idx1, last, eidf[:, :], EP)
                choose(e.idxsd, frst, eidf[:, :], 0)
                link(v.tensor_copy(srcs[:, :, :], e.gather0[:, :, 0:TU]))
                choose(e.idx2, last, srcs[:, :, :].rearrange("p a b -> p (a b)"), EP)


def attend(nc, e):
    with ExitStack() as ctx:
        s = Scope(nc, ctx, "at")
        vin = [s.sb(f"v{i}", [P, GE]) for i in range(2)]
        et = [s.sb(f"et{i}", [P, GE], I32) for i in range(2)]
        al = [s.sb(f"al{i}", [D, GE]) for i in range(2)]
        same = [s.sb(f"same{i}", [D, GE]) for i in range(2)]
        xd = [s.sb(f"xd{i}", [P, TU, TW]) for i in range(2)]
        vx = s.sb("vx", [P, 4, GE])
        am = s.sb("am", [D, GE])
        agg = [s.sb(f"agg{i}", [D, GE]) for i in range(2)]
        onehot = s.sb("onehot", [P, TU, 4])
        ysel = s.sb("ysel", [P, TU, 4, D])
        yy = s.sb("yy", [P, TU, D])
        hx = [s.sb(f"hx{i}", [P, TU, 2 * D]) for i in range(2)]
        xh = [s.sb(f"xh{i}", [P, GE]) for i in range(2)]
        ps_m, ps_y, ps_t = s.ps("m", [D, GE]), s.ps("y", [P, TU, 4, D]), s.ps("t", [P, GE])
        nrm = s.norm("n", TU)
        v_in, et_in, al_in, same_in, xd_in, h_out, xh_out = [s.sems(n) for n in ("v", "et", "al", "sa", "xd", "ho", "xho")]
        vx_done, m_ready, am_done, agg_done, y_ready, h_done, turned, kept, y_used = [
            s.sem(n) for n in ("vx", "mr", "am", "ag", "yr", "h", "tu", "kept", "yu")]

        with nc.Block() as block:
            @block.sync
            def _(sp):
                def body(st):
                    if st.on():
                        i, at = st.s, st.n * GE
                        wait(sp, vx_done, st.n - 1, e.sp_passed)
                        for half in range(2):
                            sp.dma_start(vin[i][half * D:(half + 1) * D, :], e.VT[:, bass.ds(at, GE)]).then_inc(v_in[i], 16)
                        sp.dma_start(et[i][:, :], over_parts(e.etype_row, at, P)).then_inc(et_in[i], 16)
                        wait(sp, agg_done, st.n - 1, e.sp_passed)
                        sp.dma_start(al[i][:, :], over_parts(e.alpha, at, D)).then_inc(al_in[i], 16)
                        sp.dma_start(same[i][:, :], over_parts(e.same_prev, at, D)).then_inc(same_in[i], 16)
                run_groups(sp, body, 2, 0)

            @block.gpsimd
            def _(pool):
                def body(st):
                    if st.on():
                        wait(pool, h_done, st.n - 1, e.pool_passed)
                        pool.dma_start(xd[st.s][:, :, :], edge_rows(e.XD, st.n * GE, TW)).then_inc(xd_in[st.s], 16)
                    b = st.back(2)
                    if b.on():
                        wait(pool, h_done, b.n + 1, e.pool_passed)
                        pool.dma_start(edge_rows(e.U1, b.n * GE), hx[b.s][:, :, 0:D]).then_inc(h_out[b.s], 16)
                        wait(pool, kept, b.n + 1, e.pool_passed)
                        pool.dma_start(e.XH1[:, bass.ds(b.n * GE, GE)], xh[b.s][:, :]).then_inc(xh_out[b.s], 16)
                run_groups(pool, body)
                for sems in (h_out, xh_out):
                    for i in range(2):
                        wait(pool, sems[i], 16 * (NG // 2), e.pool_passed)

            @block.vector
            def _(v):
                def body(st):
                    b, c2 = st.back(1), st.back(2)
                    if st.on():
                        i = st.s
                        v.wait_ge(v_in[i], 32 * (st.k + 1))
                        v.wait_ge(et_in[i], 16 * (st.k + 1))
                        wait(v, m_ready, st.n)
                        for r in range(4):
                            m = v.scalar_tensor_tensor(out=vx[:, r, :], in0=et[i][:, :], scalar=e.C["rels"][:, r:r + 1],
                                                       in1=vin[i][:, :], op0=ALU.is_equal, op1=ALU.mult)
                        m.then_inc(vx_done, 1)
                    if b.on():
                        i = b.s
                        v.wait_ge(m_ready, b.n + 1)
                        v.wait_ge(al_in[i], 16 * (b.k + 1))
                        v.wait_ge(same_in[i], 16 * (b.k + 1))
                        v.tensor_tensor(am[:, :], ps_m[:, :], al[i][:, :], ALU.mult).then_inc(am_done, 1)
                        v.wait_ge(am_done, b.n + 1)
                        wait(v, y_ready, b.n - 1)
                        v.tensor_tensor_scan(agg[i][:, :], same[i][:, :], am[:, :],
                                             0.0 if b.first() else agg[1 - i][:, GE - 1:GE],
                                             ALU.mult, ALU.add).then_inc(agg_done, 1)
                        v.wait_ge(agg_done, b.n + 1)
                    if c2.on():
                        i = c2.s
                        c = Chain(v, nrm.chain, c2, 6)
                        v.wait_ge(xd_in[i], 16 * (c2.k + 1))
                        v.wait_ge(y_ready, c2.n + 1)
                        c.link(v.tensor_tensor(onehot[:, :, :], e.C["types"].unsqueeze(1).broadcast_to([P, TU, 4]),
                                               xd[i][:, :, D:D + 1].broadcast_to([P, TU, 4]), ALU.is_equal))
                        v.tensor_tensor(ysel[:, :, :, :], ps_y[:, :, :, :],
                                        onehot[:, :, :].unsqueeze(3).broadcast_to([P, TU, 4, D]), ALU.mult).then_inc(y_used, 1)
                        v.wait_ge(y_used, c2.n + 1)
                        c.link(v.tensor_reduce(yy[:, :, :], ysel[:, :, :, :].rearrange("p u t f -> p u f t"), AX, ALU.add))
                        wait(v, turned, c2.n - 1)
                        wait(v, h_out[i], 16 * c2.k)
                        c.link(v.tensor_tensor(hx[i][:, :, D:2 * D], yy[:, :, :], xd[i][:, :, 0:D], ALU.add))
                        nrm.center(v, c, hx[i][:, :, D:2 * D])
                        nrm.sumsq(v, c2)
                        nrm.recip(v, c, c2)
                        nrm.relu_to(v, hx[i][:, :, 0:D]).then_inc(h_done, 1)
                        c.end()
                run_groups(v, body)

            @block.scalar
            def _(a):
                def body(st):
                    b = st.back(2)
                    if b.on():
                        nrm.square(a, b)
                        nrm.root(a, b, e.C["eps"])
                        a.wait_ge(turned, b.n + 1)
                        wait(a, xh_out[b.s], 16 * b.k)
                        a.copy(xh[b.s][:, :], ps_t[:, :]).then_inc(kept, 1)
                run_groups(a, body)

            @block.tensor
            def _(pe):
                def body(st):
                    b, c2 = st.back(1), st.back(2)
                    if st.on():
                        wait(pe, vx_done, st.n + 1, e.pe_passed)
                        wait(pe, am_done, st.n, e.pe_passed)
                        for r in range(4):
                            m = pe.matmul(ps_m[:, :], e.W["msg"][:, r * D:(r + 1) * D], vx[:, r, :], start=(r == 0), stop=(r == 3))
                        m.then_inc(m_ready, 1)
                    if c2.on():
                        wait(pe, h_done, c2.n + 1, e.pe_passed)
                        wait(pe, kept, c2.n, e.pe_passed)
                        for u in range(TU):
                            m = pe.transpose(ps_t[:, u * P:(u + 1) * P], hx[c2.s][:, u, :], e.C["ident"])
                        m.then_inc(turned, 1)
                    if b.on():
                        wait(pe, agg_done, b.n + 1, e.pe_passed)
                        wait(pe, y_used, b.n, e.pe_passed)
                        for u in range(TU):
                            m = pe.matmul(ps_y[:, u, :, :], agg[b.s][:, u * P:(u + 1) * P],
                                          e.W["a"][0:D, :].rearrange("p (t f) -> p t f", t=4), start=(u % 2 == 0), stop=(u % 2 == 1),
                                          skip_group_check=True)
                        m.then_inc(y_ready, 1)
                run_groups(pe, body)


def start_gathers(e, pool, table, idx_all, idx, gat, gathered, idx_c, st, pos, rows):
    i = st.s
    wait(pool, gathered[i], 16 * TU * st.k, e.pool_passed)
    pool.tensor_copy(idx[i][:, :], idx_all[:, bass.ds(pos * TU, TU)]).then_inc(idx_c, 1)
    wait(pool, idx_c, st.n + 1, e.pool_passed)
    for u in range(TU):
        pool.indirect_dma_start(gat[i][:, u, :], None, table,
                                bass.IndirectOffsetOnAxis(ap=idx[i][:, u:u + 1], axis=0),
                                bounds_check=rows - 1, oob_is_err=False).then_inc(gathered[i], 16)


def difference(nc, e):
    with ExitStack() as ctx:
        s = Scope(nc, ctx, "df")
        idx = [s.sb(f"idx{i}", [P, TU], I32) for i in range(2)]
        hs = [s.sb(f"hs{i}", [P, TU, D]) for i in range(2)]
        hd = [s.sb(f"hd{i}", [D, GE]) for i in range(2)]
        same = [s.sb(f"same{i}", [D, GE]) for i in range(2)]
        lastv = s.sb("lastv", [D, GE])
        hb = [s.sb(f"hb{i}", [D, GE]) for i in range(2)]
        prod = s.sb("prod", [D, GE])
        diff = s.sb("diff", [D, GE])
        sd = [s.sb(f"sd{i}", [D, GE]) for i in range(2)]
        act = s.sb("act", [D, GE])
        junk_s, junk_d = s.sb("junk_s", [P, TU, D]), s.sb("junk_d", [D, GE])
        crow = [s.sb(f"crow{i}", [1, GE]) for i in range(2)]
        sdr = [s.sb(f"sdr{i}", [P, TU, D]) for i in range(2)]
        nacc = s.sb("nacc", [P, 2, NG])
        ntot = s.sb("ntot", [P, 2])
        nsq = s.sb("nsq", [P, 2])
        scale = s.sb("scale", [P, 1])
        cosc = s.sb("cosc", [P, CH])
        ps_t, ps_p, ps_c, ps_b = s.ps("t", [D, GE]), s.ps("p", [D, GE]), s.ps("c", [1, GE]), s.ps("b", [P, TU, D])
        ps_n = s.ps("n", [P, 2])
        gathered, hd_in, same_in, c_out, sd_out = [s.sems(n) for n in ("g", "hd", "sa", "co", "so")]
        idx_c, turned, last_done, hb_done, prod_done, diff_done, sd_done = [
            s.sem(n) for n in ("ic", "tu", "ld", "hb", "pd", "dd", "sdd")]
        p_ready, relu_done, c_ready, c_kept, b_ready, b_kept, sq1, sq2 = [
            s.sem(n) for n in ("pr", "rd", "cr", "ck", "br", "bk", "sq1", "sq2")]
        cleared, fin, tot_done, n_ready, cos_in, gate_done, rooted, clip_done, g_out = [
            s.sem(n) for n in ("clr", "fin", "td", "nr", "ci", "gd", "rt", "cl", "go")]
        pos = lambda st: st.n * -1 + (NG - 1)

        with nc.Block() as block:
            @block.gpsimd
            def _(pool):
                def body(st):
                    if st.on():
                        wait(pool, turned, st.n - 1, e.pool_passed)
                        wait(pool, sq1, st.n - 1, e.pool_passed)
                        start_gathers(e, pool, e.U1, e.idx1, idx, hs, gathered, idx_c, st, pos(st), 2 * EP)
                run_groups(pool, body, 2, 0)

            @block.sync
            def _(sp):
                def body(st):
                    if st.on():
                        i, at = st.s, pos(st) * GE
                        wait(sp, sd_done, st.n - 1, e.sp_passed)
                        sp.dma_start(hd[i][:, :], e.XH1[0:D, bass.ds(at, GE)]).then_inc(hd_in[i], 16)
                        sp.dma_start(same[i][:, :], over_parts(e.same_next, at, D)).then_inc(same_in[i], 16)
                    b = st.back(2)
                    if b.on():
                        wait(sp, c_kept, b.n + 1, e.sp_passed)
                        sp.dma_start(e.cosim[bass.ds(pos(b) * GE, GE)].unsqueeze(0), crow[b.s][0:1, :]).then_inc(c_out[b.s], 16)
                        wait(sp, b_kept, b.n + 1, e.sp_passed)
                        sp.dma_start(edge_rows(e.SD, pos(b) * GE), sdr[b.s][:, :, :]).then_inc(sd_out[b.s], 16)
                run_groups(sp, body)
                for sems in (c_out, sd_out):
                    for i in range(2):
                        wait(sp, sems[i], 16 * (NG // 2), e.sp_passed)
                sp.dma_start(cosc[:, :], e.cosim.rearrange("(p j) -> p j", j=CH)).then_inc(cos_in, 16)
                wait(sp, gate_done, 1, e.sp_passed)
                sp.dma_start(e.gate.rearrange("(p j) -> p j", j=CH), cosc[:, :]).then_inc(g_out, 16)
                wait(sp, g_out, 16, e.sp_passed)

            @block.vector
            def _(v):
                v.memset(nacc[D:P, :, :], 0.0).then_inc(cleared, 1)
                def body(st):
                    if st.on():
                        i = st.s
                        v.wait_ge(hd_in[i], 16 * (st.k + 1))
                        v.wait_ge(same_in[i], 16 * (st.k + 1))
                        v.scalar_tensor_tensor(out=lastv[:, :], in0=same[i][:, :], scalar=-1.0, in1=hd[i][:, :],
                                               op0=ALU.add, op1=ALU.mult).then_inc(last_done, 1)
                        v.wait_ge(last_done, st.n + 1)
                        wait(v, sq2, st.n - 1)
                        v.tensor_tensor_scan(hb[i][:, ::-1], same[i][:, ::-1], lastv[:, ::-1],
                                             0.0 if st.first() else hb[1 - i][:, 0:1],
                                             ALU.mult, ALU.subtract).then_inc(hb_done, 1)
                        v.wait_ge(hb_done, st.n + 1)
                        v.wait_ge(turned, st.n + 1)
                        wait(v, p_ready, st.n)
                        v.tensor_tensor(prod[:, :], ps_t[:, :], hb[i][:, :], ALU.mult).then_inc(prod_done, 1)
                        v.tensor_tensor(diff[:, :], ps_t[:, :], hb[i][:, :], ALU.subtract).then_inc(diff_done, 1)
                        v.wait_ge(diff_done, st.n + 1)
                        wait(v, b_ready, st.n - 1)
                        v.tensor_tensor_scan(sd[i][:, ::-1], same[i][:, ::-1], diff[:, ::-1],
                                             0.0 if st.first() else sd[1 - i][:, 0:1],
                                             ALU.mult, ALU.add).then_inc(sd_done, 1)
                        v.wait_ge(sd_done, st.n + 1)
                run_groups(v, body, 2, 0)
                n = [0]

                def link(ins):
                    n[0] += 1
                    ins.then_inc(fin, 1)
                    v.wait_ge(fin, n[0])

                v.wait_ge(sq1, NG)
                v.wait_ge(sq2, NG)
                v.tensor_reduce(ntot[:, :], nacc[:, :, :], AX, ALU.add).then_inc(tot_done, 1)
                v.wait_ge(rooted, 1)
                link(v.tensor_tensor(scale[:, :], nsq[:, 0:1], nsq[:, 1:2], ALU.mult))
                link(v.tensor_scalar(scale[:, :], scale[:, :], 1e-6, None, ALU.add))
                link(v.reciprocal(scale[:, :], scale[:, :]))
                v.wait_ge(cos_in, 16)
                link(v.tensor_scalar(cosc[:, :], cosc[:, :], scale[:, 0:1], -5.0, ALU.mult, ALU.max))
                v.tensor_scalar(cosc[:, :], cosc[:, :], 5.0, None, ALU.min).then_inc(clip_done, 1)

            @block.scalar
            def _(a):
                def body(st):
                    b, c2 = st, st.back(1)
                    if b.on():
                        a.wait_ge(gathered[b.s], 16 * TU * (b.k + 1))
                        wait(a, sq1, b.n)
                        a.activation(junk_s[:, :, :], hs[b.s][:, :, :], ACT.Square,
                                     accum_out=nacc[:, 0, bass.ds(b.n, 1)]).then_inc(sq1, 1)
                        a.wait_ge(hb_done, b.n + 1)
                        wait(a, sq2, b.n)
                        a.activation(junk_d[:, :], hb[b.s][:, :], ACT.Square,
                                     accum_out=nacc[0:D, 1, bass.ds(b.n, 1)]).then_inc(sq2, 1)
                    if c2.on():
                        b = c2
                        a.wait_ge(p_ready, b.n + 1)
                        wait(a, c_ready, b.n)
                        a.activation(act[:, :], ps_p[:, :], ACT.Relu).then_inc(relu_done, 1)
                        a.wait_ge(b_ready, b.n + 1)
                        wait(a, sd_out[b.s], 16 * b.k)
                        a.copy(sdr[b.s][:, :, :], ps_b[:, :, :]).then_inc(b_kept, 1)
                        a.wait_ge(c_ready, b.n + 1)
                        wait(a, c_out[b.s], 16 * b.k)
                        a.copy(crow[b.s][0:1, :], ps_c[0:1, :]).then_inc(c_kept, 1)
                a.wait_ge(cleared, 1)
                run_groups(a, body)
                a.wait_ge(n_ready, 1)
                a.activation(nsq[:, :], ps_n[:, :], ACT.Sqrt).then_inc(rooted, 1)
                a.wait_ge(clip_done, 1)
                a.activation(cosc[:, :], cosc[:, :], ACT.Exp).then_inc(gate_done, 1)

            @block.tensor
            def _(pe):
                def body(st):
                    b = st.back(1)
                    if st.on():
                        i = st.s
                        wait(pe, gathered[i], 16 * TU * (st.k + 1), e.pe_passed)
                        wait(pe, diff_done, st.n, e.pe_passed)
                        for u in range(TU):
                            m = pe.transpose(ps_t[:, u * P:(u + 1) * P], hs[i][:, u, :], e.C["ident"])
                        m.then_inc(turned, 1)
                    if b.on():
                        wait(pe, prod_done, b.n + 1, e.pe_passed)
                        wait(pe, relu_done, b.n, e.pe_passed)
                        pe.matmul(ps_p[:, :], e.W["proj"][0:D, :], prod[:, :], start=True, stop=True).then_inc(p_ready, 1)
                        wait(pe, sd_done, b.n + 1, e.pe_passed)
                        wait(pe, b_kept, b.n, e.pe_passed)
                        for u in range(TU):
                            m = pe.transpose(ps_b[:, u, :], sd[b.s][:, u * P:(u + 1) * P], e.C["ident"][0:D, 0:D])
                        m.then_inc(b_ready, 1)
                        wait(pe, relu_done, b.n + 1, e.pe_passed)
                        wait(pe, c_kept, b.n, e.pe_passed)
                        pe.matmul(ps_c[:, :], e.C["ones"][0:D, 0:1], act[:, :], start=True, stop=True).then_inc(c_ready, 1)
                run_groups(pe, body)
                wait(pe, tot_done, 1, e.pe_passed)
                pe.matmul(ps_n[:, :], e.C["ones"], ntot[:, :], start=True, stop=True).then_inc(n_ready, 1)


def propagate(nc, e):
    with ExitStack() as ctx:
        s = Scope(nc, ctx, "pr")
        idx = [s.sb(f"idx{i}", [P, TU], I32) for i in range(2)]
        gat = [s.sb(f"gat{i}", [P, TU, D]) for i in range(2)]
        gm = [s.sb(f"gm{i}", [P, TU, D]) for i in range(2)]
        gate = [s.sb(f"gate{i}", [D, GE]) for i in range(2)]
        same = [s.sb(f"same{i}", [D, GE]) for i in range(2)]
        x1 = [s.sb(f"x1{i}", [D, GE]) for i in range(2)]
        gv = s.sb("gv", [D, GE])
        agg = [s.sb(f"agg{i}", [D, GE]) for i in range(2)]
        ffn = s.sb("ffn", [D, GE])
        x2 = [s.sb(f"x2{i}", [D, GE]) for i in range(2)]
        h2 = [s.sb(f"h2{i}", [P, TU, D]) for i in range(2)]
        ps_t, ps_f, ps_x = s.ps("t", [D, GE]), s.ps("f", [D, GE]), s.ps("x", [P, TU, D])
        nrm = s.norm("n", TU)
        gathered, gate_in, same_in, x1_in, x2_out, h2_out = [s.sems(n) for n in ("g", "ga", "sa", "x1", "x2", "h2")]
        idx_c, gm_done, turned, gv_done, agg_done, f_ready, relu_done, x2_done, x_ready, h_done = [
            s.sem(n) for n in ("ic", "gm", "tu", "gv", "ag", "fr", "rd", "xd", "xr", "hd")]

        with nc.Block() as block:
            @block.gpsimd
            def _(pool):
                def body(st):
                    if st.on():
                        wait(pool, gm_done, st.n - 1, e.pool_passed)
                        start_gathers(e, pool, e.SD, e.idxsd, idx, gat, gathered, idx_c, st, st.n, EP)
                run_groups(pool, body, 2, 0)

            @block.sync
            def _(sp):
                def body(st):
                    if st.on():
                        i, at = st.s, st.n * GE
                        wait(sp, agg_done, st.n - 1, e.sp_passed)
                        sp.dma_start(gate[i][:, :], over_parts(e.gate, at, D)).then_inc(gate_in[i], 16)
                        sp.dma_start(same[i][:, :], over_parts(e.same_prev, at, D)).then_inc(same_in[i], 16)
                        wait(sp, x2_done, st.n - 1, e.sp_passed)
                        sp.dma_start(x1[i][:, :], e.XH1[D:P, bass.ds(at, GE)]).then_inc(x1_in[i], 16)
                    b = st.back(2)
                    if b.on():
                        wait(sp, x2_done, b.n + 1, e.sp_passed)
                        sp.dma_start(e.X2T[:, bass.ds(b.n * GE, GE)], x2[b.s][:, :]).then_inc(x2_out[b.s], 16)
                        wait(sp, h_done, b.n + 1, e.sp_passed)
                        sp.dma_start(edge_rows(e.U2, b.n * GE), h2[b.s][:, :, :]).then_inc(h2_out[b.s], 16)
                run_groups(sp, body)
                for sems in (x2_out, h2_out):
                    for i in range(2):
                        wait(sp, sems[i], 16 * (NG // 2), e.sp_passed)

            @block.vector
            def _(v):
                def body(st):
                    b, c2 = st.back(1), st.back(2)
                    if st.on():
                        i = st.s
                        v.wait_ge(gathered[i], 16 * TU * (st.k + 1))
                        wait(v, turned, st.n - 1)
                        v.tensor_tensor(gm[i][:, :, :], gat[i][:, :, :],
                                        e.has[:, bass.ds(st.n * TU, TU)].unsqueeze(2).broadcast_to([P, TU, D]),
                                        ALU.mult).then_inc(gm_done, 1)
                    if c2.on():
                        c = Chain(v, nrm.chain, c2, 3)
                        v.wait_ge(x_ready, c2.n + 1)
                        nrm.center(v, c, ps_x[:, :, :])
                    if b.on():
                        i = b.s
                        v.wait_ge(turned, b.n + 1)
                        v.wait_ge(gate_in[i], 16 * (b.k + 1))
                        v.wait_ge(same_in[i], 16 * (b.k + 1))
                        v.tensor_tensor(gv[:, :], ps_t[:, :], gate[i][:, :], ALU.mult).then_inc(gv_done, 1)
                        v.wait_ge(gv_done, b.n + 1)
                        wait(v, f_ready, b.n - 1)
                        v.tensor_tensor_scan(agg[i][:, :], same[i][:, :], gv[:, :],
                                             0.0 if b.first() else agg[1 - i][:, GE - 1:GE],
                                             ALU.mult, ALU.add).then_inc(agg_done, 1)
                        v.wait_ge(agg_done, b.n + 1)
                    if c2.on():
                        nrm.sumsq(v, c2)
                        nrm.recip(v, c, c2)
                        wait(v, h2_out[c2.s], 16 * c2.k)
                        nrm.relu_to(v, h2[c2.s][:, :, :]).then_inc(h_done, 1)
                        c.end()
                    if b.on():
                        i = b.s
                        v.wait_ge(relu_done, b.n + 1)
                        v.wait_ge(x1_in[i], 16 * (b.k + 1))
                        wait(v, x2_out[i], 16 * b.k)
                        v.tensor_tensor(x2[i][:, :], ffn[:, :], x1[i][:, :], ALU.add).then_inc(x2_done, 1)
                run_groups(v, body)

            @block.scalar
            def _(a):
                def body(st):
                    b, c2 = st.back(1), st.back(2)
                    if c2.on():
                        nrm.square(a, c2)
                        nrm.root(a, c2, e.C["eps"])
                    if b.on():
                        a.wait_ge(f_ready, b.n + 1)
                        wait(a, x2_done, b.n)
                        a.activation(ffn[:, :], ps_f[:, :], ACT.Relu, bias=e.W["bffn"][0:D, :]).then_inc(relu_done, 1)
                run_groups(a, body)

            @block.tensor
            def _(pe):
                def body(st):
                    b = st.back(1)
                    if st.on():
                        i = st.s
                        wait(pe, gm_done, st.n + 1, e.pe_passed)
                        wait(pe, gv_done, st.n, e.pe_passed)
                        for u in range(TU):
                            m = pe.transpose(ps_t[:, u * P:(u + 1) * P], gm[i][:, u, :], e.C["ident"])
                        m.then_inc(turned, 1)
                    if b.on():
                        i = b.s
                        wait(pe, agg_done, b.n + 1, e.pe_passed)
                        wait(pe, relu_done, b.n, e.pe_passed)
                        pe.matmul(ps_f[:, :], e.W["ffnT"][0:D, :], agg[i][:, :], start=True, stop=True).then_inc(f_ready, 1)
                        wait(pe, x2_done, b.n + 1, e.pe_passed)
                        wait(pe, nrm.centered, b.n, e.pe_passed)
                        for u in range(TU):
                            m = pe.transpose(ps_x[:, u, :], x2[i][:, u * P:(u + 1) * P], e.C["ident"][0:D, 0:D])
                        m.then_inc(x_ready, 1)
                run_groups(pe, body)


def mlp(nc, e):
    with ExitStack() as ctx:
        s = Scope(nc, ctx, "ml")
        idx = [s.sb(f"idx{i}", [P, TU], I32) for i in range(2)]
        gat = [s.sb(f"gat{i}", [P, TU, D]) for i in range(2)]
        own = [s.sb(f"own{i}", [P, TU, D]) for i in range(2)]
        same = [s.sb(f"same{i}", [D, GE]) for i in range(2)]
        x2 = [s.sb(f"x2{i}", [D, GE]) for i in range(2)]
        agg = [s.sb(f"agg{i}", [D, GE]) for i in range(2)]
        hh = s.sb("hh", [D, GE])
        hid = s.sb("hid", [P, GE])
        x3 = [s.sb(f"x3{i}", [D, GE]) for i in range(2)]
        hx = [s.sb(f"hx{i}", [P, TU, 2 * D]) for i in range(2)]
        xh = [s.sb(f"xh{i}", [P, GE]) for i in range(2)]
        ps_t, ps_o, ps_1, ps_2, ps_x, ps_h = (s.ps("t", [D, GE]), s.ps("o", [D, GE]), s.ps("h1", [P, GE]),
                                              s.ps("h2", [D, GE]), s.ps("x", [P, TU, D]), s.ps("h", [P, GE]))
        nrm = s.norm("n", TU)
        gathered, own_in, same_in, x2_in, h_out, xh_out = [s.sems(n) for n in ("g", "own", "sa", "x2", "ho", "xo")]
        idx_c, t_ready, o_ready, agg_done, hh_done, h1_ready, hid_done, h2_ready, x3_done = [
            s.sem(n) for n in ("ic", "tr", "or", "ag", "hh", "h1", "hid", "h2", "x3")]
        x_ready, x_kept, h_done, hx_turned, kept = [s.sem(n) for n in ("xr", "xk", "hd", "ht", "kp")]

        with nc.Block() as block:
            @block.gpsimd
            def _(pool):
                def body(st):
                    if st.on():
                        wait(pool, t_ready, st.n - 1, e.pool_passed)
                        start_gathers(e, pool, e.U2, e.idx2, idx, gat, gathered, idx_c, st, st.n, EP + NP)
                run_groups(pool, body, 2, 0)

            @block.sync
            def _(sp):
                def body(st):
                    if st.on():
                        i, at = st.s, st.n * GE
                        wait(sp, o_ready, st.n - 1, e.sp_passed)
                        sp.dma_start(own[i][:, :, :], edge_rows(e.U2, at)).then_inc(own_in[i], 16)
                        wait(sp, agg_done, st.n - 1, e.sp_passed)
                        sp.dma_start(same[i][:, :], over_parts(e.same_prev, at, D)).then_inc(same_in[i], 16)
                        wait(sp, x3_done, st.n - 1, e.sp_passed)
                        sp.dma_start(x2[i][:, :], e.X2T[:, bass.ds(at, GE)]).then_inc(x2_in[i], 16)
                    b = st.back(2)
                    if b.on():
                        wait(sp, h_done, b.n + 1, e.sp_passed)
                        sp.dma_start(edge_rows(e.U3, b.n * GE), hx[b.s][:, :, 0:D]).then_inc(h_out[b.s], 16)
                        wait(sp, kept, b.n + 1, e.sp_passed)
                        sp.dma_start(e.XH3[:, bass.ds(b.n * GE, GE)], xh[b.s][:, :]).then_inc(xh_out[b.s], 16)
                run_groups(sp, body)
                for sems in (h_out, xh_out):
                    for i in range(2):
                        wait(sp, sems[i], 16 * (NG // 2), e.sp_passed)

            @block.vector
            def _(v):
                def body(st):
                    b, c2 = st, st.back(2)
                    if c2.on():
                        c = Chain(v, nrm.chain, c2, 3)
                        v.wait_ge(x_kept, c2.n + 1)
                        nrm.center(v, c, hx[c2.s][:, :, D:2 * D])
                    if b.on():
                        i = b.s
                        v.wait_ge(t_ready, b.n + 1)
                        v.wait_ge(same_in[i], 16 * (b.k + 1))
                        v.tensor_tensor_scan(agg[i][:, :], same[i][:, :], ps_t[:, :],
                                             0.0 if b.first() else agg[1 - i][:, GE - 1:GE],
                                             ALU.mult, ALU.add).then_inc(agg_done, 1)
                        v.wait_ge(agg_done, b.n + 1)
                        v.wait_ge(o_ready, b.n + 1)
                        wait(v, h1_ready, b.n)
                        v.tensor_tensor(hh[:, :], ps_o[:, :], agg[i][:, :], ALU.add).then_inc(hh_done, 1)
                    if c2.on():
                        nrm.sumsq(v, c2)
                        nrm.recip(v, c, c2)
                        wait(v, h_out[c2.s], 16 * c2.k)
                        nrm.relu_to(v, hx[c2.s][:, :, 0:D]).then_inc(h_done, 1)
                        c.end()
                    b = st.back(1)
                    if b.on():
                        i = b.s
                        v.wait_ge(h2_ready, b.n + 1)
                        v.wait_ge(x2_in[i], 16 * (b.k + 1))
                        wait(v, x_ready, b.n - 1)
                        v.scalar_tensor_tensor(out=x3[i][:, :], in0=ps_2[:, :], scalar=e.W["b1"][0:D, :], in1=x2[i][:, :],
                                               op0=ALU.add, op1=ALU.add).then_inc(x3_done, 1)
                run_groups(v, body)

            @block.scalar
            def _(a):
                def body(st):
                    b, c2 = st.back(1), st.back(2)
                    if c2.on():
                        a.wait_ge(x_ready, c2.n + 1)
                        wait(a, hx_turned, c2.n - 1)
                        a.copy(hx[c2.s][:, :, D:2 * D], ps_x[:, :, :]).then_inc(x_kept, 1)
                        nrm.square(a, c2)
                    if b.on():
                        a.wait_ge(h1_ready, b.n + 1)
                        wait(a, h2_ready, b.n)
                        a.activation(hid[:, :], ps_1[:, :], ACT.Relu, bias=e.W["b0"]).then_inc(hid_done, 1)
                    if c2.on():
                        nrm.root(a, c2, e.C["eps"])
                        a.wait_ge(hx_turned, c2.n + 1)
                        wait(a, xh_out[c2.s], 16 * c2.k)
                        a.copy(xh[c2.s][:, :], ps_h[:, :]).then_inc(kept, 1)
                run_groups(a, body)

            @block.tensor
            def _(pe):
                def body(st):
                    b, c2 = st.back(1), st.back(2)
                    if b.on():
                        wait(pe, hh_done, b.n + 1, e.pe_passed)
                        wait(pe, hid_done, b.n, e.pe_passed)
                        pe.matmul(ps_1[:, :], e.W["w0"][0:D, :], hh[:, :], start=True, stop=True).then_inc(h1_ready, 1)
                    if st.on():
                        i = st.s
                        wait(pe, gathered[i], 16 * TU * (st.k + 1), e.pe_passed)
                        wait(pe, agg_done, st.n, e.pe_passed)
                        for u in range(TU):
                            m = pe.transpose(ps_t[:, u * P:(u + 1) * P], gat[i][:, u, :], e.C["ident"])
                        m.then_inc(t_ready, 1)
                        wait(pe, own_in[i], 16 * (st.k + 1), e.pe_passed)
                        wait(pe, hh_done, st.n, e.pe_passed)
                        for u in range(TU):
                            m = pe.transpose(ps_o[:, u * P:(u + 1) * P], own[i][:, u, :], e.C["ident"])
                        m.then_inc(o_ready, 1)
                    if b.on():
                        wait(pe, hid_done, b.n + 1, e.pe_passed)
                        wait(pe, x3_done, b.n, e.pe_passed)
                        pe.matmul(ps_2[:, :], e.W["w1"], hid[:, :], start=True, stop=True).then_inc(h2_ready, 1)
                    if c2.on():
                        wait(pe, h_done, c2.n + 1, e.pe_passed)
                        wait(pe, kept, c2.n, e.pe_passed)
                        for u in range(TU):
                            m = pe.transpose(ps_h[:, u * P:(u + 1) * P], hx[c2.s][:, u, :], e.C["ident"])
                        m.then_inc(hx_turned, 1)
                    if b.on():
                        wait(pe, x3_done, b.n + 1, e.pe_passed)
                        wait(pe, x_kept, b.n, e.pe_passed)
                        for u in range(TU):
                            m = pe.transpose(ps_x[:, u, :], x3[b.s][:, u * P:(u + 1) * P], e.C["ident"][0:D, 0:D])
                        m.then_inc(x_ready, 1)
                run_groups(pe, body)


def heads(nc, e):
    with ExitStack() as ctx:
        s = Scope(nc, ctx, "hd")
        idx = [s.sb(f"idx{i}", [P, TU], I32) for i in range(2)]
        oidx = [s.sb(f"oidx{i}", [P, TU], I32) for i in range(2)]
        gat = [s.sb(f"gat{i}", [P, TU, D]) for i in range(2)]
        xl = [s.sb(f"xl{i}", [P, GE]) for i in range(2)]
        same = [s.sb(f"same{i}", [P, GE]) for i in range(2)]
        lastv = s.sb("lastv", [P, GE])
        xb = [s.sb(f"xb{i}", [P, GE]) for i in range(2)]
        ht = s.sb("ht", [D, GE])
        qt = s.sb("qt", [D, GE])
        prod = s.sb("prod", [D, GE])
        clip = s.sb("clip", [P, GE])
        wgt = s.sb("wgt", [D, GE])
        wz = s.sb("wz", [P, GE])
        wv = [s.sb(f"wv{i}", [P, GE]) for i in range(2)]
        z1 = s.sb("z1", [D, GE])
        wn = s.sb("wn", [D, GE])
        f1 = s.sb("f1", [P, TU, D])
        x4 = [s.sb(f"x4{i}", [P, TU, D]) for i in range(2)]
        ps_t, ps_q, ps_k, ps_v, ps_s = s.ps("t", [D, GE]), s.ps("q", [D, GE]), s.ps("k", [D, GE]), s.ps("v", [D, GE]), s.ps("s", [P, GE])
        ps_h, ps_x = s.ps("h", [P, TU, D]), s.ps("x", [P, GE])
        nrm = s.norm("n", TU)
        gathered, xl_in, same_in, x4_out = [s.sems(n) for n in ("g", "xl", "sa", "xo")]
        (idx_c, oidx_c, turned, ht_kept, last_done, xb_done, k_ready, q_ready, v_ready, q_kept, prod_done, s_ready, clip_done,
         w_done, z_done, wz_done, wv_done, z1_done, wn_done, h_ready, x_ready, x4_done, zc, lnc) = [
            s.sem(n) for n in ("ic", "oc", "tu", "htk", "ld", "xb", "kr", "qr", "vr", "qk", "pd", "sr", "cl",
                               "wd", "zd", "wzd", "wvd", "z1", "wn", "hr", "xr", "x4", "zc", "ln")]
        pos = lambda st: st.n * -1 + (NG - 1)

        with nc.Block() as block:
            @block.gpsimd
            def _(pool):
                def body(st):
                    if st.on():
                        wait(pool, turned, st.n - 1, e.pool_passed)
                        start_gathers(e, pool, e.U3, e.idx2, idx, gat, gathered, idx_c, st, pos(st), EP + NP)
                    b = st.back(4)
                    if b.on():
                        i = b.s
                        wait(pool, x4_out[i], 16 * TU * b.k, e.pool_passed)
                        pool.tensor_copy(oidx[i][:, :], e.scat_out[:, bass.ds(pos(b) * TU, TU)]).then_inc(oidx_c, 1)
                        wait(pool, oidx_c, b.n + 1, e.pool_passed)
                        wait(pool, x4_done, b.n + 1, e.pool_passed)
                        for u in range(TU):
                            pool.indirect_dma_start(e.out, bass.IndirectOffsetOnAxis(ap=oidx[i][:, u:u + 1], axis=0),
                                                    x4[i][:, u, :], None, bounds_check=NP - 1,
                                                    oob_is_err=False).then_inc(x4_out[i], 16)
                run_groups(pool, body, 2, 4)
                for i in range(2):
                    wait(pool, x4_out[i], 16 * TU * (NG // 2), e.pool_passed)

            @block.sync
            def _(sp):
                def body(st):
                    if st.on():
                        i, at = st.s, pos(st) * GE
                        wait(sp, xb_done, st.n - 1, e.sp_passed)
                        sp.dma_start(xl[i][:, :], e.XH3[:, bass.ds(at, GE)]).then_inc(xl_in[i], 16)
                        wait(sp, wv_done, st.n - 1, e.sp_passed)
                        sp.dma_start(same[i][:, :], over_parts(e.same_next, at, P)).then_inc(same_in[i], 16)
                run_groups(sp, body, 2, 0)

            @block.vector
            def _(v):
                def body(st):
                    a0, b, c2 = st, st.back(1), st.back(2)
                    if a0.on():
                        i = a0.s
                        v.wait_ge(xl_in[i], 16 * (a0.k + 1))
                        v.wait_ge(same_in[i], 16 * (a0.k + 1))
                        wait(v, xb_done, a0.n)
                        v.scalar_tensor_tensor(out=lastv[:, :], in0=same[i][:, :], scalar=-1.0, in1=xl[i][:, :],
                                               op0=ALU.add, op1=ALU.mult).then_inc(last_done, 1)
                        v.wait_ge(last_done, a0.n + 1)
                        wait(v, h_ready, a0.n - 1)
                        v.tensor_tensor_scan(xb[i][:, ::-1], same[i][:, ::-1], lastv[:, ::-1],
                                             0.0 if a0.first() else xb[1 - i][:, 0:1],
                                             ALU.mult, ALU.subtract).then_inc(xb_done, 1)
                    if c2.on():
                        c = Chain(v, nrm.chain, c2, 7)
                        v.wait_ge(h_ready, c2.n + 1)
                        nrm.center(v, c, ps_h[:, :, :])
                    if b.on():
                        i = b.s
                        v.wait_ge(k_ready, b.n + 1)
                        v.wait_ge(q_kept, b.n + 1)
                        wait(v, s_ready, b.n)
                        v.scalar_tensor_tensor(out=prod[:, :], in0=ps_k[:, :], scalar=e.W["bk"][0:D, :], in1=qt[:, :],
                                               op0=ALU.add, op1=ALU.mult).then_inc(prod_done, 1)
                    if c2.on():
                        nrm.sumsq(v, c2)
                    if b.on():
                        v.wait_ge(s_ready, b.n + 1)
                        wait(v, z_done, b.n)
                        v.tensor_scalar(clip[:, :], ps_s[:, :], 1.0 / 8.0, 5.0, ALU.mult, ALU.min).then_inc(zc, 1)
                        v.wait_ge(zc, b.n + 1)
                        v.tensor_scalar(clip[:, :], clip[:, :], -5.0, None, ALU.max).then_inc(clip_done, 1)
                    if c2.on():
                        nrm.recip(v, c, c2)
                        c.link(v.tensor_tensor(f1[:, :, :], nrm.cent[:, :, :], nrm.over(nrm.rstd), ALU.mult))
                        c.link(v.tensor_tensor(f1[:, :, :], f1[:, :, :],
                                               e.W["gamma"].unsqueeze(1).broadcast_to([P, TU, D]), ALU.mult))
                        c.link(v.tensor_tensor(f1[:, :, :], f1[:, :, :], ps_h[:, :, :], ALU.add))
                        v.wait_ge(x_ready, c2.n + 1)
                        c.link(v.tensor_tensor(f1[:, :, :], f1[:, :, :],
                                               ps_x[:, :].rearrange("p (u f) -> p u f", u=TU)[:, :, D:2 * D], ALU.add))
                        wait(v, x4_out[c2.s], 16 * TU * c2.k)
                        v.tensor_tensor(x4[c2.s][:, :, :], f1[:, :, :],
                                        e.W["beta"].unsqueeze(1).broadcast_to([P, TU, D]), ALU.add).then_inc(x4_done, 1)
                        c.end()
                    if b.on():
                        i = b.s
                        v.wait_ge(w_done, b.n + 1)
                        v.wait_ge(z_done, b.n + 1)
                        v.wait_ge(v_ready, b.n + 1)
                        v.scalar_tensor_tensor(out=wz[0:D, :], in0=ps_v[:, :], scalar=e.W["bv"][0:D, :], in1=wgt[:, :],
                                               op0=ALU.add, op1=ALU.mult).then_inc(wz_done, 1)
                        v.wait_ge(wz_done, b.n + 1)
                        v.tensor_tensor_scan(wv[i][:, ::-1], same[i][:, ::-1], wz[:, ::-1],
                                             0.0 if b.first() else wv[1 - i][:, 0:1],
                                             ALU.mult, ALU.add).then_inc(wv_done, 1)
                        v.wait_ge(wv_done, b.n + 1)
                        v.tensor_scalar(z1[:, :], wv[i][D:P, :], 1.0, None, ALU.add).then_inc(z1_done, 1)
                        v.wait_ge(z1_done, 2 * b.n + 1)
                        v.reciprocal(z1[:, :], z1[:, :]).then_inc(z1_done, 1)
                        v.wait_ge(z1_done, 2 * b.n + 2)
                        wait(v, h_ready, b.n)
                        v.tensor_tensor(wn[:, :], wv[i][0:D, :], z1[:, :], ALU.mult).then_inc(wn_done, 1)
                run_groups(v, body)

            @block.scalar
            def _(a):
                def body(st):
                    b, c2 = st.back(1), st.back(2)
                    if st.on():
                        a.wait_ge(turned, st.n + 1)
                        wait(a, v_ready, st.n)
                        a.copy(ht[:, :], ps_t[:, :]).then_inc(ht_kept, 1)
                        a.wait_ge(q_ready, st.n + 1)
                        wait(a, prod_done, st.n)
                        a.activation(qt[:, :], ps_q[:, :], ACT.Identity, bias=e.W["bq"][0:D, :]).then_inc(q_kept, 1)
                    if c2.on():
                        nrm.square(a, c2)
                        a.wait_ge(nrm.summed, c2.n + 1)
                        a.activation(nrm.std[:, :], nrm.ss[:, :], ACT.Ln, bias=e.C["eps"], scale=1.0 / D).then_inc(lnc, 1)
                        a.wait_ge(lnc, c2.n + 1)
                        a.activation(nrm.std[:, :], nrm.std[:, :], ACT.Exp, scale=0.5).then_inc(nrm.rooted, 1)
                    if b.on():
                        a.wait_ge(clip_done, b.n + 1)
                        wait(a, wz_done, b.n)
                        a.activation(wgt[:, :], clip[0:D, :], ACT.Exp).then_inc(w_done, 1)
                        wait(a, wv_done, b.n)
                        a.activation(wz[D:P, :], clip[D:P, :], ACT.Exp).then_inc(z_done, 1)
                run_groups(a, body)

            @block.tensor
            def _(pe):
                def body(st):
                    b = st.back(1)
                    if b.on():
                        wait(pe, prod_done, b.n + 1, e.pe_passed)
                        wait(pe, clip_done, b.n, e.pe_passed)
                        pe.matmul(ps_s[:, :], e.C["heads"][0:D, :], prod[:, :], start=True, stop=True).then_inc(s_ready, 1)
                    if st.on():
                        i = st.s
                        wait(pe, gathered[i], 16 * TU * (st.k + 1), e.pe_passed)
                        wait(pe, ht_kept, st.n, e.pe_passed)
                        for u in range(TU):
                            m2 = pe.transpose(ps_t[:, u * P:(u + 1) * P], gat[i][:, u, :], e.C["ident"])
                        m2.then_inc(turned, 1)
                        wait(pe, xb_done, st.n + 1, e.pe_passed)
                        wait(pe, q_kept, st.n, e.pe_passed)
                        pe.matmul(ps_q[:, :], e.W["wq"][0:D, :], xb[i][0:D, :], start=True, stop=True).then_inc(q_ready, 1)
                    if b.on():
                        wait(pe, x4_done, b.n, e.pe_passed)
                        for u in range(TU):
                            m = pe.transpose(ps_x[:, u * P:(u + 1) * P], xb[b.s][:, u * P:(u + 1) * P], e.C["ident"])
                        m.then_inc(x_ready, 1)
                        wait(pe, wn_done, b.n + 1, e.pe_passed)
                        for u in range(TU):
                            pe.matmul(ps_h[:, u, :], e.C["ones"][0:D, :], e.bfo[0:D, :], start=(u == 0), stop=False,
                                      skip_group_check=True)
                        for u in range(TU):
                            pe.matmul(ps_h[:, u, :], xb[b.s][0:D, u * P:(u + 1) * P], e.W["wf2"][0:D, 0:D], start=False,
                                      stop=False, skip_group_check=True)
                        for u in range(TU):
                            m = pe.matmul(ps_h[:, u, :], wn[:, u * P:(u + 1) * P], e.W["wo"][0:D, :], start=False,
                                          stop=(u == TU - 1), skip_group_check=True)
                        m.then_inc(h_ready, 1)
                    if st.on():
                        wait(pe, ht_kept, st.n + 1, e.pe_passed)
                        wait(pe, prod_done, st.n, e.pe_passed)
                        pe.matmul(ps_k[:, :], e.W["wk"][0:D, :], ht[:, :], start=True, stop=True).then_inc(k_ready, 1)
                        wait(pe, wz_done, st.n, e.pe_passed)
                        pe.matmul(ps_v[:, :], e.W["wv"][0:D, :], ht[:, :], start=True, stop=True).then_inc(v_ready, 1)
                run_groups(pe, body)


def constants():
    c = np.zeros((P, CONST_W), np.float32)
    put = lambda name, a: c.__setitem__((slice(0, a.shape[0]), slice(*CONST_AT[name])), a)
    put("ident", np.eye(P, dtype=np.float32))
    put("ones", np.ones((P, P), np.float32))
    f, m = np.arange(D)[:, None], np.arange(P)[None, :]
    put("heads", (f // 16 == (m % D) // 16).astype(np.float32))
    put("types", np.tile(np.arange(4, dtype=np.float32), (P, 1)))
    put("rels", (2 * np.arange(4)[None, :] + (np.arange(P)[:, None] >= D)).astype(np.float32))
    put("eps", np.full((P, 1), EPS, np.float32))
    return c


def pack_weights(i):
    w = np.zeros((P, WEIGHT_W), np.float32)

    def put(name, a, row=0, col=0):
        a = np.asarray(a)
        at = WEIGHT_AT[name][0] + col
        w[row:row + a.shape[0], at:at + a.shape[1]] = a

    def pairs(name, a, col, width):
        for c in range(a.shape[0] // 2):
            put(name, a[2 * c:2 * c + 2].reshape(P, D), 0, c * width + col)

    q, k, v = (np.asarray(i[f"L0_gnn_{n}_lin"]) for n in "qkv")
    for half in range(2):
        pairs("q", q, half * D, P)
    pairs("kv", k, 0, P)
    pairs("kv", v, D, P)
    pairs("att", np.asarray(i["L0_gnn_rel_att"]), 0, D)
    pairs("msg", np.asarray(i["L0_gnn_rel_msg"]), 0, D)
    pri = np.asarray(i["L0_gnn_rel_pri"]).reshape(4, 2)
    put("pri", np.repeat(pri.T, D, axis=0))
    put("a", np.asarray(i["L0_gnn_a_lin"]).transpose(1, 0, 2).reshape(D, 4 * D))
    put("skip", np.tile(np.repeat(np.asarray(i["L0_gnn_skip"]), D)[None], (D, 1)))
    put("proj", i["L1_gnn_proj_cosim"])
    put("ffnT", np.asarray(i["L1_gnn_W_ffn"]).T)
    put("bffn", np.asarray(i["L1_gnn_b_ffn"])[:, None])
    put("bffn_row", np.tile(np.asarray(i["L1_gnn_b_ffn"])[None], (P, 1)))
    for half in range(2):
        put("w0", i["L2_gnn_W0"], half * D)
        put("wf2", i["L3_gnn_Wf"], half * D, half * D)
    put("b0", np.asarray(i["L2_gnn_b0"])[:, None])
    put("w1", i["L2_gnn_W1"])
    put("b1", np.asarray(i["L2_gnn_b1"])[:, None])
    put("b1_top", np.asarray(i["L2_gnn_b1"])[None])
    for n in "qkv":
        put("w" + n, i[f"L3_gnn_W{n}"])
        put("b" + n, np.asarray(i[f"L3_gnn_b{n}"])[:, None])
    put("wo", i["L3_gnn_Wo"])
    put("bo_top", np.asarray(i["L3_gnn_bo"])[None])
    put("bf_top", np.asarray(i["L3_gnn_bf"])[None])
    put("gamma", np.tile(np.asarray(i["L3_gnn_gamma"])[None], (P, 1)))
    put("beta", np.tile(np.asarray(i["L3_gnn_beta"])[None], (P, 1)))
    return w


def lay_out(i):
    def padded(a, n, fill):
        a = np.asarray(a)
        p = np.full((n,) + a.shape[1:], fill, a.dtype)
        p[:a.shape[0]] = a
        return p

    src, dst = padded(i["src"], EP, PADN), padded(i["dst"], EP, PADN)
    etype = padded(i["edge_type_8"], EP, 0)
    major = lambda a: np.ascontiguousarray(a.reshape(NG, TU, P).transpose(2, 0, 1))
    ntype = padded(i["node_type_4"], NP, 0).reshape(NG, P, RN).transpose(1, 0, 2).reshape(P, NG * RN)
    return {
        "x": padded(i["x"], NP, 0.0), "node_type": np.ascontiguousarray(ntype),
        "src_idx": major(src), "dst_idx": major(dst), "etype_row": etype,
        "dst_row": np.concatenate([np.full(1, -1, dst.dtype), dst, np.full(1, -1, dst.dtype)]),
        "chunk_id": np.arange(1, EP + 1, dtype=np.float32).reshape(P, CH),
        "consts": constants(), "weights": pack_weights(i),
    }


def kernel(**inputs):
    import concourse.bacc as bacc
    from concourse.bass_utils import run_bass_kernel_spmd

    arrays = lay_out(inputs)
    nc = bacc.Bacc("TRN2", target_bir_lowering=False, num_devices=1)
    aps = {n: nc.dram_tensor("in_" + n, a.shape, mybir.dt.from_np(a.dtype), kind="ExternalInput").ap()
           for n, a in arrays.items()}
    out = nc.dram_tensor("out_x", (NP, D), F32, kind="ExternalOutput").ap()
    build(nc, out=out, **aps)
    r = run_bass_kernel_spmd(nc, [{"in_" + n: a for n, a in arrays.items()}], core_ids=[0])
    return r.results[0]["out_x"][:NODES]
```

```python
from contextlib import ExitStack

import numpy as np
import concourse.bass as bass
from concourse import mybir

P = 128
D = 64
NODES = 100000
EDGES = 50000
GE = 512
TU = GE // P
U = 3
NG = -(-EDGES // (GE * U)) * U
EP = NG * GE
CH = EP // P
GN = 1024
RN = GN // P
NP = NG * GN
PADN = NODES
TW = 68
FAR = 8388608.0
BIG = 1.7e38
EPS = 1e-5
LAST = 2

F32 = mybir.dt.float32
I32 = mybir.dt.int32
ALU = mybir.AluOpType
ACT = mybir.ActivationFunctionType
AX = mybir.AxisListType.X

CONST_COLS = [("ident", 128), ("ones", 128), ("heads", 128), ("types", 4), ("rels", 4), ("less_rels", 4), ("eps", 1)]
WEIGHT_COLS = [
    ("q", 256), ("kv", 256), ("att", 256), ("msg", 256), ("pri", 4), ("a", 256), ("skip", 256),
    ("proj", 64), ("ffnT", 64), ("bffn", 1), ("bffn_row", 64),
    ("w0", 128), ("b0", 1), ("w1", 64), ("b1", 1), ("b1_row", 64),
    ("wq", 64), ("bq", 1), ("wk", 64), ("bk", 1), ("wv", 64), ("bv", 1),
    ("wo", 64), ("bo_row", 64), ("wf2", 128), ("bf_row", 64), ("gamma", 64), ("beta", 64),
    ("wfx", 128), ("wob", 128), ("bf_64", 128), ("beta_64", 64),
]


def spans(cols):
    at, out = 0, {}
    for name, n in cols:
        out[name] = (at, at + n)
        at += n
    return out, at


CONST_AT, CONST_W = spans(CONST_COLS)
WEIGHT_AT, WEIGHT_W = spans(WEIGHT_COLS)


class Step:

    def __init__(self, n, k, s, u):
        self.n, self.k, self.s, self.u = n, k, s, u

    def back(self, lag):
        return Step(self.n - lag, self.k + (self.s - lag) // self.u, (self.s - lag) % self.u, self.u)

    def on(self):
        return not isinstance(self.n, int) or 0 <= self.n < NG

    def first(self):
        return isinstance(self.n, int) and self.n == 0


def run_groups(eng, body, u=U, tail=LAST, peel=3):
    for n in range(peel * u):
        body(Step(n, n // u, n % u, u))
    with eng.Fori(peel, NG // u) as i:
        for s in range(u):
            body(Step(i * u + s, i, s, u))
    for n in range(NG, NG + tail):
        body(Step(n, n // u, n % u, u))


def wait(eng, sem, value, passed=None):
    if isinstance(value, int) and value <= 0:
        return
    eng.wait_ge(sem, value)
    if passed is not None and not isinstance(value, int):
        eng.sem_inc(passed, 1)


class Chain:

    def __init__(self, eng, sem, step, per):
        self.eng, self.sem, self.base, self.per, self.i = eng, sem, step.n * per, per, 0

    def link(self, ins):
        self.i += 1
        assert self.i <= self.per
        ins.then_inc(self.sem, 1)
        self.eng.wait_ge(self.sem, self.base + self.i)

    def put(self, ins):
        self.i += 1
        assert self.i <= self.per
        ins.then_inc(self.sem, 1)

    def join(self):
        self.eng.wait_ge(self.sem, self.base + self.i)

    def end(self):
        assert self.i == self.per, (self.i, self.per)


class Norm:

    def __init__(self, sb, sem, name, rows):
        self.rows = rows
        self.sum = sb(f"{name}_sum", [P, rows], F32)
        self.cent = sb(f"{name}_cent", [P, rows, D], F32)
        self.sq = sb(f"{name}_sq", [P, rows, D], F32)
        self.ss = sb(f"{name}_ss", [P, rows], F32)
        self.std = sb(f"{name}_std", [P, rows], F32)
        self.rstd = sb(f"{name}_rstd", [P, rows], F32)
        self.centered = sem(f"{name}_centered")
        self.squared = sem(f"{name}_squared")
        self.summed = sem(f"{name}_summed")
        self.rooted = sem(f"{name}_rooted")
        self.chain = sem(f"{name}_chain")

    def over(self, small):
        return small[:, :].unsqueeze(2).broadcast_to([P, self.rows, D])

    def total(self, v, x):
        return v.tensor_reduce(self.sum[:, :], x, AX, ALU.add)

    def shift(self, v, x):
        v.scalar_tensor_tensor(out=self.cent[:, :, :], in0=self.over(self.sum), scalar=-1.0 / D, in1=x,
                               op0=ALU.mult, op1=ALU.add).then_inc(self.centered, 1)

    def center(self, v, c, x):
        c.link(self.total(v, x))
        self.shift(v, x)

    def square(self, a, st):
        a.wait_ge(self.centered, st.n + 1)
        wait(a, self.summed, st.n)
        a.activation(self.sq[:, :, :], self.cent[:, :, :], ACT.Square).then_inc(self.squared, 1)

    def sumsq(self, v, st):
        v.wait_ge(self.squared, st.n + 1)
        v.tensor_reduce(self.ss[:, :], self.sq[:, :, :], AX, ALU.add).then_inc(self.summed, 1)

    def root(self, a, st, eps):
        a.wait_ge(self.summed, st.n + 1)
        a.activation(self.std[:, :], self.ss[:, :], ACT.Sqrt, bias=eps, scale=1.0 / D).then_inc(self.rooted, 1)

    def recip(self, v, c, st):
        v.wait_ge(self.rooted, st.n + 1)
        c.link(v.reciprocal(self.rstd[:, :], self.std[:, :]))

    def relu_to(self, v, out):
        return v.scalar_tensor_tensor(out=out, in0=self.cent[:, :, :], scalar=0.0, in1=self.over(self.rstd),
                                      op0=ALU.max, op1=ALU.mult)


class Scope:

    def __init__(self, nc, ctx, tag):
        self.nc, self.ctx, self.tag, self.used = nc, ctx, tag, []
        ctx.callback(self.clear)

    def clear(self):
        if self.used:
            self.nc.clear_and_free_semaphores(self.used)
            self.nc.all_engine_barrier()

    def sb(self, name, shape, dt=F32):
        return self.ctx.enter_context(self.nc.sbuf_tensor(f"{self.tag}_{name}", shape, dt))

    def ps(self, name, shape, dt=F32):
        return self.ctx.enter_context(self.nc.psum_tensor(f"{self.tag}_ps_{name}", shape, dt))

    def sem(self, name):
        self.used.append(self.nc.alloc_semaphore(f"{self.tag}_s_{name}"))
        return self.used[-1]

    def sems(self, name, n=U):
        return [self.sem(f"{name}{i}") for i in range(n)]

    def norm(self, name, rows):
        return Norm(self.sb, self.sem, f"{self.tag}_{name}", rows)


def edge_rows(table, at, width=D):
    return table[bass.ds(at, GE), :].rearrange("(u p) f -> p u f", p=P)


def node_rows(table, at):
    return table[bass.ds(at, GN), :].rearrange("(p j) f -> p j f", j=RN)


def over_parts(row, at, parts):
    return row[bass.ds(at, GE)].partition_broadcast(parts)


class Env:
    pass


def build(nc, x, node_type, src_idx, dst_idx, etype_row, dst_row, chunk_id, consts, weights, out):
    e = Env()
    e.x, e.out = x, out
    e.etype_row = etype_row

    def dram(name, shape, dt=F32):
        return nc.dram_tensor(name, shape, dt).ap()

    e.T0 = dram("t0", [NP, TW])
    e.XD = dram("xd", [EP, TW])
    e.VT = dram("vt", [D, EP])
    e.U1 = dram("u1", [2 * EP, D])
    e.SD = dram("sd", [EP, D])
    e.U2 = dram("u2", [EP + NP, D])
    e.U3 = dram("u3", [EP + NP, D])
    e.XH1 = dram("xh1", [P, EP])
    e.X2T = dram("x2t", [D, EP])
    e.XH3 = dram("xh3", [P, EP])
    e.same_prev = dram("same_prev", [EP])
    e.same_next = dram("same_next", [EP])
    e.logit = dram("logit", [EP])
    e.alpha = dram("alpha", [EP])
    e.cosim = dram("cosim", [EP])
    e.gate = dram("gate", [EP])
    e.meta_i = dram("meta_i", [2, EP], I32)
    e.meta_f = dram("meta_f", [2, EP])

    with ExitStack() as ctx:
        keep = Scope(nc, ctx, "keep")
        e.pe_passed, e.sp_passed, e.pool_passed = [keep.sem(f"{n}_passed") for n in ("pe", "sp", "pool")]
        e.cst = keep.sb("consts", [P, CONST_W])
        e.wts = keep.sb("weights", [P, WEIGHT_W])
        e.C = {n: e.cst[:, a:b] for n, (a, b) in CONST_AT.items()}
        e.W = {n: e.wts[:, a:b] for n, (a, b) in WEIGHT_AT.items()}
        e.relu_b = keep.sb("relu_b", [P, D])
        e.bq8 = keep.sb("bq8", [P, 1])
        e.bfo = keep.sb("bfo", [P, D])
        e.gather0 = keep.sb("gather0", [P, NG, 2 * TU], I32)
        e.scat_ptr = keep.sb("scat_ptr", [P, CH], I32)
        e.scat_out = keep.sb("scat_out", [P, CH], I32)
        e.ptr_pay = keep.sb("ptr_pay", [P, CH, 2])
        e.ptrs = keep.sb("ptrs", [P, CH, 2])
        e.has = keep.sb("has", [P, CH])
        e.idx1 = keep.sb("idx1", [P, CH], I32)
        e.idxsd = keep.sb("idxsd", [P, CH], I32)
        e.idx2 = keep.sb("idx2", [P, CH], I32)
        e.segc = keep.sb("segc", [P, CH])
        e.segn = keep.sb("segn", [P, CH])
        meta(nc, e, dst_row, chunk_id, src_idx, dst_idx, consts, weights)
        node_table(nc, e, node_type)
        dense(nc, e)
        scores(nc, e)
        softmax(nc, e)
        attend(nc, e)
        difference(nc, e)
        propagate(nc, e)
        mlp(nc, e)
        heads(nc, e)


def meta(nc, e, dst_row, chunk_id, src_idx, dst_idx, consts, weights):
    with ExitStack() as ctx:
        s = Scope(nc, ctx, "meta")
        dst = s.sb("dst", [P, CH], I32)
        prv = s.sb("prev", [P, CH], I32)
        nxt = s.sb("next", [P, CH], I32)
        eid = s.sb("eid", [P, CH])
        dstf = s.sb("dstf", [P, CH])
        tmp = s.sb("tmp", [P, CH])
        start = s.sb("start", [P, CH])
        rows = s.sb("rows", [P, P + 1])
        ends = s.sb("ends", [P, P])
        carry = s.sb("carry", [P, 1])
        si = s.sb("si", [P, 2, CH], I32)
        sig = s.sb("sig", [P, 256])
        row_sum = s.sb("row_sum", [P, 1])
        pt = s.ps("pt", [P, P])
        pc = s.ps("pc", [P, 1])
        loaded, chain, turned, carried, stored, back = [s.sem(n) for n in
                                                        ("loaded", "chain", "turned", "carried", "stored", "back")]
        sig_e, weights_in, row_done, meta_done = s.sem("sig_e"), s.sem("weights_in"), s.sem("row_done"), s.sem("meta_done")
        local_done = s.sem("local_done")

        with nc.Block() as block:
            @block.sync
            def _(sp):
                chunks = lambda off: dst_row[off:off + EP].rearrange("(p j) -> p j", j=CH)
                sp.dma_start(dst[:, :], chunks(1)).then_inc(loaded, 16)
                sp.dma_start(prv[:, :], chunks(0)).then_inc(loaded, 16)
                sp.dma_start(nxt[:, :], chunks(2)).then_inc(loaded, 16)
                sp.dma_start(eid[:, :], chunk_id).then_inc(loaded, 16)
                sp.dma_start(e.cst[:, :], consts).then_inc(loaded, 16)
                sp.dma_start(e.wts[:, :], weights).then_inc(weights_in, 16)
                sp.dma_start(e.gather0[:, :, 0:TU], src_idx).then_inc(back, 16)
                sp.dma_start(e.gather0[:, :, TU:2 * TU], dst_idx).then_inc(back, 16)
                wait(sp, meta_done, 1, e.sp_passed)
                rows_of = lambda t: t.rearrange("(p j) -> p j", j=CH)
                sp.dma_start(rows_of(e.same_prev), e.segc[:, :]).then_inc(stored, 16)
                sp.dma_start(rows_of(e.same_next), e.segn[:, :]).then_inc(stored, 16)
                sp.dma_start(rows_of(e.meta_f[0]), eid[:, :]).then_inc(stored, 16)
                sp.dma_start(rows_of(e.meta_f[1]), start[:, :]).then_inc(stored, 16)
                for i in range(2):
                    sp.dma_start(rows_of(e.meta_i[i]), si[:, i, :]).then_inc(stored, 16)
                wait(sp, stored, 96, e.sp_passed)
                major = lambda t: t.rearrange("(t p) -> p t", p=P)
                sp.dma_start(e.scat_ptr[:, :], major(e.meta_i[0]), allow_slow_non_contiguous=True).then_inc(back, 16)
                sp.dma_start(e.scat_out[:, :], major(e.meta_i[1]), allow_slow_non_contiguous=True).then_inc(back, 16)
                sp.dma_start(e.ptr_pay[:, :, 0], major(e.meta_f[0]), allow_slow_non_contiguous=True).then_inc(back, 16)
                sp.dma_start(e.ptr_pay[:, :, 1], major(e.meta_f[1]), allow_slow_non_contiguous=True).then_inc(back, 16)
                wait(sp, back, 96, e.sp_passed)

            @block.scalar
            def _(act):
                act.wait_ge(weights_in, 16)
                act.activation(sig[0:D, :], e.W["skip"][0:D, :], ACT.Sigmoid).then_inc(sig_e, 1)

            @block.vector
            def _(v):
                n = [0]

                def link(ins):
                    n[0] += 1
                    ins.then_inc(chain, 1)
                    v.wait_ge(chain, n[0])

                v.wait_ge(weights_in, 16)
                v.wait_ge(sig_e, 1)
                link(v.tensor_tensor(e.W["a"][0:D, :], e.W["a"][0:D, :], sig[0:D, :], ALU.mult))
                att = e.W["att"].rearrange("p (c m) -> p c m", c=4)
                pri = e.W["pri"].unsqueeze(2).broadcast_to([P, 4, D])
                link(v.tensor_tensor(att, att, pri, ALU.mult))
                link(v.tensor_scalar(e.W["att"], e.W["att"], 1.0 / 8.0, None, ALU.mult))
                link(v.tensor_scalar(e.relu_b[:, :], e.W["bffn_row"], 0.0, None, ALU.max))
                link(v.tensor_tensor(e.bfo[:, :], e.W["bf_row"], e.W["bo_row"], ALU.add))
                link(v.tensor_tensor(e.W["wob"], e.W["wob"], e.W["bf_64"], ALU.add))
                link(v.tensor_tensor(e.W["wob"][:, D:P], e.W["wob"][:, D:P], e.W["beta_64"], ALU.add))
                for w in (e.W["wfx"], e.W["wob"]):
                    link(v.tensor_reduce(row_sum[:, :], w[:, 0:D], AX, ALU.add))
                    link(v.tensor_scalar(row_sum[:, :], row_sum[:, :], 1.0 / D, None, ALU.mult))
                    link(v.tensor_scalar(w[:, 0:D], w[:, 0:D], row_sum[:, 0:1], None, ALU.subtract))
                link(v.tensor_scalar(e.bq8[:, :], e.W["bq"], 1.0 / 8.0, None, ALU.mult))
                v.wait_ge(loaded, 80)
                link(v.tensor_tensor(e.segc[:, :], dst[:, :], prv[:, :], ALU.is_equal))
                link(v.tensor_tensor(e.segn[:, :], dst[:, :], nxt[:, :], ALU.is_equal))
                link(v.tensor_copy(dstf[:, :], dst[:, :]))
                link(v.tensor_scalar(tmp[:, :], dstf[:, :], TW / 2.0, TW / 2.0 - 1.0, ALU.mult, ALU.add))
                link(v.scalar_tensor_tensor(out=si[:, 0, :], in0=e.segn[:, :], scalar=FAR, in1=tmp[:, :],
                                            op0=ALU.mult, op1=ALU.add))
                link(v.scalar_tensor_tensor(out=si[:, 1, :], in0=e.segc[:, :], scalar=FAR, in1=dstf[:, :],
                                            op0=ALU.mult, op1=ALU.add))
                link(v.tensor_tensor(tmp[:, :], eid[:, :], e.segc[:, :], ALU.mult))
                link(v.tensor_tensor(tmp[:, :], eid[:, :], tmp[:, :], ALU.subtract))
                v.tensor_tensor_scan(start[:, :], tmp[:, :], tmp[:, :], 0.0, ALU.max, ALU.max).then_inc(local_done, 1)
                link(v.memset(rows[0:1, :], 0.0))
                v.wait_ge(turned, 1)
                link(v.tensor_copy(ends[0:1, :], pt[0:1, :]))
                v.tensor_tensor_scan(rows[0:1, 1:P + 1], ends[0:1, :], ends[0:1, :], 0.0,
                                     ALU.max, ALU.max).then_inc(row_done, 1)
                v.wait_ge(carried, 1)
                link(v.tensor_copy(carry[:, :], pc[:, :]))
                v.tensor_scalar(start[:, :], start[:, :], carry[:, 0:1], None, ALU.max).then_inc(meta_done, 1)

            @block.tensor
            def _(pe):
                wait(pe, loaded, 80, e.pe_passed)
                wait(pe, local_done, 1, e.pe_passed)
                pe.transpose(pt[0:1, :], start[:, CH - 1:CH], e.C["ident"]).then_inc(turned, 1)
                wait(pe, row_done, 1, e.pe_passed)
                pe.matmul(pc[:, :], rows[0:1, 0:P], e.C["ones"][0:1, 0:1], start=True, stop=True).then_inc(carried, 1)


def node_table(nc, e, node_type):
    UT = 9
    with ExitStack() as ctx:
        s = Scope(nc, ctx, "tab")
        types = s.sb("types", [P, NG * RN], I32)
        row = [s.sb(f"row{i}", [P, RN, TW]) for i in range(UT)]
        xin = [s.sb(f"x{i}", [P, RN, D]) for i in range(UT)]
        loaded, copied, typed, stored = s.sems("loaded", UT), s.sem("copied"), s.sem("typed"), s.sems("stored", UT)
        types_in, cleared = s.sem("types_in"), s.sem("cleared")
        with nc.Block() as block:
            @block.sync
            def _(sp):
                sp.dma_start(types[:, :], node_type).then_inc(types_in, 16)
                wait(sp, cleared, UT, e.sp_passed)

                def body(st):
                    if st.on():
                        wait(sp, copied, st.n - (UT - 1), e.sp_passed)
                        sp.dma_start(xin[st.s][:, :, :], node_rows(e.x, st.n * GN)).then_inc(loaded[st.s], 16)
                run_groups(sp, body, UT, 0, 1)

            @block.vector
            def _(v):
                for i in range(UT):
                    v.memset(row[i][:, :, :], 0.0).then_inc(cleared, 1)
                v.wait_ge(types_in, 16)

                def body(st):
                    if st.on():
                        v.wait_ge(loaded[st.s], 16 * (st.k + 1))
                        wait(v, stored[st.s], 16 * st.k)
                        v.tensor_copy(row[st.s][:, :, 0:D], xin[st.s][:, :, :]).then_inc(copied, 1)
                        v.tensor_copy(row[st.s][:, :, D], types[:, bass.ds(st.n * RN, RN)]).then_inc(typed, 1)
                run_groups(v, body, UT, 0, 1)

            @block.scalar
            def _(act):
                def body(st):
                    if st.on():
                        act.wait_ge(copied, st.n + 1)
                        act.wait_ge(typed, st.n + 1)
                        act.dma_start(node_rows(e.T0, st.n * GN), row[st.s][:, :, :]).then_inc(stored[st.s], 16)
                run_groups(act, body, UT, 0, 1)
                for i in range(UT):
                    act.wait_ge(stored[i], 16 * (NG // UT))


def dense(nc, e):
    with ExitStack() as ctx:
        s = Scope(nc, ctx, "den")
        slots = lambda name: [s.sb(f"{name}_{i}", [P, RN, D]) for i in range(U)]
        xin, x2, x2b, h2, x3, x3b, h3, hb, hx, x4 = [slots(n) for n in
                                                     ("x", "x2", "x2b", "h2", "x3", "x3b", "h3", "hb", "hx", "x4")]
        h2t = s.sb("h2t", [P, GE])
        h3t = s.sb("h3t", [P, GE])
        hid = s.sb("hid", [P, 2, GE])
        f1 = s.sb("f1", [P, RN, D])
        ps_t2, ps_t3 = s.ps("t2", [P, GE]), s.ps("t3", [P, GE])
        ps_hid = s.ps("hid", [P, 2, GE])
        ps_m, ps_h = [s.ps(f"m{i}", [P, RN, D]) for i in range(U)], s.ps("h", [P, RN, D])
        n2, n3, n4 = s.norm("n2", RN), s.norm("n3", RN), s.norm("n4", RN)
        x_in, h2_out, h3_out, x4_out = s.sems("x_in"), s.sems("h2_out"), s.sems("h3_out"), s.sems("x4_out")
        x2_done, x2b_done, h2_done, x3_done, x3b_done, h3_done, hb_done, hx_done, x4_done = [
            s.sem(n) for n in ("x2", "x2b", "h2", "x3", "x3b", "h3", "hb", "hx", "x4")]
        t2, t2_kept, hid_ready, hid_kept, m_ready = [s.sem(n) for n in ("t2", "t2k", "hidr", "hidk", "mr")]
        t3, t3_kept, h_ready = [s.sem(n) for n in ("t3", "t3k", "hr")]
        idx_c, ptr_out = s.sem("idx_c"), s.sems("ptr_out")
        sidx = [s.sb(f"sidx{i}", [P, TU], I32) for i in range(U)]
        spay = [s.sb(f"spay{i}", [P, TU, 2]) for i in range(U)]
        rows = lambda b: b.unsqueeze(1).broadcast_to([P, RN, D])

        with nc.Block() as block:
            @block.gpsimd
            def _(pool):
                pairs = e.T0.rearrange("n (a b) -> (n a) b", b=2)

                def body(st):
                    f, g = st.back(3), st.back(4)
                    if st.on():
                        i = st.s
                        wait(pool, x_in[i], 16 * (st.k + 1), e.pool_passed)
                        wait(pool, n2.centered, st.n - (U - 1), e.pool_passed)
                        pool.tensor_tensor(x2[i][:, :, :], xin[i][:, :, :], rows(e.relu_b[:, :]), ALU.add).then_inc(x2_done, 1)
                        wait(pool, x3_done, st.n - (U - 1), e.pool_passed)
                        wait(pool, x2_done, st.n + 1, e.pool_passed)
                        pool.tensor_tensor(x2b[i][:, :, :], x2[i][:, :, :], rows(e.W["b1_row"]), ALU.add).then_inc(x2b_done, 1)
                        wait(pool, ptr_out[i], 16 * TU * st.k, e.pool_passed)
                        pool.tensor_copy(sidx[i][:, :], e.scat_ptr[:, bass.ds(st.n * TU, TU)]).then_inc(idx_c, 1)
                        pool.tensor_copy(spay[i][:, :, :], e.ptr_pay[:, bass.ds(st.n * TU, TU), :]).then_inc(idx_c, 1)
                        wait(pool, idx_c, (st.n + 1) * 2, e.pool_passed)
                        for u in range(TU):
                            pool.indirect_dma_start(pairs, bass.IndirectOffsetOnAxis(ap=sidx[i][:, u:u + 1], axis=0),
                                                    spay[i][:, u, :], None, bounds_check=NP * TW // 2 - 1,
                                                    oob_is_err=False).then_inc(ptr_out[i], 16)
                    if f.on():
                        wait(pool, x3_done, f.n + 1, e.pool_passed)
                        wait(pool, hx_done, f.n - (U - 1), e.pool_passed)
                        pool.tensor_tensor(x3b[f.s][:, :, :], x3[f.s][:, :, :], rows(e.W["beta"]), ALU.add).then_inc(x3b_done, 1)
                    if g.on():
                        wait(pool, hb_done, g.n + 1, e.pool_passed)
                        wait(pool, x3b_done, g.n + 1, e.pool_passed)
                        wait(pool, x4_done, g.n - (U - 1), e.pool_passed)
                        pool.tensor_tensor(hx[g.s][:, :, :], hb[g.s][:, :, :], x3b[g.s][:, :, :], ALU.add).then_inc(hx_done, 1)
                run_groups(pool, body, U, 4)
                for i in range(U):
                    wait(pool, ptr_out[i], 16 * TU * (NG // U), e.pool_passed)

            @block.sync
            def _(sp):
                def body(st):
                    if st.on():
                        wait(sp, x2_done, st.n - (U - 1), e.sp_passed)
                        sp.dma_start(xin[st.s][:, :, :], node_rows(e.x, st.n * GN)).then_inc(x_in[st.s], 16)
                    b = st.back(2)
                    if b.on():
                        wait(sp, h2_done, b.n + 1, e.sp_passed)
                        sp.dma_start(node_rows(e.U2, b.n * GN + EP), h2[b.s][:, :, :]).then_inc(h2_out[b.s], 16)
                    b = st.back(4)
                    if b.on():
                        wait(sp, h3_done, b.n + 1, e.sp_passed)
                        sp.dma_start(node_rows(e.U3, b.n * GN + EP), h3[b.s][:, :, :]).then_inc(h3_out[b.s], 16)
                    b = st.back(6)
                    if b.on():
                        wait(sp, x4_done, b.n + 1, e.sp_passed)
                        sp.dma_start(node_rows(e.out, b.n * GN), x4[b.s][:, :, :]).then_inc(x4_out[b.s], 16)
                run_groups(sp, body, U, 6)
                for sems in (h2_out, h3_out, x4_out):
                    for i in range(U):
                        wait(sp, sems[i], 16 * (NG // U), e.sp_passed)

            @block.vector
            def _(v):
                def body(st):
                    d, f, g = st, st.back(2), st.back(4)
                    cd, cf, cg = (Chain(v, n.chain, b, k) for n, b, k in ((n2, d, 2), (n3, f, 2), (n4, g, 4)))
                    if g.on():
                        v.wait_ge(h_ready, g.n + 1)
                        wait(v, hx_done, g.n - (U - 1))
                        v.tensor_tensor(hb[g.s][:, :, :], ps_h[:, :, :], rows(e.bfo[:, :]), ALU.add).then_inc(hb_done, 1)
                    if f.on():
                        v.wait_ge(m_ready, f.n + 1)
                        v.wait_ge(x2b_done, f.n + 1)
                        wait(v, x3b_done, f.n - (U - 1))
                        v.tensor_tensor(x3[f.s][:, :, :], ps_m[f.s][:, :, :], x2b[f.s][:, :, :], ALU.add).then_inc(x3_done, 1)
                    if g.on():
                        v.wait_ge(hb_done, g.n + 1)
                        cg.put(n4.total(v, hb[g.s][:, :, :]))
                    if d.on():
                        v.wait_ge(x2_done, d.n + 1)
                        cd.put(n2.total(v, x2[d.s][:, :, :]))
                    if g.on():
                        cg.join()
                        n4.shift(v, hb[g.s][:, :, :])
                    if f.on():
                        v.wait_ge(x3_done, f.n + 1)
                        cf.put(n3.total(v, x3[f.s][:, :, :]))
                    if d.on():
                        cd.join()
                        n2.shift(v, x2[d.s][:, :, :])
                    if f.on():
                        cf.join()
                        n3.shift(v, x3[f.s][:, :, :])
                    for norm, b in ((n4, g), (n2, d), (n3, f)):
                        if b.on():
                            norm.sumsq(v, b)
                    for norm, b, c in ((n4, g, cg), (n2, d, cd)):
                        if b.on():
                            v.wait_ge(norm.rooted, b.n + 1)
                            c.put(v.reciprocal(norm.rstd[:, :], norm.std[:, :]))
                    if g.on():
                        cg.join()
                        cg.put(v.tensor_tensor(f1[:, :, :], n4.cent[:, :, :], n4.over(n4.rstd), ALU.mult))
                    if d.on():
                        cd.join()
                        wait(v, h2_out[d.s], 16 * d.k)
                        n2.relu_to(v, h2[d.s][:, :, :]).then_inc(h2_done, 1)
                        cd.end()
                    if f.on():
                        v.wait_ge(n3.rooted, f.n + 1)
                        cf.put(v.reciprocal(n3.rstd[:, :], n3.std[:, :]))
                    if g.on():
                        cg.join()
                        cg.put(v.tensor_tensor(f1[:, :, :], f1[:, :, :], rows(e.W["gamma"]), ALU.mult))
                    if f.on():
                        cf.join()
                        wait(v, h3_out[f.s], 16 * f.k)
                        n3.relu_to(v, h3[f.s][:, :, :]).then_inc(h3_done, 1)
                        cf.end()
                    if g.on():
                        cg.join()
                        v.wait_ge(hx_done, g.n + 1)
                        wait(v, x4_out[g.s], 16 * g.k)
                        v.tensor_tensor(x4[g.s][:, :, :], f1[:, :, :], hx[g.s][:, :, :], ALU.add).then_inc(x4_done, 1)
                        cg.end()
                run_groups(v, body, U, 4)

            @block.scalar
            def _(a):
                eps = e.C["eps"]

                def body(st):
                    d, f, g, d1, f1 = st, st.back(2), st.back(4), st.back(1), st.back(3)
                    if d1.on():
                        a.wait_ge(t2, d1.n + 1)
                        a.copy(h2t[:, :], ps_t2[:, :]).then_inc(t2_kept, 1)
                    if f1.on():
                        a.wait_ge(t3, f1.n + 1)
                        a.copy(h3t[:, :], ps_t3[:, :]).then_inc(t3_kept, 1)
                    if g.on():
                        n4.square(a, g)
                    if d.on():
                        n2.square(a, d)
                    if d1.on():
                        a.wait_ge(hid_ready, d1.n + 1)
                        a.activation(hid[:, :, :], ps_hid[:, :, :], ACT.Relu, bias=e.W["b0"]).then_inc(hid_kept, 1)
                    if f.on():
                        n3.square(a, f)
                    for norm, b in ((n4, g), (n2, d), (n3, f)):
                        if b.on():
                            norm.root(a, b, eps)
                run_groups(a, body, U, 4)

            @block.tensor
            def _(pe):
                def turn(ps, rows):
                    for c in range(4):
                        m = pe.transpose(ps[:, c * P:(c + 1) * P], rows[:, 2 * c:2 * c + 2, :].rearrange("p a f -> p (a f)"),
                                         e.C["ident"])
                    return m

                def body(st):
                    d, f = st.back(1), st.back(3)
                    if d.on():
                        wait(pe, h2_done, d.n + 1, e.pe_passed)
                        wait(pe, t2_kept, d.n, e.pe_passed)
                        turn(ps_t2, h2[d.s]).then_inc(t2, 1)
                    if f.on():
                        wait(pe, h3_done, f.n + 1, e.pe_passed)
                        wait(pe, t3_kept, f.n, e.pe_passed)
                        turn(ps_t3, h3[f.s]).then_inc(t3, 1)
                    if d.on():
                        wait(pe, t2_kept, d.n + 1, e.pe_passed)
                        wait(pe, hid_kept, d.n, e.pe_passed)
                        for a in range(2):
                            m = pe.matmul(ps_hid[:, a, :], e.W["w0"][64 * a:64 * a + 64, :], h2t[64 * a:64 * a + 64, :],
                                          start=True, stop=True)
                        m.then_inc(hid_ready, 1)
                    if f.on():
                        wait(pe, t3_kept, f.n + 1, e.pe_passed)
                        wait(pe, hb_done, f.n, e.pe_passed)
                        for c in range(4):
                            m = pe.matmul(ps_h[:, 2 * c:2 * c + 2, :], h3t[:, c * P:(c + 1) * P],
                                          e.W["wf2"], start=(c == 0), stop=(c == 3), skip_group_check=True)
                        m.then_inc(h_ready, 1)
                    if d.on():
                        wait(pe, hid_kept, d.n + 1, e.pe_passed)
                        wait(pe, x3_done, d.n - (U - 1), e.pe_passed)
                        for j in range(RN):
                            a, c = j % 2, j // 2
                            m = pe.matmul(ps_m[d.s][:, j, :], hid[:, a, c * P:(c + 1) * P], e.W["w1"],
                                          start=(j == 0), stop=(j == RN - 1), skip_group_check=True)
                        m.then_inc(m_ready, 1)
                run_groups(pe, body, U, 4)


def scores(nc, e):
    with ExitStack() as ctx:
        s = Scope(nc, ctx, "sc")
        R = 2 * TU
        idx = [s.sb(f"idx{i}", [P, R], I32) for i in range(U)]
        xg = [s.sb(f"xg{i}", [P, R, TW]) for i in range(U)]
        hid = [s.sb(f"h{i}", [P, R, D]) for i in range(U)]
        onehot = s.sb("onehot", [P, R, 4])
        hx = [s.sb(f"hx{i}", [P, R, 4, D]) for i in range(U)]
        ht = s.sb("ht", [P, 4, GE])
        et = [s.sb(f"et{i}", [P, GE], I32) for i in range(U)]
        qx = s.sb("qx", [P, 4, GE])
        kv = [s.sb(f"kv{i}", [P, GE]) for i in range(U)]
        prod = s.sb("prod", [D, GE])
        lrow = [s.sb(f"lrow{i}", [1, GE]) for i in range(U)]
        ps_t = s.ps("t", [P, 4, GE])
        ps_q, ps_kv, ps_r, ps_l = s.ps("q", [P, GE]), s.ps("kv", [P, GE]), s.ps("r", [D, GE]), s.ps("l", [1, GE])
        nrm = s.norm("n", R)
        gathered, et_in, h_out, xd_out, v_out, l_out = [s.sems(n) for n in ("g", "et", "ho", "xd", "vo", "lo")]
        idx_c, h_done, hx_done, turned, ht_kept, q_ready, kv_ready = [
            s.sem(n) for n in ("ic", "h", "hx", "tu", "hk", "q", "kv")]
        q_used, r_ready, kv_kept, prod_done, l_ready, l_kept = [s.sem(n) for n in ("qu", "rr", "kvk", "pd", "lr", "lk")]
        ptr_c = s.sem("ptr")

        with nc.Block() as block:
            @block.gpsimd
            def _(pool):
                def body(st):
                    if not st.on():
                        return
                    i = st.s
                    wait(pool, gathered[i], 16 * R * st.k, e.pool_passed)
                    pool.tensor_copy(idx[i][:, :], e.gather0[:, st.n, :] if isinstance(st.n, int) else
                                     e.gather0[:, bass.ds(st.n, 1), :].rearrange("p a r -> p (a r)")).then_inc(idx_c, 1)
                    wait(pool, idx_c, st.n + 1, e.pool_passed)
                    wait(pool, h_done, st.n - (U - 1), e.pool_passed)
                    wait(pool, ptr_c, st.n - (U - 1), e.pool_passed)
                    wait(pool, xd_out[i], 16 * st.k, e.pool_passed)
                    for u in range(R):
                        pool.indirect_dma_start(xg[i][:, u, :], None, e.T0,
                                                bass.IndirectOffsetOnAxis(ap=idx[i][:, u:u + 1], axis=0),
                                                bounds_check=NP - 1, oob_is_err=False).then_inc(gathered[i], 16)
                run_groups(pool, body, U, 0)

            @block.sync
            def _(sp):
                def body(st):
                    if st.on():
                        wait(sp, q_used, st.n - (U - 1), e.sp_passed)
                        sp.dma_start(et[st.s][:, :], over_parts(e.etype_row, st.n * GE, P)).then_inc(et_in[st.s], 16)
                        wait(sp, gathered[st.s], 16 * R * (st.k + 1), e.sp_passed)
                        sp.dma_start(edge_rows(e.XD, st.n * GE, TW), xg[st.s][:, TU:R, :]).then_inc(xd_out[st.s], 16)
                    b = st.back(1)
                    if b.on():
                        wait(sp, h_done, b.n + 1, e.sp_passed)
                        sp.dma_start(edge_rows(e.U1, b.n * GE + EP), hid[b.s][:, 0:TU, :]).then_inc(h_out[b.s], 16)
                    b = st.back(3)
                    if b.on():
                        wait(sp, kv_kept, b.n + 1, e.sp_passed)
                        sp.dma_start(e.VT[:, bass.ds(b.n * GE, GE)], kv[b.s][D:P, :]).then_inc(v_out[b.s], 16)
                    b = st.back(5)
                    if b.on():
                        wait(sp, l_kept, b.n + 1, e.sp_passed)
                        sp.dma_start(e.logit[bass.ds(b.n * GE, GE)].unsqueeze(0), lrow[b.s][0:1, :]).then_inc(l_out[b.s], 16)
                run_groups(sp, body, U, 5)
                for sems in (xd_out, h_out, v_out, l_out):
                    for i in range(U):
                        wait(sp, sems[i], 16 * (NG // U), e.sp_passed)

            @block.vector
            def _(v):
                def body(st):
                    b, g = st.back(2), st.back(3)
                    c = Chain(v, nrm.chain, st, 3)

                    def mask(r):
                        return v.scalar_tensor_tensor(out=qx[:, r, :], in0=et[b.s][:, :], scalar=e.C["rels"][:, r:r + 1],
                                                      in1=ps_q[:, :], op0=ALU.is_equal, op1=ALU.mult)

                    if st.on():
                        v.wait_ge(gathered[st.s], 16 * R * (st.k + 1))
                        c.put(nrm.total(v, xg[st.s][:, :, 0:D]))
                    if b.on():
                        v.wait_ge(q_ready, b.n + 1)
                        v.wait_ge(et_in[b.s], 16 * (b.k + 1))
                        wait(v, r_ready, b.n)
                        mask(0)
                    if st.on():
                        c.join()
                        nrm.shift(v, xg[st.s][:, :, 0:D])
                    if b.on():
                        mask(1)
                        mask(2)
                        mask(3).then_inc(q_used, 1)
                    if g.on():
                        v.wait_ge(r_ready, g.n + 1)
                        v.wait_ge(kv_kept, g.n + 1)
                        wait(v, l_ready, g.n)
                        v.tensor_tensor(prod[:, :], ps_r[:, :], kv[g.s][0:D, :], ALU.mult).then_inc(prod_done, 1)
                    if st.on():
                        nrm.sumsq(v, st)
                        v.tensor_copy(e.ptrs[:, bass.ds(st.n * TU, TU), :], xg[st.s][:, 0:TU, TW - 2:TW]).then_inc(ptr_c, 1)
                        wait(v, hx_done, st.n)
                        c.put(v.tensor_tensor(onehot[:, :, :], e.C["types"].unsqueeze(1).broadcast_to([P, R, 4]),
                                              xg[st.s][:, :, D:D + 1].broadcast_to([P, R, 4]), ALU.is_equal))
                        nrm.recip(v, c, st)
                        wait(v, h_out[st.s], 16 * st.k)
                        nrm.relu_to(v, hid[st.s][:, :, :]).then_inc(h_done, 1)
                        v.wait_ge(h_done, st.n + 1)
                        wait(v, turned, 2 * (st.n - (U - 1)))
                        for r in range(2):
                            m = v.tensor_tensor(hx[st.s][:, r * TU:(r + 1) * TU, :, :],
                                                hid[st.s][:, r * TU:(r + 1) * TU, :].unsqueeze(2).broadcast_to([P, TU, 4, D]),
                                                onehot[:, r * TU:(r + 1) * TU, :].unsqueeze(3).broadcast_to([P, TU, 4, D]),
                                                ALU.mult)
                        m.then_inc(hx_done, 1)
                        c.end()
                run_groups(v, body, U, 3)

            @block.scalar
            def _(a):
                def body(st):
                    d, b, g = st.back(1), st.back(2), st.back(4)

                    def keep(side):
                        a.wait_ge(turned, 2 * d.n + side + 1)
                        a.copy(ht[:, 2 * side:2 * side + 2, :], ps_t[:, 2 * side:2 * side + 2, :]).then_inc(ht_kept, 1)

                    if b.on():
                        a.wait_ge(kv_ready, b.n + 1)
                        wait(a, prod_done, b.n - (U - 1))
                        wait(a, v_out[b.s], 16 * b.k)
                        a.copy(kv[b.s][:, :], ps_kv[:, :]).then_inc(kv_kept, 1)
                    if d.on():
                        keep(0)
                    if st.on():
                        nrm.square(a, st)
                    if d.on():
                        keep(1)
                    if g.on():
                        a.wait_ge(l_ready, g.n + 1)
                        wait(a, l_out[g.s], 16 * g.k)
                        a.copy(lrow[g.s][0:1, :], ps_l[0:1, :]).then_inc(l_kept, 1)
                    if st.on():
                        nrm.root(a, st, e.C["eps"])
                run_groups(a, body, U, 4)

            @block.tensor
            def _(pe):
                def body(st):
                    d, b, g = st.back(1), st.back(2), st.back(4)
                    if d.on():
                        wait(pe, hx_done, d.n + 1, e.pe_passed)
                        wait(pe, ht_kept, 2 * d.n, e.pe_passed)
                        for side in range(2):
                            for u in range(TU):
                                for c in range(2):
                                    m = pe.transpose(ps_t[:, 2 * side + c, u * P:(u + 1) * P],
                                                     hx[d.s][:, (1 - side) * TU + u, 2 * c:2 * c + 2, :].rearrange("p a f -> p (a f)"),
                                                     e.C["ident"])
                            m.then_inc(turned, 1)
                    if g.on():
                        wait(pe, prod_done, g.n + 1, e.pe_passed)
                        wait(pe, l_kept, g.n, e.pe_passed)
                        pe.matmul(ps_l[:, :], e.C["ones"][0:D, 0:1], prod[:, :], start=True, stop=True).then_inc(l_ready, 1)
                    if d.on():
                        wait(pe, ht_kept, 2 * d.n + 1, e.pe_passed)
                        wait(pe, q_used, d.n, e.pe_passed)
                        for c in range(2):
                            m = pe.matmul(ps_q[:, :], e.W["q"][:, c * P:(c + 1) * P], ht[:, c, :], start=(c == 0), stop=(c == 1))
                        m.then_inc(q_ready, 1)
                    if b.on():
                        wait(pe, q_used, b.n + 1, e.pe_passed)
                        wait(pe, prod_done, b.n, e.pe_passed)
                        for r in range(4):
                            m = pe.matmul(ps_r[:, :], e.W["att"][:, r * D:(r + 1) * D], qx[:, r, :], start=(r == 0), stop=(r == 3))
                        m.then_inc(r_ready, 1)
                    if d.on():
                        wait(pe, ht_kept, 2 * d.n + 2, e.pe_passed)
                        wait(pe, kv_kept, d.n, e.pe_passed)
                        for c in range(2):
                            m = pe.matmul(ps_kv[:, :], e.W["kv"][:, c * P:(c + 1) * P], ht[:, 2 + c, :], start=(c == 0), stop=(c == 1))
                        m.then_inc(kv_ready, 1)
                run_groups(pe, body, U, 4)


def softmax(nc, e):
    with ExitStack() as ctx:
        s = Scope(nc, ctx, "sm")
        lg, a1, a2, a3, a4, m = [s.sb(n, [P, CH]) for n in ("lg", "a1", "a2", "a3", "a4", "m")]
        ones = s.sb("ones", [P, CH])
        ends = s.sb("ends", [1, 2, P])
        srcs = s.sb("srcs", [P, NG, TU])
        carried = s.sb("carried", [1, P + 1])
        carry = s.sb("carry", [P, 1])
        eid = s.sb("eid", [P, CH], I32)
        eidf = s.sb("eidf", [P, CH])
        ps_a, ps_b, ps_c = s.ps("a", [1, P]), s.ps("b", [1, P]), s.ps("c", [P, 1])
        loaded, stored, chain, p_ready, iot = s.sem("loaded"), s.sem("stored"), s.sem("chain"), s.sem("pr"), s.sem("iot")
        local, turned, row_done, back, alpha_done = [s.sem(n) for n in ("local", "turned", "row", "back", "alpha")]
        max_done = s.sem("maxd")

        with nc.Block() as block:
            @block.sync
            def _(sp):
                sp.dma_start(lg[:, :], e.logit.rearrange("(p j) -> p j", j=CH)).then_inc(loaded, 16)
                wait(sp, alpha_done, 1, e.sp_passed)
                sp.dma_start(e.alpha.rearrange("(p j) -> p j", j=CH), a1[:, :]).then_inc(stored, 16)
                wait(sp, stored, 16, e.sp_passed)

            @block.gpsimd
            def _(pool):
                pool.iota(eid[:, :], [[P, CH]], base=0, channel_multiplier=1).then_inc(iot, 1)

            @block.scalar
            def _(a):
                a.wait_ge(max_done, 1)
                a.activation(m[:, :], lg[:, :], ACT.Exp).then_inc(p_ready, 1)

            @block.tensor
            def _(pe):
                for i in range(4):
                    wait(pe, local, i + 1, e.pe_passed)
                    col = CH - 1 if i % 2 == 0 else 0
                    val = a1 if i % 2 == 0 else a3
                    pre = a2 if i % 2 == 0 else a4
                    pe.transpose(ps_a[:, :], val[:, col:col + 1], e.C["ident"])
                    pe.transpose(ps_b[:, :], pre[:, col:col + 1], e.C["ident"]).then_inc(turned, 1)
                    wait(pe, row_done, i + 1, e.pe_passed)
                    row = carried[0:1, 0:P] if i % 2 == 0 else carried[0:1, 1:P + 1]
                    pe.matmul(ps_c[:, :], row, e.C["ones"][0:1, 0:1], start=True, stop=True).then_inc(back, 1)

            @block.vector
            def _(v):
                n = [0]

                def link(ins):
                    n[0] += 1
                    ins.then_inc(chain, 1)
                    v.wait_ge(chain, n[0])

                def seg_scan(i, val, pre, x, is_max):
                    rev = slice(None, None, -1 if i % 2 else 1)
                    same = e.segn if i % 2 else e.segc
                    link(v.tensor_tensor_scan(pre[:, rev], same[:, rev], ones[:, :], 1.0, ALU.mult, ALU.mult))
                    if is_max:
                        link(v.tensor_scalar(val[:, :], same[:, :], -1.0, BIG, ALU.add, ALU.mult))
                        v.tensor_tensor_scan(val[:, rev], val[:, rev], x[:, rev], -BIG, ALU.add, ALU.max).then_inc(local, 1)
                    else:
                        v.tensor_tensor_scan(val[:, rev], same[:, rev], x[:, rev], 0.0, ALU.mult, ALU.add).then_inc(local, 1)
                    v.wait_ge(turned, i + 1)
                    none = -BIG if is_max else 0.0
                    link(v.memset(carried[0:1, :], none))
                    link(v.tensor_copy(ends[0:1, 0, :], ps_a[:, :]))
                    out = carried[0:1, 1:P + 1] if i % 2 == 0 else carried[0:1, 0:P]
                    if is_max:
                        link(v.tensor_scalar(ends[0:1, 1, :], ps_b[:, :], -1.0, BIG, ALU.add, ALU.mult))
                    else:
                        link(v.tensor_copy(ends[0:1, 1, :], ps_b[:, :]))
                    v.tensor_tensor_scan(out[:, rev], ends[0:1, 1, rev], ends[0:1, 0, rev], none,
                                         ALU.add if is_max else ALU.mult, ALU.max if is_max else ALU.add).then_inc(row_done, 1)
                    v.wait_ge(back, i + 1)
                    link(v.tensor_copy(carry[:, :], ps_c[:, :]))
                    if is_max:
                        link(v.tensor_scalar(pre[:, :], pre[:, :], -1.0, BIG, ALU.add, ALU.mult))
                        link(v.scalar_tensor_tensor(out=val[:, :], in0=pre[:, :], scalar=carry[:, 0:1], in1=val[:, :],
                                                    op0=ALU.add, op1=ALU.max))
                    else:
                        link(v.scalar_tensor_tensor(out=val[:, :], in0=pre[:, :], scalar=carry[:, 0:1], in1=val[:, :],
                                                    op0=ALU.mult, op1=ALU.add))

                link(v.memset(ones[:, :], 1.0))
                v.wait_ge(loaded, 16)
                seg_scan(0, a1, a2, lg, True)
                seg_scan(1, a3, a4, lg, True)
                link(v.tensor_tensor(a1[:, :], a1[:, :], a3[:, :], ALU.max))
                v.tensor_tensor(lg[:, :], lg[:, :], a1[:, :], ALU.subtract).then_inc(max_done, 1)
                v.wait_ge(p_ready, 1)
                seg_scan(2, a1, a2, m, False)
                seg_scan(3, a3, a4, m, False)
                link(v.tensor_tensor(a1[:, :], a1[:, :], a3[:, :], ALU.add))
                link(v.tensor_tensor(a1[:, :], a1[:, :], m[:, :], ALU.subtract))
                link(v.tensor_scalar(a2[:, :], a1[:, :], 0.0, None, ALU.is_equal))
                link(v.tensor_tensor(a1[:, :], a1[:, :], a2[:, :], ALU.add))
                link(v.reciprocal(a1[:, :], a1[:, :]))
                v.tensor_tensor(a1[:, :], a1[:, :], m[:, :], ALU.mult).then_inc(alpha_done, 1)

                v.wait_ge(iot, 1)
                link(v.tensor_copy(eidf[:, :], eid[:, :]))
                last, frst = e.ptrs[:, :, 0], e.ptrs[:, :, 1]
                link(v.tensor_scalar(e.has[:, :], last, 1.0, None, ALU.min))

                def choose(out, ptr, base, off):
                    link(v.tensor_scalar(a4[:, :], base, float(off), None, ALU.add))
                    link(v.tensor_tensor(a3[:, :], ptr, a4[:, :], ALU.subtract))
                    link(v.scalar_tensor_tensor(out=a3[:, :], in0=a3[:, :], scalar=-1.0, in1=e.has[:, :],
                                                op0=ALU.add, op1=ALU.mult))
                    link(v.tensor_tensor(out[:, :], a3[:, :], a4[:, :], ALU.add))

                choose(e.idx1, last, eidf[:, :], EP)
                choose(e.idxsd, frst, eidf[:, :], 0)
                link(v.tensor_copy(srcs[:, :, :], e.gather0[:, :, 0:TU]))
                choose(e.idx2, last, srcs[:, :, :].rearrange("p a b -> p (a b)"), EP)


def attend(nc, e):
    with ExitStack() as ctx:
        s = Scope(nc, ctx, "at")
        vin = [s.sb(f"v{i}", [P, GE]) for i in range(U)]
        et = [s.sb(f"et{i}", [P, GE], I32) for i in range(U)]
        al = [s.sb(f"al{i}", [D, GE]) for i in range(U)]
        same = [s.sb(f"same{i}", [D, GE]) for i in range(U)]
        xd = [s.sb(f"xd{i}", [P, TU, TW]) for i in range(U)]
        vx = [s.sb(f"vx{i}", [P, 4, GE]) for i in range(U)]
        eq = [s.sb(f"eq{i}", [P, 2, GE]) for i in range(U)]
        am = s.sb("am", [D, GE])
        agg = [s.sb(f"agg{i}", [D, GE]) for i in range(U)]
        onehot = s.sb("onehot", [P, TU, 4])
        ysel = [s.sb(f"ysel{i}", [P, TU, 4, D]) for i in range(U)]
        y2 = s.sb("y2", [P, TU, 2, D])
        y1 = s.sb("y1", [P, TU, D])
        hx = [s.sb(f"hx{i}", [P, TU, 2 * D]) for i in range(U)]
        xh = [s.sb(f"xh{i}", [P, GE]) for i in range(U)]
        ps_m, ps_y, ps_t = [s.ps(f"m{i}", [D, GE]) for i in range(U)], s.ps("y", [P, TU, 4, D]), s.ps("t", [P, GE])
        nrm = s.norm("n", TU)
        v_in, et_in, al_in, same_in, xd_in, h_out, xh_out = [s.sems(n) for n in ("v", "et", "al", "sa", "xd", "ho", "xho")]
        vx_low, vx_high, m_ready, am_done, agg_done, y_ready, y_sel, y2_done, y1_done, x1_done, h_done, turned, kept, oh_done, eq_off, eq_done = [
            s.sem(n) for n in ("vxl", "vxh", "mr", "am", "ag", "yr", "ys", "y2", "y1", "x1", "h", "tu", "kept", "oh", "eo", "ed")]

        with nc.Block() as block:
            @block.sync
            def _(sp):
                def body(st):
                    i, at = st.s, st.n * GE
                    if st.on():
                        wait(sp, vx_low, st.n - (U - 1), e.sp_passed)
                        wait(sp, vx_high, st.n - (U - 1), e.sp_passed)
                        for half in range(2):
                            sp.dma_start(vin[i][half * D:(half + 1) * D, :], e.VT[:, bass.ds(at, GE)]).then_inc(v_in[i], 16)
                        sp.dma_start(et[i][:, :], over_parts(e.etype_row, at, P)).then_inc(et_in[i], 16)
                    b = st.back(1)
                    if b.on():
                        wait(sp, agg_done, b.n - (U - 1), e.sp_passed)
                        sp.dma_start(al[b.s][:, :], over_parts(e.alpha, b.n * GE, D)).then_inc(al_in[b.s], 16)
                        sp.dma_start(same[b.s][:, :], over_parts(e.same_prev, b.n * GE, D)).then_inc(same_in[b.s], 16)
                    b = st.back(2)
                    if b.on():
                        wait(sp, x1_done, b.n - (U - 1), e.sp_passed)
                        sp.dma_start(xd[b.s][:, :, :], edge_rows(e.XD, b.n * GE, TW)).then_inc(xd_in[b.s], 16)
                run_groups(sp, body, U, 2)

            @block.gpsimd
            def _(pool):
                def body(st):
                    b = st.back(4)
                    if b.on():
                        i = b.s
                        wait(pool, y_sel, b.n + 1, e.pool_passed)
                        wait(pool, y1_done, b.n, e.pool_passed)
                        pool.tensor_tensor(y2[:, :, :, :], ysel[i][:, :, 0:2, :], ysel[i][:, :, 2:4, :], ALU.add).then_inc(y2_done, 1)
                        wait(pool, y2_done, b.n + 1, e.pool_passed)
                        wait(pool, x1_done, b.n, e.pool_passed)
                        pool.tensor_tensor(y1[:, :, :], y2[:, :, 0, :], y2[:, :, 1, :], ALU.add).then_inc(y1_done, 1)
                        wait(pool, y1_done, b.n + 1, e.pool_passed)
                        wait(pool, turned, b.n - (U - 1), e.pool_passed)
                        pool.tensor_tensor(hx[i][:, :, D:2 * D], y1[:, :, :], xd[i][:, :, 0:D], ALU.add).then_inc(x1_done, 1)
                    if st.on():
                        i = st.s
                        wait(pool, v_in[i], 32 * (st.k + 1), e.pool_passed)
                        wait(pool, eq_done, st.n + 1, e.pool_passed)
                        wait(pool, m_ready, st.n - (U - 1), e.pool_passed)
                        pool.tensor_tensor(vx[i][:, 2:4, :], eq[i][:, :, :],
                                           vin[i][:, :].unsqueeze(1).broadcast_to([P, 2, GE]), ALU.mult).then_inc(vx_high, 1)
                run_groups(pool, body, U, 4)

            @block.vector
            def _(v):
                def body(st):
                    b, f, g = st.back(2), st.back(4), st.back(5)
                    c = Chain(v, nrm.chain, g, 2)

                    def mask(r):
                        return v.scalar_tensor_tensor(out=vx[st.s][:, r, :], in0=et[st.s][:, :], scalar=e.C["rels"][:, r:r + 1],
                                                      in1=vin[st.s][:, :], op0=ALU.is_equal, op1=ALU.mult)

                    if b.on():
                        i = b.s
                        v.wait_ge(m_ready, b.n + 1)
                        v.wait_ge(al_in[i], 16 * (b.k + 1))
                        wait(v, agg_done, b.n)
                        v.tensor_tensor(am[:, :], ps_m[i][:, :], al[i][:, :], ALU.mult).then_inc(am_done, 1)
                    if g.on():
                        v.wait_ge(x1_done, g.n + 1)
                        c.put(nrm.total(v, hx[g.s][:, :, D:2 * D]))
                    if f.on():
                        v.wait_ge(xd_in[f.s], 16 * (f.k + 1))
                        wait(v, y_sel, f.n)
                        v.tensor_tensor(onehot[:, :, :], e.C["types"].unsqueeze(1).broadcast_to([P, TU, 4]),
                                        xd[f.s][:, :, D:D + 1].broadcast_to([P, TU, 4]), ALU.is_equal).then_inc(oh_done, 1)
                    if b.on():
                        v.wait_ge(am_done, b.n + 1)
                        v.wait_ge(same_in[i], 16 * (b.k + 1))
                        wait(v, y_ready, b.n - (U - 1))
                        v.tensor_tensor_scan(agg[i][:, :], same[i][:, :], am[:, :],
                                             0.0 if b.first() else agg[(i - 1) % U][:, GE - 1:GE],
                                             ALU.mult, ALU.add).then_inc(agg_done, 1)
                    if g.on():
                        c.join()
                        nrm.shift(v, hx[g.s][:, :, D:2 * D])
                    if f.on():
                        v.wait_ge(y_ready, f.n + 1)
                        v.wait_ge(oh_done, f.n + 1)
                        wait(v, y2_done, f.n - (U - 1))
                        v.tensor_tensor(ysel[f.s][:, :, :, :], ps_y[:, :, :, :],
                                        onehot[:, :, :].unsqueeze(3).broadcast_to([P, TU, 4, D]), ALU.mult).then_inc(y_sel, 1)
                    if g.on():
                        nrm.sumsq(v, g)
                    if st.on():
                        v.wait_ge(v_in[st.s], 32 * (st.k + 1))
                        v.wait_ge(et_in[st.s], 16 * (st.k + 1))
                        wait(v, m_ready, st.n - (U - 1))
                        mask(0)
                    if g.on():
                        nrm.recip(v, c, g)
                        wait(v, h_out[g.s], 16 * g.k)
                        nrm.relu_to(v, hx[g.s][:, :, 0:D]).then_inc(h_done, 1)
                        c.end()
                    if st.on():
                        mask(1).then_inc(vx_low, 1)
                run_groups(v, body, U, 5)

            @block.scalar
            def _(a):
                def body(st):
                    g, t = st.back(5), st.back(6)
                    if st.on():
                        i = st.s
                        a.wait_ge(et_in[i], 16 * (st.k + 1))
                        wait(a, vx_high, st.n - (U - 1))
                        for r in range(2):
                            m = a.activation(eq[i][:, r, :], et[i][:, :], ACT.Square, bias=e.C["less_rels"][:, 2 + r:3 + r])
                        m.then_inc(eq_off, 1)
                        a.wait_ge(eq_off, st.n + 1)
                        a.activation(eq[i][:, :, :], eq[i][:, :, :], ACT.Relu, bias=e.C["ones"][:, 0:1], scale=-1.0).then_inc(eq_done, 1)
                    if t.on():
                        a.dma_start(edge_rows(e.U1, t.n * GE), hx[t.s][:, :, 0:D]).then_inc(h_out[t.s], 16)
                        a.wait_ge(turned, t.n + 1)
                        wait(a, xh_out[t.s], 16 * t.k)
                        a.copy(xh[t.s][:, :], ps_t[:, :]).then_inc(kept, 1)
                    if g.on():
                        nrm.square(a, g)
                    if t.on():
                        a.wait_ge(kept, t.n + 1)
                        a.dma_start(e.XH1[:, bass.ds(t.n * GE, GE)], xh[t.s][:, :]).then_inc(xh_out[t.s], 16)
                    if g.on():
                        nrm.root(a, g, e.C["eps"])
                        a.wait_ge(h_done, g.n + 1)
                run_groups(a, body, U, 6)
                for sems in (h_out, xh_out):
                    for i in range(U):
                        a.wait_ge(sems[i], 16 * (NG // U))

            @block.tensor
            def _(pe):
                def body(st):
                    d, f, t = st.back(1), st.back(3), st.back(6)
                    if t.on():
                        wait(pe, h_done, t.n + 1, e.pe_passed)
                        wait(pe, kept, t.n, e.pe_passed)
                        for u in range(TU):
                            m = pe.transpose(ps_t[:, u * P:(u + 1) * P], hx[t.s][:, u, :], e.C["ident"])
                        m.then_inc(turned, 1)
                    if d.on():
                        wait(pe, vx_low, d.n + 1, e.pe_passed)
                        wait(pe, vx_high, d.n + 1, e.pe_passed)
                        wait(pe, am_done, d.n - (U - 1), e.pe_passed)
                        for r in range(4):
                            m = pe.matmul(ps_m[d.s][:, :], e.W["msg"][:, r * D:(r + 1) * D], vx[d.s][:, r, :], start=(r == 0), stop=(r == 3))
                        m.then_inc(m_ready, 1)
                    if f.on():
                        wait(pe, agg_done, f.n + 1, e.pe_passed)
                        wait(pe, y_sel, f.n, e.pe_passed)
                        for u in range(TU):
                            m = pe.matmul(ps_y[:, u, :, :], agg[f.s][:, u * P:(u + 1) * P],
                                          e.W["a"][0:D, :].rearrange("p (t f) -> p t f", t=4), start=(u % 2 == 0), stop=(u % 2 == 1),
                                          skip_group_check=True)
                        m.then_inc(y_ready, 1)
                run_groups(pe, body, U, 6)


def start_gathers(e, pool, table, idx_all, idx, gat, gathered, idx_c, st, pos, rows):
    i = st.s
    wait(pool, gathered[i], 16 * TU * st.k, e.pool_passed)
    pool.tensor_copy(idx[i][:, :], idx_all[:, bass.ds(pos * TU, TU)]).then_inc(idx_c, 1)
    wait(pool, idx_c, st.n + 1, e.pool_passed)
    for u in range(TU):
        pool.indirect_dma_start(gat[i][:, u, :], None, table,
                                bass.IndirectOffsetOnAxis(ap=idx[i][:, u:u + 1], axis=0),
                                bounds_check=rows - 1, oob_is_err=False).then_inc(gathered[i], 16)


def difference(nc, e):
    with ExitStack() as ctx:
        s = Scope(nc, ctx, "df")
        idx = [s.sb(f"idx{i}", [P, TU], I32) for i in range(U)]
        hs = [s.sb(f"hs{i}", [P, TU, D]) for i in range(U)]
        hd = [s.sb(f"hd{i}", [D, GE]) for i in range(U)]
        same = [s.sb(f"same{i}", [D, GE]) for i in range(U)]
        lastv = s.sb("lastv", [D, GE])
        hb = [s.sb(f"hb{i}", [D, GE]) for i in range(U)]
        prod = [s.sb(f"prod{i}", [D, GE]) for i in range(U)]
        diff = s.sb("diff", [D, GE])
        sd = [s.sb(f"sd{i}", [D, GE]) for i in range(U)]
        act = s.sb("act", [D, GE])
        junk_s, junk_d = s.sb("junk_s", [P, TU, D]), s.sb("junk_d", [D, GE])
        crow = [s.sb(f"crow{i}", [1, GE]) for i in range(U)]
        sdr = [s.sb(f"sdr{i}", [P, TU, D]) for i in range(U)]
        nacc = s.sb("nacc", [P, 2, NG])
        ntot = s.sb("ntot", [P, 2])
        nsq = s.sb("nsq", [P, 2])
        scale = s.sb("scale", [P, 1])
        cosc = s.sb("cosc", [P, CH])
        ps_t = [s.ps(f"t{i}", [D, GE]) for i in range(U)]
        ps_p, ps_c, ps_b = s.ps("p", [D, GE]), s.ps("c", [1, GE]), s.ps("b", [P, TU, D])
        ps_n = s.ps("n", [P, 2])
        gathered, hd_in, same_in, c_out, sd_out = [s.sems(n) for n in ("g", "hd", "sa", "co", "so")]
        idx_c, turned, last_done, hb_done, prod_done, diff_done, sd_done = [
            s.sem(n) for n in ("ic", "tu", "ld", "hb", "pd", "dd", "sdd")]
        p_ready, relu_done, c_ready, c_kept, b_ready, b_kept, sq1, sq2 = [
            s.sem(n) for n in ("pr", "rd", "cr", "ck", "br", "bk", "sq1", "sq2")]
        cleared, fin, tot_done, n_ready, cos_in, gate_done, rooted, clip_done, g_out = [
            s.sem(n) for n in ("clr", "fin", "td", "nr", "ci", "gd", "rt", "cl", "go")]
        pos = lambda st: st.n * -1 + (NG - 1)

        with nc.Block() as block:
            @block.gpsimd
            def _(pool):
                def body(st):
                    if st.on():
                        wait(pool, turned, st.n - (U - 1), e.pool_passed)
                        wait(pool, sq1, st.n - (U - 1), e.pool_passed)
                        start_gathers(e, pool, e.U1, e.idx1, idx, hs, gathered, idx_c, st, pos(st), 2 * EP)
                run_groups(pool, body, U, 0)

            @block.sync
            def _(sp):
                def body(st):
                    if st.on():
                        i, at = st.s, pos(st) * GE
                        wait(sp, sd_done, st.n - (U - 1), e.sp_passed)
                        sp.dma_start(hd[i][:, :], e.XH1[0:D, bass.ds(at, GE)]).then_inc(hd_in[i], 16)
                        sp.dma_start(same[i][:, :], over_parts(e.same_next, at, D)).then_inc(same_in[i], 16)
                    b = st.back(4)
                    if b.on():
                        wait(sp, c_kept, b.n + 1, e.sp_passed)
                        sp.dma_start(e.cosim[bass.ds(pos(b) * GE, GE)].unsqueeze(0), crow[b.s][0:1, :]).then_inc(c_out[b.s], 16)
                        wait(sp, b_kept, b.n + 1, e.sp_passed)
                        sp.dma_start(edge_rows(e.SD, pos(b) * GE), sdr[b.s][:, :, :]).then_inc(sd_out[b.s], 16)
                run_groups(sp, body, U, 4)
                for sems in (c_out, sd_out):
                    for i in range(U):
                        wait(sp, sems[i], 16 * (NG // U), e.sp_passed)
                sp.dma_start(cosc[:, :], e.cosim.rearrange("(p j) -> p j", j=CH)).then_inc(cos_in, 16)
                wait(sp, gate_done, 1, e.sp_passed)
                sp.dma_start(e.gate.rearrange("(p j) -> p j", j=CH), cosc[:, :]).then_inc(g_out, 16)
                wait(sp, g_out, 16, e.sp_passed)

            @block.vector
            def _(v):
                v.memset(nacc[D:P, :, :], 0.0).then_inc(cleared, 1)

                def body(st):
                    b = st.back(1)
                    if b.on():
                        v.wait_ge(turned, b.n + 1)
                        wait(v, b_ready, b.n - (U - 1))
                        v.tensor_tensor(diff[:, :], ps_t[b.s][:, :], hb[b.s][:, :], ALU.subtract).then_inc(diff_done, 1)
                    if st.on():
                        i = st.s
                        v.wait_ge(hd_in[i], 16 * (st.k + 1))
                        v.wait_ge(same_in[i], 16 * (st.k + 1))
                        v.scalar_tensor_tensor(out=lastv[:, :], in0=same[i][:, :], scalar=-1.0, in1=hd[i][:, :],
                                               op0=ALU.add, op1=ALU.mult).then_inc(last_done, 1)
                    if b.on():
                        v.wait_ge(diff_done, b.n + 1)
                        v.tensor_tensor_scan(sd[b.s][:, ::-1], same[b.s][:, ::-1], diff[:, ::-1],
                                             0.0 if b.first() else sd[(b.s - 1) % U][:, 0:1],
                                             ALU.mult, ALU.add).then_inc(sd_done, 1)
                    if st.on():
                        v.wait_ge(last_done, st.n + 1)
                        wait(v, sq2, st.n - (U - 1))
                        v.tensor_tensor_scan(hb[i][:, ::-1], same[i][:, ::-1], lastv[:, ::-1],
                                             0.0 if st.first() else hb[(i - 1) % U][:, 0:1],
                                             ALU.mult, ALU.subtract).then_inc(hb_done, 1)
                    if b.on():
                        v.tensor_tensor(prod[b.s][:, :], ps_t[b.s][:, :], hb[b.s][:, :], ALU.mult).then_inc(prod_done, 1)
                    if st.on():
                        v.wait_ge(hb_done, st.n + 1)
                    if b.on():
                        v.wait_ge(sd_done, b.n + 1)
                run_groups(v, body, U, 1)
                n = [0]

                def link(ins):
                    n[0] += 1
                    ins.then_inc(fin, 1)
                    v.wait_ge(fin, n[0])

                v.wait_ge(sq1, NG)
                v.wait_ge(sq2, NG)
                v.tensor_reduce(ntot[:, :], nacc[:, :, :], AX, ALU.add).then_inc(tot_done, 1)
                v.wait_ge(rooted, 1)
                link(v.tensor_tensor(scale[:, :], nsq[:, 0:1], nsq[:, 1:2], ALU.mult))
                link(v.tensor_scalar(scale[:, :], scale[:, :], 1e-6, None, ALU.add))
                link(v.reciprocal(scale[:, :], scale[:, :]))
                v.wait_ge(cos_in, 16)
                link(v.tensor_scalar(cosc[:, :], cosc[:, :], scale[:, 0:1], -5.0, ALU.mult, ALU.max))
                v.tensor_scalar(cosc[:, :], cosc[:, :], 5.0, None, ALU.min).then_inc(clip_done, 1)

            @block.scalar
            def _(a):
                def body(st):
                    b = st.back(2)
                    if b.on():
                        a.wait_ge(p_ready, b.n + 1)
                        a.activation(act[:, :], ps_p[:, :], ACT.Relu).then_inc(relu_done, 1)
                    if st.on():
                        a.wait_ge(gathered[st.s], 16 * TU * (st.k + 1))
                        wait(a, sq1, st.n)
                        a.activation(junk_s[:, :, :], hs[st.s][:, :, :], ACT.Square,
                                     accum_out=nacc[:, 0, bass.ds(st.n, 1)]).then_inc(sq1, 1)
                    if b.on():
                        a.wait_ge(b_ready, b.n + 1)
                        wait(a, sd_out[b.s], 16 * b.k)
                        a.copy(sdr[b.s][:, :, :], ps_b[:, :, :]).then_inc(b_kept, 1)
                    if st.on():
                        a.wait_ge(hb_done, st.n + 1)
                        wait(a, sq2, st.n)
                        a.activation(junk_d[:, :], hb[st.s][:, :], ACT.Square,
                                     accum_out=nacc[0:D, 1, bass.ds(st.n, 1)]).then_inc(sq2, 1)
                    if b.on():
                        a.wait_ge(c_ready, b.n + 1)
                        wait(a, c_out[b.s], 16 * b.k)
                        a.copy(crow[b.s][0:1, :], ps_c[0:1, :]).then_inc(c_kept, 1)
                a.wait_ge(cleared, 1)
                run_groups(a, body)
                a.wait_ge(n_ready, 1)
                a.activation(nsq[:, :], ps_n[:, :], ACT.Sqrt).then_inc(rooted, 1)
                a.wait_ge(clip_done, 1)
                a.activation(cosc[:, :], cosc[:, :], ACT.Exp).then_inc(gate_done, 1)

            @block.tensor
            def _(pe):
                def body(st):
                    b = st.back(2)
                    if b.on():
                        wait(pe, prod_done, b.n + 1, e.pe_passed)
                        wait(pe, relu_done, b.n, e.pe_passed)
                        pe.matmul(ps_p[:, :], e.W["proj"][0:D, :], prod[b.s][:, :], start=True, stop=True).then_inc(p_ready, 1)
                        wait(pe, sd_done, b.n + 1, e.pe_passed)
                        wait(pe, b_kept, b.n, e.pe_passed)
                        for u in range(TU):
                            m = pe.transpose(ps_b[:, u, :], sd[b.s][:, u * P:(u + 1) * P], e.C["ident"][0:D, 0:D])
                        m.then_inc(b_ready, 1)
                    if st.on():
                        i = st.s
                        wait(pe, gathered[i], 16 * TU * (st.k + 1), e.pe_passed)
                        wait(pe, prod_done, st.n - (U - 1), e.pe_passed)
                        for u in range(TU):
                            m = pe.transpose(ps_t[i][:, u * P:(u + 1) * P], hs[i][:, u, :], e.C["ident"])
                        m.then_inc(turned, 1)
                    if b.on():
                        wait(pe, relu_done, b.n + 1, e.pe_passed)
                        wait(pe, c_kept, b.n, e.pe_passed)
                        pe.matmul(ps_c[:, :], e.C["ones"][0:D, 0:1], act[:, :], start=True, stop=True).then_inc(c_ready, 1)
                run_groups(pe, body)
                wait(pe, tot_done, 1, e.pe_passed)
                pe.matmul(ps_n[:, :], e.C["ones"], ntot[:, :], start=True, stop=True).then_inc(n_ready, 1)


def propagate(nc, e):
    with ExitStack() as ctx:
        s = Scope(nc, ctx, "pr")
        idx = [s.sb(f"idx{i}", [P, TU], I32) for i in range(U)]
        gat = [s.sb(f"gat{i}", [P, TU, D]) for i in range(U)]
        gm = [s.sb(f"gm{i}", [P, TU, D]) for i in range(U)]
        gate = [s.sb(f"gate{i}", [D, GE]) for i in range(U)]
        same = [s.sb(f"same{i}", [D, GE]) for i in range(U)]
        x1 = [s.sb(f"x1{i}", [D, GE]) for i in range(U)]
        gv = s.sb("gv", [D, GE])
        agg = [s.sb(f"agg{i}", [D, GE]) for i in range(U)]
        ffn = [s.sb(f"ffn{i}", [D, GE]) for i in range(U)]
        x2 = [s.sb(f"x2{i}", [D, GE]) for i in range(U)]
        h2 = [s.sb(f"h2{i}", [P, TU, D]) for i in range(U)]
        ps_t, ps_x = [s.ps(f"t{i}", [D, GE]) for i in range(U)], [s.ps(f"x{i}", [P, TU, D]) for i in range(U)]
        ps_f = s.ps("f", [D, GE])
        nrm = s.norm("n", TU)
        gathered, gate_in, same_in, x1_in, x2_out, h2_out = [s.sems(n) for n in ("g", "ga", "sa", "x1", "x2", "h2")]
        idx_c, gm_done, turned, gv_done, agg_done, f_ready, relu_done, x2_done, x_ready, h_done = [
            s.sem(n) for n in ("ic", "gm", "tu", "gv", "ag", "fr", "rd", "xd", "xr", "hd")]

        with nc.Block() as block:
            @block.gpsimd
            def _(pool):
                def body(st):
                    if st.on():
                        wait(pool, gm_done, st.n - (U - 1), e.pool_passed)
                        start_gathers(e, pool, e.SD, e.idxsd, idx, gat, gathered, idx_c, st, st.n, EP)
                run_groups(pool, body, U, 0)

            @block.sync
            def _(sp):
                def body(st):
                    b = st.back(1)
                    if b.on():
                        wait(sp, agg_done, b.n - (U - 1), e.sp_passed)
                        sp.dma_start(gate[b.s][:, :], over_parts(e.gate, b.n * GE, D)).then_inc(gate_in[b.s], 16)
                        sp.dma_start(same[b.s][:, :], over_parts(e.same_prev, b.n * GE, D)).then_inc(same_in[b.s], 16)
                    b = st.back(3)
                    if b.on():
                        wait(sp, x2_done, b.n - (U - 1), e.sp_passed)
                        sp.dma_start(x1[b.s][:, :], e.XH1[D:P, bass.ds(b.n * GE, GE)]).then_inc(x1_in[b.s], 16)
                    b = st.back(5)
                    if b.on():
                        wait(sp, x2_done, b.n + 1, e.sp_passed)
                        sp.dma_start(e.X2T[:, bass.ds(b.n * GE, GE)], x2[b.s][:, :]).then_inc(x2_out[b.s], 16)
                run_groups(sp, body, U, 5)
                for i in range(U):
                    wait(sp, x2_out[i], 16 * (NG // U), e.sp_passed)

            @block.vector
            def _(v):
                def body(st):
                    b, f, g = st.back(2), st.back(4), st.back(6)
                    c = Chain(v, nrm.chain, g, 2)
                    if b.on():
                        i = b.s
                        v.wait_ge(turned, b.n + 1)
                        v.wait_ge(gate_in[i], 16 * (b.k + 1))
                        wait(v, agg_done, b.n)
                        v.tensor_tensor(gv[:, :], ps_t[i][:, :], gate[i][:, :], ALU.mult).then_inc(gv_done, 1)
                    if g.on():
                        v.wait_ge(x_ready, g.n + 1)
                        c.put(nrm.total(v, ps_x[g.s][:, :, :]))
                    if b.on():
                        v.wait_ge(gv_done, b.n + 1)
                        v.wait_ge(same_in[i], 16 * (b.k + 1))
                        wait(v, f_ready, b.n - (U - 1))
                        v.tensor_tensor_scan(agg[i][:, :], same[i][:, :], gv[:, :],
                                             0.0 if b.first() else agg[(i - 1) % U][:, GE - 1:GE],
                                             ALU.mult, ALU.add).then_inc(agg_done, 1)
                    if g.on():
                        c.join()
                        nrm.shift(v, ps_x[g.s][:, :, :])
                    if f.on():
                        v.wait_ge(relu_done, f.n + 1)
                        v.wait_ge(x1_in[f.s], 16 * (f.k + 1))
                        wait(v, x2_out[f.s], 16 * f.k)
                        wait(v, x_ready, f.n - (U - 1))
                        v.tensor_tensor(x2[f.s][:, :], ffn[f.s][:, :], x1[f.s][:, :], ALU.add).then_inc(x2_done, 1)
                    if g.on():
                        nrm.sumsq(v, g)
                    if st.on():
                        i = st.s
                        v.wait_ge(gathered[i], 16 * TU * (st.k + 1))
                        wait(v, turned, st.n - (U - 1))
                        v.tensor_tensor(gm[i][:, :, :], gat[i][:, :, :],
                                        e.has[:, bass.ds(st.n * TU, TU)].unsqueeze(2).broadcast_to([P, TU, D]),
                                        ALU.mult).then_inc(gm_done, 1)
                    if g.on():
                        nrm.recip(v, c, g)
                        wait(v, h2_out[g.s], 16 * g.k)
                        nrm.relu_to(v, h2[g.s][:, :, :]).then_inc(h_done, 1)
                        c.end()
                run_groups(v, body, U, 6)

            @block.scalar
            def _(a):
                def body(st):
                    b, g = st.back(3), st.back(6)
                    if g.on():
                        nrm.square(a, g)
                        nrm.root(a, g, e.C["eps"])
                    if b.on():
                        a.wait_ge(f_ready, b.n + 1)
                        wait(a, x2_done, b.n - (U - 1))
                        a.activation(ffn[b.s][:, :], ps_f[:, :], ACT.Relu, bias=e.W["bffn"][0:D, :]).then_inc(relu_done, 1)
                    if g.on():
                        a.wait_ge(h_done, g.n + 1)
                        a.dma_start(edge_rows(e.U2, g.n * GE), h2[g.s][:, :, :]).then_inc(h2_out[g.s], 16)
                run_groups(a, body, U, 6)
                for i in range(U):
                    a.wait_ge(h2_out[i], 16 * (NG // U))

            @block.tensor
            def _(pe):
                def body(st):
                    d, f, x = st.back(1), st.back(3), st.back(5)
                    if d.on():
                        i = d.s
                        wait(pe, gm_done, d.n + 1, e.pe_passed)
                        wait(pe, gv_done, d.n - (U - 1), e.pe_passed)
                        for u in range(TU):
                            m = pe.transpose(ps_t[i][:, u * P:(u + 1) * P], gm[i][:, u, :], e.C["ident"])
                        m.then_inc(turned, 1)
                    if f.on():
                        wait(pe, agg_done, f.n + 1, e.pe_passed)
                        wait(pe, relu_done, f.n, e.pe_passed)
                        pe.matmul(ps_f[:, :], e.W["ffnT"][0:D, :], agg[f.s][:, :], start=True, stop=True).then_inc(f_ready, 1)
                    if x.on():
                        wait(pe, x2_done, x.n + 1, e.pe_passed)
                        wait(pe, nrm.centered, x.n - (U - 1), e.pe_passed)
                        for u in range(TU):
                            m = pe.transpose(ps_x[x.s][:, u, :], x2[x.s][:, u * P:(u + 1) * P], e.C["ident"][0:D, 0:D])
                        m.then_inc(x_ready, 1)
                run_groups(pe, body, U, 5)


def mlp(nc, e):
    with ExitStack() as ctx:
        s = Scope(nc, ctx, "ml")
        idx = [s.sb(f"idx{i}", [P, TU], I32) for i in range(U)]
        gat = [s.sb(f"gat{i}", [P, TU, D]) for i in range(U)]
        own = [s.sb(f"own{i}", [P, TU, D]) for i in range(U)]
        same = [s.sb(f"same{i}", [D, GE]) for i in range(U)]
        x2 = [s.sb(f"x2{i}", [D, GE]) for i in range(U)]
        agg = [s.sb(f"agg{i}", [D, GE]) for i in range(U)]
        hh = [s.sb(f"hh{i}", [D, GE]) for i in range(U)]
        hid = s.sb("hid", [P, GE])
        x3 = [s.sb(f"x3{i}", [D, GE]) for i in range(U)]
        hx = [s.sb(f"hx{i}", [P, TU, 2 * D]) for i in range(U)]
        xh = [s.sb(f"xh{i}", [P, GE]) for i in range(U)]
        ps_t = [s.ps(f"t{i}", [D, GE]) for i in range(U)]
        ps_o, ps_1, ps_2, ps_x, ps_h = (s.ps("o", [D, GE]), s.ps("h1", [P, GE]), s.ps("h2", [D, GE]),
                                        s.ps("x", [P, TU, D]), s.ps("h", [P, GE]))
        last = s.sb("last", [P, CH])
        nrm = s.norm("n", TU)
        gathered, own_in, same_in, x2_in, h_out, xh_out = [s.sems(n) for n in ("g", "own", "sa", "x2", "ho", "xo")]
        idx_c, t_ready, o_ready, agg_done, hh_done, h1_ready, hid_done, h2_ready, x3_done = [
            s.sem(n) for n in ("ic", "tr", "or", "ag", "hh", "h1", "hid", "h2", "x3")]
        x_ready, x_kept, h_done, hx_turned, kept, last_done = [s.sem(n) for n in ("xr", "xk", "hd", "ht", "kp", "ld")]

        with nc.Block() as block:
            @block.gpsimd
            def _(pool):
                def body(st):
                    if st.on():
                        wait(pool, t_ready, st.n - (U - 1), e.pool_passed)
                        start_gathers(e, pool, e.U2, e.idx2, idx, gat, gathered, idx_c, st, st.n, EP + NP)
                run_groups(pool, body, U, 0)

            @block.sync
            def _(sp):
                def body(st):
                    if st.on():
                        i, at = st.s, st.n * GE
                        wait(sp, o_ready, st.n - (U - 1), e.sp_passed)
                        sp.dma_start(own[i][:, :, :], edge_rows(e.U2, at)).then_inc(own_in[i], 16)
                        wait(sp, agg_done, st.n - (U - 1), e.sp_passed)
                        sp.dma_start(same[i][:, :], over_parts(e.same_prev, at, D)).then_inc(same_in[i], 16)
                    b = st.back(2)
                    if b.on():
                        wait(sp, x3_done, b.n - (U - 1), e.sp_passed)
                        sp.dma_start(x2[b.s][:, :], e.X2T[:, bass.ds(b.n * GE, GE)]).then_inc(x2_in[b.s], 16)
                run_groups(sp, body, U, 2)

            @block.vector
            def _(v):
                v.tensor_scalar(last[:, :], e.scat_ptr[:, :], FAR, None, ALU.is_lt).then_inc(last_done, 1)
                v.wait_ge(last_done, 1)

                def body(st):
                    b, f, g = st.back(1), st.back(3), st.back(5)
                    c = Chain(v, nrm.chain, g, 2)
                    if g.on():
                        v.wait_ge(x_ready, g.n + 1)
                        wait(v, hx_turned, g.n - (U - 1))
                        v.tensor_tensor(hx[g.s][:, :, D:2 * D], ps_x[:, :, :],
                                        last[:, bass.ds(g.n * TU, TU)].unsqueeze(2).broadcast_to([P, TU, D]),
                                        ALU.mult).then_inc(x_kept, 1)
                    if b.on():
                        i = b.s
                        v.wait_ge(t_ready, b.n + 1)
                        v.wait_ge(same_in[i], 16 * (b.k + 1))
                        v.tensor_tensor_scan(agg[i][:, :], same[i][:, :], ps_t[i][:, :],
                                             0.0 if b.first() else agg[(i - 1) % U][:, GE - 1:GE],
                                             ALU.mult, ALU.add).then_inc(agg_done, 1)
                    if f.on():
                        v.wait_ge(h2_ready, f.n + 1)
                        v.wait_ge(x2_in[f.s], 16 * (f.k + 1))
                        wait(v, x_ready, f.n - (U - 1))
                        v.scalar_tensor_tensor(out=x3[f.s][:, :], in0=ps_2[:, :], scalar=e.W["b1"][0:D, :], in1=x2[f.s][:, :],
                                               op0=ALU.add, op1=ALU.add).then_inc(x3_done, 1)
                    if g.on():
                        v.wait_ge(x_kept, g.n + 1)
                        c.put(nrm.total(v, hx[g.s][:, :, D:2 * D]))
                    if b.on():
                        v.wait_ge(agg_done, b.n + 1)
                        v.wait_ge(o_ready, b.n + 1)
                        wait(v, h1_ready, b.n - (U - 1))
                        v.tensor_tensor(hh[i][:, :], ps_o[:, :], agg[i][:, :], ALU.add).then_inc(hh_done, 1)
                    if g.on():
                        c.join()
                        nrm.shift(v, hx[g.s][:, :, D:2 * D])
                        nrm.sumsq(v, g)
                        nrm.recip(v, c, g)
                        wait(v, h_out[g.s], 16 * g.k)
                        nrm.relu_to(v, hx[g.s][:, :, 0:D]).then_inc(h_done, 1)
                        c.end()
                run_groups(v, body, U, 5)

            @block.scalar
            def _(a):
                def body(st):
                    d, g, t = st.back(2), st.back(5), st.back(6)
                    if t.on():
                        a.dma_start(edge_rows(e.U3, t.n * GE), hx[t.s][:, :, 0:D]).then_inc(h_out[t.s], 16)
                    if d.on():
                        a.wait_ge(h1_ready, d.n + 1)
                        a.activation(hid[:, :], ps_1[:, :], ACT.Relu, bias=e.W["b0"]).then_inc(hid_done, 1)
                    if t.on():
                        a.wait_ge(hx_turned, t.n + 1)
                        wait(a, xh_out[t.s], 16 * t.k)
                        a.copy(xh[t.s][:, :], ps_h[:, :]).then_inc(kept, 1)
                    if g.on():
                        nrm.square(a, g)
                    if t.on():
                        a.wait_ge(kept, t.n + 1)
                        a.dma_start(e.XH3[:, bass.ds(t.n * GE, GE)], xh[t.s][:, :]).then_inc(xh_out[t.s], 16)
                    if g.on():
                        nrm.root(a, g, e.C["eps"])
                    if g.on():
                        a.wait_ge(h_done, g.n + 1)
                run_groups(a, body, U, 6)
                for sems in (h_out, xh_out):
                    for i in range(U):
                        a.wait_ge(sems[i], 16 * (NG // U))

            @block.tensor
            def _(pe):
                def body(st):
                    d, x, t = st.back(2), st.back(4), st.back(6)
                    if d.on():
                        wait(pe, hh_done, d.n + 1, e.pe_passed)
                        wait(pe, hid_done, d.n, e.pe_passed)
                        pe.matmul(ps_1[:, :], e.W["w0"][0:D, :], hh[d.s][:, :], start=True, stop=True).then_inc(h1_ready, 1)
                    if t.on():
                        wait(pe, h_done, t.n + 1, e.pe_passed)
                        wait(pe, kept, t.n, e.pe_passed)
                        for u in range(TU):
                            m = pe.transpose(ps_h[:, u * P:(u + 1) * P], hx[t.s][:, u, :], e.C["ident"])
                        m.then_inc(hx_turned, 1)
                    if st.on():
                        i = st.s
                        wait(pe, gathered[i], 16 * TU * (st.k + 1), e.pe_passed)
                        wait(pe, agg_done, st.n - (U - 1), e.pe_passed)
                        for u in range(TU):
                            m = pe.transpose(ps_t[i][:, u * P:(u + 1) * P], gat[i][:, u, :], e.C["ident"])
                        m.then_inc(t_ready, 1)
                    if d.on():
                        wait(pe, hid_done, d.n + 1, e.pe_passed)
                        wait(pe, x3_done, d.n, e.pe_passed)
                        pe.matmul(ps_2[:, :], e.W["w1"], hid[:, :], start=True, stop=True).then_inc(h2_ready, 1)
                    if x.on():
                        wait(pe, x3_done, x.n + 1, e.pe_passed)
                        wait(pe, x_kept, x.n, e.pe_passed)
                        for u in range(TU):
                            m = pe.transpose(ps_x[:, u, :], x3[x.s][:, u * P:(u + 1) * P], e.C["ident"][0:D, 0:D])
                        m.then_inc(x_ready, 1)
                    if st.on():
                        wait(pe, own_in[i], 16 * (st.k + 1), e.pe_passed)
                        wait(pe, hh_done, st.n, e.pe_passed)
                        for u in range(TU):
                            m = pe.transpose(ps_o[:, u * P:(u + 1) * P], own[i][:, u, :], e.C["ident"])
                        m.then_inc(o_ready, 1)
                run_groups(pe, body, U, 6)


def heads(nc, e):
    with ExitStack() as ctx:
        s = Scope(nc, ctx, "hd")
        idx = [s.sb(f"idx{i}", [P, TU], I32) for i in range(U)]
        oidx = [s.sb(f"oidx{i}", [P, TU], I32) for i in range(U)]
        gat = [s.sb(f"gat{i}", [P, TU, D]) for i in range(U)]
        xl = [s.sb(f"xl{i}", [P, GE]) for i in range(U)]
        same = [s.sb(f"same{i}", [P, GE]) for i in range(U)]
        xb = [s.sb(f"xb{i}", [P, GE]) for i in range(U)]
        ht = s.sb("ht", [D, GE])
        qt = [s.sb(f"qt{i}", [D, GE]) for i in range(U)]
        vt = [s.sb(f"vt{i}", [D, GE]) for i in range(U)]
        prod = s.sb("prod", [D, GE])
        clip = s.sb("clip", [P, GE])
        wz = [s.sb(f"wz{i}", [P, GE]) for i in range(U)]
        wv = [s.sb(f"wv{i}", [P, GE]) for i in range(U)]
        lnz = s.sb("lnz", [P, GE])
        rz = s.sb("rz", [P, GE])
        tz = s.sb("tz", [P, GE])
        rn = s.sb("rn", [D, GE])
        wn = [s.sb(f"wn{i}", [P, GE]) for i in range(U)]
        f1 = s.sb("f1", [P, TU, D])
        x4 = [s.sb(f"x4{i}", [P, TU, D]) for i in range(U)]
        ps_t, ps_q, ps_k, ps_v, ps_s = s.ps("t", [D, GE]), s.ps("q", [D, GE]), s.ps("k", [D, GE]), s.ps("v", [D, GE]), s.ps("s", [P, GE])
        ps_h = [s.ps(f"h{i}", [P, TU, 2 * D]) for i in range(U)]
        nrm = s.norm("n", TU)
        gathered, xl_in, same_in, x4_out = [s.sems(n) for n in ("g", "xl", "sa", "xo")]
        (idx_c, oidx_c, turned, ht_kept, xb_done, k_ready, q_ready, v_ready, q_kept, v_kept, prod_done, s_ready, clip_done,
         w_done, wz_done, wv_done, lnz_done, rz_done, tz_done, rn_done, wn_done, h_ready, x4_done, lnc, ones_in) = [
            s.sem(n) for n in ("ic", "oc", "tu", "htk", "xb", "kr", "qr", "vr", "qk", "vk", "pd", "sr", "cl", "wd",
                               "wzd", "wvd", "lz", "rz", "tz", "rn", "wn", "hr", "x4", "ln", "on")]
        pos = lambda st: st.n * -1 + (NG - 1)

        with nc.Block() as block:
            @block.gpsimd
            def _(pool):
                def body(st):
                    if st.on():
                        wait(pool, turned, st.n - (U - 1), e.pool_passed)
                        start_gathers(e, pool, e.U3, e.idx2, idx, gat, gathered, idx_c, st, pos(st), EP + NP)
                    b = st.back(5)
                    if b.on():
                        i = b.s
                        wait(pool, x4_out[i], 16 * TU * b.k, e.pool_passed)
                        pool.tensor_copy(oidx[i][:, :], e.scat_out[:, bass.ds(pos(b) * TU, TU)]).then_inc(oidx_c, 1)
                        wait(pool, oidx_c, b.n + 1, e.pool_passed)
                        wait(pool, x4_done, b.n + 1, e.pool_passed)
                        for u in range(TU):
                            pool.indirect_dma_start(e.out, bass.IndirectOffsetOnAxis(ap=oidx[i][:, u:u + 1], axis=0),
                                                    x4[i][:, u, :], None, bounds_check=NP - 1,
                                                    oob_is_err=False).then_inc(x4_out[i], 16)
                run_groups(pool, body, U, 5)
                for i in range(U):
                    wait(pool, x4_out[i], 16 * TU * (NG // U), e.pool_passed)

            @block.sync
            def _(sp):
                def body(st):
                    if st.on():
                        i, at = st.s, pos(st) * GE
                        wait(sp, xb_done, st.n - (U - 1), e.sp_passed)
                        sp.dma_start(xl[i][:, :], e.XH3[:, bass.ds(at, GE)]).then_inc(xl_in[i], 16)
                        wait(sp, wv_done, st.n - (U - 1), e.sp_passed)
                        sp.dma_start(same[i][:, :], over_parts(e.same_next, at, P)).then_inc(same_in[i], 16)
                run_groups(sp, body, U, 0)

            @block.vector
            def _(v):
                for i in range(U):
                    v.memset(wn[i][D:P, :], 1.0).then_inc(ones_in, 1)

                def body(st):
                    b, c, g = st.back(1), st.back(2), st.back(4)
                    ch = Chain(v, nrm.chain, g, 3)
                    if c.on():
                        i = c.s
                        v.wait_ge(w_done, c.n + 1)
                        v.wait_ge(v_kept, c.n + 1)
                        v.tensor_tensor(wz[i][0:D, :], vt[i][:, :], wz[i][0:D, :], ALU.mult).then_inc(wz_done, 1)
                    if b.on():
                        v.wait_ge(k_ready, b.n + 1)
                        v.wait_ge(q_kept, b.n + 1)
                        wait(v, s_ready, b.n)
                        v.scalar_tensor_tensor(out=prod[:, :], in0=ps_k[:, :], scalar=e.W["bk"][0:D, :], in1=qt[b.s][:, :],
                                               op0=ALU.add, op1=ALU.mult).then_inc(prod_done, 1)
                    if c.on():
                        v.wait_ge(wz_done, c.n + 1)
                        wait(v, wn_done, c.n - (U - 1))
                        v.tensor_tensor_scan(wv[i][:, ::-1], same[i][:, ::-1], wz[i][:, ::-1],
                                             0.0 if c.first() else wv[(i - 1) % U][:, 0:1],
                                             ALU.mult, ALU.add).then_inc(wv_done, 1)
                    if st.on():
                        j = st.s
                        v.wait_ge(xl_in[j], 16 * (st.k + 1))
                        v.wait_ge(same_in[j], 16 * (st.k + 1))
                        wait(v, h_ready, st.n - (U - 1))
                        wait(v, xb_done, st.n)
                        v.tensor_tensor_scan(xb[j][:, ::-1], same[j][:, ::-1], xl[j][:, ::-1],
                                             0.0 if st.first() else xb[(j - 1) % U][:, 0:1],
                                             ALU.mult, ALU.add).then_inc(xb_done, 1)
                    if g.on():
                        nrm.sumsq(v, g)
                    if b.on():
                        v.wait_ge(s_ready, b.n + 1)
                        wait(v, w_done, b.n)
                        v.tensor_scalar(clip[:, :], ps_s[:, :], 5.0, -5.0, ALU.min, ALU.max).then_inc(clip_done, 1)
                    if g.on():
                        nrm.recip(v, ch, g)
                        ch.put(v.tensor_tensor(f1[:, :, :], ps_h[g.s][:, :, 0:D], nrm.over(nrm.rstd), ALU.mult))
                    if c.on():
                        v.wait_ge(rz_done, c.n + 1)
                        wait(v, rn_done, c.n)
                        v.scalar_tensor_tensor(out=tz[D:P, :], in0=wv[i][D:P, :], scalar=1.0, in1=rz[D:P, :],
                                               op0=ALU.add, op1=ALU.mult).then_inc(tz_done, 1)
                    if g.on():
                        ch.join()
                        ch.put(v.tensor_tensor(f1[:, :, :], f1[:, :, :],
                                               e.W["gamma"].unsqueeze(1).broadcast_to([P, TU, D]), ALU.mult))
                    if c.on():
                        v.wait_ge(tz_done, c.n + 1)
                        v.scalar_tensor_tensor(out=rn[:, :], in0=tz[D:P, :], scalar=-2.0, in1=rz[D:P, :],
                                               op0=ALU.add, op1=ALU.mult).then_inc(rn_done, 1)
                    if g.on():
                        ch.join()
                        wait(v, x4_out[g.s], 16 * TU * g.k)
                        v.tensor_tensor(x4[g.s][:, :, :], f1[:, :, :], ps_h[g.s][:, :, D:2 * D], ALU.add).then_inc(x4_done, 1)
                        ch.end()
                    if c.on():
                        v.wait_ge(rn_done, c.n + 1)
                        wait(v, h_ready, c.n - (U - 1))
                        v.scalar_tensor_tensor(out=wn[i][0:D, :], in0=wv[i][0:D, :], scalar=-1.0, in1=rn[:, :],
                                               op0=ALU.mult, op1=ALU.mult).then_inc(wn_done, 1)
                run_groups(v, body, U, 4)

            @block.scalar
            def _(a):
                a.preload_act_table_set("natural_log_exp_and_others")

                def body(st):
                    b, c, g = st.back(1), st.back(2), st.back(4)
                    if g.on():
                        a.wait_ge(h_ready, g.n + 1)
                        wait(a, nrm.summed, g.n)
                        a.activation(nrm.sq[:, :, :], ps_h[g.s][:, :, 0:D], ACT.Square).then_inc(nrm.squared, 1)
                    if st.on():
                        a.wait_ge(turned, st.n + 1)
                        wait(a, v_ready, st.n)
                        a.copy(ht[:, :], ps_t[:, :]).then_inc(ht_kept, 1)
                    if c.on():
                        a.wait_ge(wv_done, c.n + 1)
                        a.activation(lnz[D:P, :], wv[c.s][D:P, :], ACT.Ln, bias=e.C["ones"][D:P, 0:1]).then_inc(lnz_done, 1)
                    if g.on():
                        a.wait_ge(nrm.summed, g.n + 1)
                        a.activation(nrm.std[:, :], nrm.ss[:, :], ACT.Ln, bias=e.C["eps"], scale=1.0 / D).then_inc(lnc, 1)
                    if c.on():
                        a.wait_ge(lnz_done, c.n + 1)
                        wait(a, rn_done, c.n)
                        a.activation(rz[D:P, :], lnz[D:P, :], ACT.Exp, scale=-1.0).then_inc(rz_done, 1)
                    if g.on():
                        a.wait_ge(lnc, g.n + 1)
                        a.activation(nrm.std[:, :], nrm.std[:, :], ACT.Exp, scale=0.5).then_inc(nrm.rooted, 1)
                    if st.on():
                        a.wait_ge(q_ready, st.n + 1)
                        wait(a, prod_done, st.n - (U - 1))
                        a.activation(qt[st.s][:, :], ps_q[:, :], ACT.Identity, bias=e.bq8[0:D, :], scale=1.0 / 8.0).then_inc(q_kept, 1)
                    if b.on():
                        a.wait_ge(clip_done, b.n + 1)
                        wait(a, wv_done, b.n - (U - 1))
                        a.activation(wz[b.s][:, :], clip[:, :], ACT.Exp).then_inc(w_done, 1)
                    if st.on():
                        a.wait_ge(v_ready, st.n + 1)
                        wait(a, wz_done, st.n - (U - 1))
                        a.activation(vt[st.s][:, :], ps_v[:, :], ACT.Identity, bias=e.W["bv"][0:D, :]).then_inc(v_kept, 1)
                run_groups(a, body, U, 4)

            @block.tensor
            def _(pe):
                wait(pe, ones_in, U)

                def body(st):
                    b, f = st.back(1), st.back(3)
                    if f.on():
                        i = f.s
                        wait(pe, wn_done, f.n + 1, e.pe_passed)
                        wait(pe, x4_done, f.n - (U - 1), e.pe_passed)
                        for u in range(TU):
                            pe.matmul(ps_h[i][:, u, :], xb[i][:, u * P:(u + 1) * P], e.W["wfx"], start=(u == 0),
                                      stop=False, skip_group_check=True)
                            m = pe.matmul(ps_h[i][:, u, :], wn[i][:, u * P:(u + 1) * P], e.W["wob"], start=False,
                                          stop=(u == TU - 1), skip_group_check=True)
                        m.then_inc(h_ready, 1)
                    if st.on():
                        i = st.s
                        wait(pe, gathered[i], 16 * TU * (st.k + 1), e.pe_passed)
                        wait(pe, ht_kept, st.n, e.pe_passed)
                        for u in range(TU):
                            m = pe.transpose(ps_t[:, u * P:(u + 1) * P], gat[i][:, u, :], e.C["ident"])
                        m.then_inc(turned, 1)
                    if b.on():
                        wait(pe, prod_done, b.n + 1, e.pe_passed)
                        wait(pe, clip_done, b.n, e.pe_passed)
                        pe.matmul(ps_s[:, :], e.C["heads"][0:D, :], prod[:, :], start=True, stop=True).then_inc(s_ready, 1)
                    if st.on():
                        wait(pe, xb_done, st.n + 1, e.pe_passed)
                        wait(pe, q_kept, st.n, e.pe_passed)
                        pe.matmul(ps_q[:, :], e.W["wq"][0:D, :], xb[i][0:D, :], start=True, stop=True).then_inc(q_ready, 1)
                        wait(pe, ht_kept, st.n + 1, e.pe_passed)
                        wait(pe, prod_done, st.n, e.pe_passed)
                        pe.matmul(ps_k[:, :], e.W["wk"][0:D, :], ht[:, :], start=True, stop=True).then_inc(k_ready, 1)
                        wait(pe, v_kept, st.n, e.pe_passed)
                        pe.matmul(ps_v[:, :], e.W["wv"][0:D, :], ht[:, :], start=True, stop=True).then_inc(v_ready, 1)
                run_groups(pe, body, U, 3)


def constants():
    c = np.zeros((P, CONST_W), np.float32)
    put = lambda name, a: c.__setitem__((slice(0, a.shape[0]), slice(*CONST_AT[name])), a)
    put("ident", np.eye(P, dtype=np.float32))
    put("ones", np.ones((P, P), np.float32))
    f, m = np.arange(D)[:, None], np.arange(P)[None, :]
    put("heads", (f // 16 == (m % D) // 16).astype(np.float32))
    put("types", np.tile(np.arange(4, dtype=np.float32), (P, 1)))
    put("rels", (2 * np.arange(4)[None, :] + (np.arange(P)[:, None] >= D)).astype(np.float32))
    put("less_rels", -(2 * np.arange(4)[None, :] + (np.arange(P)[:, None] >= D)).astype(np.float32))
    put("eps", np.full((P, 1), EPS, np.float32))
    return c


def pack_weights(i):
    w = np.zeros((P, WEIGHT_W), np.float32)

    def put(name, a, row=0, col=0):
        a = np.asarray(a)
        at = WEIGHT_AT[name][0] + col
        w[row:row + a.shape[0], at:at + a.shape[1]] = a

    def pairs(name, a, col, width):
        for c in range(a.shape[0] // 2):
            put(name, a[2 * c:2 * c + 2].reshape(P, D), 0, c * width + col)

    q, k, v = (np.asarray(i[f"L0_gnn_{n}_lin"]) for n in "qkv")
    for half in range(2):
        pairs("q", q, half * D, P)
    pairs("kv", k, 0, P)
    pairs("kv", v, D, P)
    pairs("att", np.asarray(i["L0_gnn_rel_att"]), 0, D)
    pairs("msg", np.asarray(i["L0_gnn_rel_msg"]), 0, D)
    pri = np.asarray(i["L0_gnn_rel_pri"]).reshape(4, 2)
    put("pri", np.repeat(pri.T, D, axis=0))
    put("a", np.asarray(i["L0_gnn_a_lin"]).transpose(1, 0, 2).reshape(D, 4 * D))
    put("skip", np.tile(np.repeat(np.asarray(i["L0_gnn_skip"]), D)[None], (D, 1)))
    put("proj", i["L1_gnn_proj_cosim"])
    put("ffnT", np.asarray(i["L1_gnn_W_ffn"]).T)
    put("bffn", np.asarray(i["L1_gnn_b_ffn"])[:, None])
    put("bffn_row", np.tile(np.asarray(i["L1_gnn_b_ffn"])[None], (P, 1)))
    for half in range(2):
        put("w0", i["L2_gnn_W0"], half * D)
        put("wf2", i["L3_gnn_Wf"], half * D, half * D)
    put("b0", np.asarray(i["L2_gnn_b0"])[:, None])
    put("w1", i["L2_gnn_W1"])
    put("b1", np.asarray(i["L2_gnn_b1"])[:, None])
    put("b1_row", np.tile(np.asarray(i["L2_gnn_b1"])[None], (P, 1)))
    for n in "qkv":
        put("w" + n, i[f"L3_gnn_W{n}"])
        put("b" + n, np.asarray(i[f"L3_gnn_b{n}"])[:, None])
    put("wo", i["L3_gnn_Wo"])
    put("bo_row", np.tile(np.asarray(i["L3_gnn_bo"])[None], (P, 1)))
    put("bf_row", np.tile(np.asarray(i["L3_gnn_bf"])[None], (P, 1)))
    for half in range(2):
        put("wfx", i["L3_gnn_Wf"], 0, half * D)
        put("wob", i["L3_gnn_Wo"], 0, half * D)
        put("wob", np.asarray(i["L3_gnn_bo"])[None], D, half * D)
        put("bf_64", np.asarray(i["L3_gnn_bf"])[None], D, half * D)
    put("wfx", np.eye(D, dtype=np.float32), D, D)
    put("beta_64", np.asarray(i["L3_gnn_beta"])[None], D)
    put("gamma", np.tile(np.asarray(i["L3_gnn_gamma"])[None], (P, 1)))
    put("beta", np.tile(np.asarray(i["L3_gnn_beta"])[None], (P, 1)))
    return w


def lay_out(i):
    def padded(a, n, fill):
        a = np.asarray(a)
        p = np.full((n,) + a.shape[1:], fill, a.dtype)
        p[:a.shape[0]] = a
        return p

    src, dst = padded(i["src"], EP, PADN), padded(i["dst"], EP, PADN)
    etype = padded(i["edge_type_8"], EP, 0)
    major = lambda a: np.ascontiguousarray(a.reshape(NG, TU, P).transpose(2, 0, 1))
    ntype = padded(i["node_type_4"], NP, 0).reshape(NG, P, RN).transpose(1, 0, 2).reshape(P, NG * RN)
    return {
        "x": padded(i["x"], NP, 0.0), "node_type": np.ascontiguousarray(ntype),
        "src_idx": major(src), "dst_idx": major(dst), "etype_row": etype,
        "dst_row": np.concatenate([np.full(1, -1, dst.dtype), dst, np.full(1, -1, dst.dtype)]),
        "chunk_id": np.arange(1, EP + 1, dtype=np.float32).reshape(P, CH),
        "consts": constants(), "weights": pack_weights(i),
    }


def kernel(**inputs):
    import concourse.bacc as bacc
    from concourse.bass_utils import run_bass_kernel_spmd

    arrays = lay_out(inputs)
    nc = bacc.Bacc("TRN2", target_bir_lowering=False, num_devices=1)
    aps = {n: nc.dram_tensor("in_" + n, a.shape, mybir.dt.from_np(a.dtype), kind="ExternalInput").ap()
           for n, a in arrays.items()}
    out = nc.dram_tensor("out_x", (NP, D), F32, kind="ExternalOutput").ap()
    build(nc, out=out, **aps)
    r = run_bass_kernel_spmd(nc, [{"in_" + n: a for n, a in arrays.items()}], core_ids=[0])
    return r.results[0]["out_x"][:NODES]
```

```python
from contextlib import ExitStack

import numpy as np
import concourse.bass as bass
from concourse import mybir

P = 128
D = 64
NODES = 100000
EDGES = 50000
GE = 512
TU = GE // P
U = 3
NG = -(-EDGES // (GE * U)) * U
EP = NG * GE
CH = EP // P
GN = 1024
RN = GN // P
NP = NG * GN
PADN = NODES
TW = 68
FAR = 8388608.0
BIG = 1.7e38
EPS = 1e-5
LAST = 2

F32 = mybir.dt.float32
I32 = mybir.dt.int32
ALU = mybir.AluOpType
ACT = mybir.ActivationFunctionType
AX = mybir.AxisListType.X

CONST_COLS = [("ident", 128), ("ones", 128), ("heads", 128), ("types", 4), ("rels", 4), ("less_rels", 4), ("eps", 1)]
WEIGHT_COLS = [
    ("q", 256), ("kv", 256), ("att", 256), ("msg", 256), ("pri", 4), ("a", 256), ("skip", 256),
    ("proj", 64), ("ffnT", 64), ("bffn", 1), ("bffn_row", 64),
    ("w0", 128), ("b0", 1), ("w1", 64), ("b1", 1), ("b1_row", 64),
    ("wq", 64), ("bq", 1), ("wk", 64), ("bk", 1), ("wv", 64), ("bv", 1),
    ("wo", 64), ("bo_row", 64), ("wf2", 256), ("bf_row", 64), ("gamma", 64), ("beta", 64),
    ("wfx", 128), ("wob", 128), ("bf_64", 128), ("beta_64", 64),
]


def spans(cols):
    at, out = 0, {}
    for name, n in cols:
        out[name] = (at, at + n)
        at += n
    return out, at


CONST_AT, CONST_W = spans(CONST_COLS)
WEIGHT_AT, WEIGHT_W = spans(WEIGHT_COLS)


class Step:

    def __init__(self, n, k, s, u):
        self.n, self.k, self.s, self.u = n, k, s, u

    def back(self, lag):
        return Step(self.n - lag, self.k + (self.s - lag) // self.u, (self.s - lag) % self.u, self.u)

    def on(self):
        return not isinstance(self.n, int) or 0 <= self.n < NG

    def first(self):
        return isinstance(self.n, int) and self.n == 0


def run_groups(eng, body, u=U, tail=LAST, peel=3):
    for n in range(peel * u):
        body(Step(n, n // u, n % u, u))
    with eng.Fori(peel, NG // u) as i:
        for s in range(u):
            body(Step(i * u + s, i, s, u))
    for n in range(NG, NG + tail):
        body(Step(n, n // u, n % u, u))


def wait(eng, sem, value, passed=None):
    if isinstance(value, int) and value <= 0:
        return
    eng.wait_ge(sem, value)
    if passed is not None and not isinstance(value, int):
        eng.sem_inc(passed, 1)


class Chain:

    def __init__(self, eng, sem, step, per):
        self.eng, self.sem, self.base, self.per, self.i = eng, sem, step.n * per, per, 0

    def link(self, ins):
        self.i += 1
        assert self.i <= self.per
        ins.then_inc(self.sem, 1)
        self.eng.wait_ge(self.sem, self.base + self.i)

    def put(self, ins):
        self.i += 1
        assert self.i <= self.per
        ins.then_inc(self.sem, 1)

    def join(self):
        self.eng.wait_ge(self.sem, self.base + self.i)

    def end(self):
        assert self.i == self.per, (self.i, self.per)


class Norm:

    def __init__(self, sb, sem, name, rows):
        self.rows = rows
        self.sum = sb(f"{name}_sum", [P, rows], F32)
        self.cent = sb(f"{name}_cent", [P, rows, D], F32)
        self.sq = sb(f"{name}_sq", [P, rows, D], F32)
        self.ss = sb(f"{name}_ss", [P, rows], F32)
        self.std = sb(f"{name}_std", [P, rows], F32)
        self.rstd = sb(f"{name}_rstd", [P, rows], F32)
        self.centered = sem(f"{name}_centered")
        self.squared = sem(f"{name}_squared")
        self.summed = sem(f"{name}_summed")
        self.rooted = sem(f"{name}_rooted")
        self.chain = sem(f"{name}_chain")

    def over(self, small):
        return small[:, :].unsqueeze(2).broadcast_to([P, self.rows, D])

    def total(self, v, x):
        return v.tensor_reduce(self.sum[:, :], x, AX, ALU.add)

    def shift(self, v, x):
        v.scalar_tensor_tensor(out=self.cent[:, :, :], in0=self.over(self.sum), scalar=-1.0 / D, in1=x,
                               op0=ALU.mult, op1=ALU.add).then_inc(self.centered, 1)

    def center(self, v, c, x):
        c.link(self.total(v, x))
        self.shift(v, x)

    def square(self, a, st):
        a.wait_ge(self.centered, st.n + 1)
        wait(a, self.summed, st.n)
        a.activation(self.sq[:, :, :], self.cent[:, :, :], ACT.Square).then_inc(self.squared, 1)

    def sum_squares(self, a, st):
        a.wait_ge(self.centered, st.n + 1)
        wait(a, self.rooted, st.n)
        for j in range(self.rows):
            m = a.activation(self.sq[:, j, :], self.cent[:, j, :], ACT.Square, accum_out=self.ss[:, j:j + 1])
        m.then_inc(self.summed, 1)

    def sumsq(self, v, st):
        v.wait_ge(self.squared, st.n + 1)
        v.tensor_reduce(self.ss[:, :], self.sq[:, :, :], AX, ALU.add).then_inc(self.summed, 1)

    def root(self, a, st, eps):
        a.wait_ge(self.summed, st.n + 1)
        a.activation(self.std[:, :], self.ss[:, :], ACT.Sqrt, bias=eps, scale=1.0 / D).then_inc(self.rooted, 1)

    def recip(self, v, c, st):
        v.wait_ge(self.rooted, st.n + 1)
        c.link(v.reciprocal(self.rstd[:, :], self.std[:, :]))

    def relu_to(self, v, out):
        return v.scalar_tensor_tensor(out=out, in0=self.cent[:, :, :], scalar=0.0, in1=self.over(self.rstd),
                                      op0=ALU.max, op1=ALU.mult)


class Scope:

    def __init__(self, nc, ctx, tag):
        self.nc, self.ctx, self.tag, self.used = nc, ctx, tag, []
        ctx.callback(self.clear)

    def clear(self):
        if self.used:
            self.nc.clear_and_free_semaphores(self.used)
            self.nc.all_engine_barrier()

    def sb(self, name, shape, dt=F32):
        return self.ctx.enter_context(self.nc.sbuf_tensor(f"{self.tag}_{name}", shape, dt))

    def ps(self, name, shape, dt=F32):
        return self.ctx.enter_context(self.nc.psum_tensor(f"{self.tag}_ps_{name}", shape, dt))

    def sem(self, name):
        self.used.append(self.nc.alloc_semaphore(f"{self.tag}_s_{name}"))
        return self.used[-1]

    def sems(self, name, n=U):
        return [self.sem(f"{name}{i}") for i in range(n)]

    def norm(self, name, rows):
        return Norm(self.sb, self.sem, f"{self.tag}_{name}", rows)


def edge_rows(table, at, width=D):
    return table[bass.ds(at, GE), :].rearrange("(u p) f -> p u f", p=P)


def node_rows(table, at):
    return table[bass.ds(at, GN), :].rearrange("(p j) f -> p j f", j=RN)


def over_parts(row, at, parts):
    return row[bass.ds(at, GE)].partition_broadcast(parts)


class Env:
    pass


def build(nc, x, node_type, src_idx, dst_idx, etype_row, dst_row, chunk_id, edge_id, consts, weights, out):
    e = Env()
    e.x, e.out = x, out
    e.etype_row = etype_row

    def dram(name, shape, dt=F32):
        return nc.dram_tensor(name, shape, dt).ap()

    e.T0 = dram("t0", [NP, TW])
    e.XD = dram("xd", [EP, TW])
    e.VT = dram("vt", [D, EP])
    e.U1 = dram("u1", [2 * EP, D])
    e.SD = dram("sd", [EP, D])
    e.U2 = dram("u2", [EP + NP, D])
    e.U3 = dram("u3", [EP + NP, D])
    e.XH1 = dram("xh1", [P, EP])
    e.X2T = dram("x2t", [D, EP])
    e.XH3 = dram("xh3", [P, EP])
    e.same_prev = dram("same_prev", [EP])
    e.same_next = dram("same_next", [EP])
    e.logit = dram("logit", [EP])
    e.alpha = dram("alpha", [EP])
    e.first_edge = dram("first_edge", [EP])

    with ExitStack() as ctx:
        keep = Scope(nc, ctx, "keep")
        e.pe_passed, e.sp_passed, e.pool_passed = [keep.sem(f"{n}_passed") for n in ("pe", "sp", "pool")]
        e.cst = keep.sb("consts", [P, CONST_W])
        e.wts = keep.sb("weights", [P, WEIGHT_W])
        e.C = {n: e.cst[:, a:b] for n, (a, b) in CONST_AT.items()}
        e.W = {n: e.wts[:, a:b] for n, (a, b) in WEIGHT_AT.items()}
        e.relu_b = keep.sb("relu_b", [P, D])
        e.bq8 = keep.sb("bq8", [P, 1])
        e.bfo = keep.sb("bfo", [P, D])
        e.bfo_cent = keep.sb("bfo_cent", [P, D])
        e.bfo_beta = keep.sb("bfo_beta", [P, D])
        e.gather0 = keep.sb("gather0", [P, NG, 2 * TU], I32)
        e.scat_ptr = keep.sb("scat_ptr", [P, CH], I32)
        e.scat_out = keep.sb("scat_out", [P, CH], I32)
        e.ptr_pay = keep.sb("ptr_pay", [P, CH, 2])
        e.ptrs = keep.sb("ptrs", [P, CH, 2])
        e.has = keep.sb("has", [P, CH])
        e.gate = keep.sb("gate", [P, CH])
        e.idx1 = keep.sb("idx1", [P, CH], I32)
        e.idxsd = keep.sb("idxsd", [P, CH], I32)
        e.idx2 = keep.sb("idx2", [P, CH], I32)
        e.segc = keep.sb("segc", [P, CH])
        e.segn = keep.sb("segn", [P, CH])
        tables(nc, e, dst_row, chunk_id, edge_id, src_idx, dst_idx, node_type, consts, weights)
        dense(nc, e)
        scores(nc, e)
        softmax(nc, e)
        attend(nc, e)
        difference(nc, e)
        propagate(nc, e)
        mlp(nc, e)
        heads(nc, e)


def tables(nc, e, dst_row, chunk_id, edge_id, src_idx, dst_idx, node_type, consts, weights):
    UT = 9
    NB = -(-CH // P)
    with ExitStack() as ctx:
        s = Scope(nc, ctx, "tab")
        dst = s.sb("dst", [P, CH], I32)
        prv = s.sb("prev", [P, CH], I32)
        nxt = s.sb("next", [P, CH], I32)
        eid = s.sb("eid", [P, CH])
        eid_major = s.sb("eid_major", [P, CH])
        tmp = s.sb("tmp", [P, CH])
        start = s.sb("start", [P, CH])
        rows = s.sb("rows", [P, P + 1])
        ends = s.sb("ends", [P, P])
        carry = s.sb("carry", [P, 1])
        sig = s.sb("sig", [P, 256])
        row_sum = s.sb("row_sum", [P, 1])
        blocks = s.sb("blocks", [P, 3, NB, P])
        dstf = s.sb("dstf", [P, NG, TU])
        types = s.sb("types", [P, NG * RN], I32)
        row = [s.sb(f"row{i}", [P, RN, TW]) for i in range(UT)]
        xin = [s.sb(f"x{i}", [P, RN, D]) for i in range(UT)]
        pt = s.ps("pt", [P, P])
        pc = s.ps("pc", [P, 1])
        ps_major = [s.ps(f"major{i}", [P, CH]) for i in range(3)]
        loaded, chain, turned, carried, stored, back = [s.sem(n) for n in
                                                        ("loaded", "chain", "turned", "carried", "stored", "back")]
        sig_e, weights_in, row_done, meta_done = s.sem("sig_e"), s.sem("weights_in"), s.sem("row_done"), s.sem("meta_done")
        local_done, idx_in, majored = s.sem("local_done"), s.sem("idx_in"), s.sem("majored")
        x_in, copied, typed, row_out = s.sems("x_in", UT), s.sem("copied"), s.sem("typed"), s.sems("row_out", UT)
        types_in, cleared = s.sem("types_in"), s.sem("cleared")

        with nc.Block() as block:
            @block.gpsimd
            def _(pool):
                pool.dma_start(e.gather0[:, :, 0:TU], src_idx).then_inc(idx_in, 16)
                pool.dma_start(e.gather0[:, :, TU:2 * TU], dst_idx).then_inc(idx_in, 16)
                pool.dma_start(eid_major[:, :], edge_id).then_inc(idx_in, 16)
                wait(pool, meta_done, 1, e.pool_passed)
                rows_of = lambda t: t.rearrange("(p j) -> p j", j=CH)
                pool.dma_start(rows_of(e.same_prev), e.segc[:, :]).then_inc(stored, 16)
                pool.dma_start(rows_of(e.same_next), e.segn[:, :]).then_inc(stored, 16)
                pool.dma_start(rows_of(e.first_edge), start[:, :]).then_inc(stored, 16)
                wait(pool, stored, 48, e.pool_passed)
                for a, t in enumerate((e.same_prev, e.same_next, e.first_edge)):
                    for b in range(NB):
                        n = min(P, CH - b * P)
                        pool.dma_start(blocks[0:n, a, b, :], t[b * P * P:(b * P + n) * P].rearrange("(r p) -> r p", p=P)).then_inc(back, 16)

            @block.sync
            def _(sp):
                chunks = lambda off: dst_row[off:off + EP].rearrange("(p j) -> p j", j=CH)
                sp.dma_start(e.wts[:, :], weights).then_inc(weights_in, 16)
                sp.dma_start(dst[:, :], chunks(1)).then_inc(loaded, 16)
                sp.dma_start(prv[:, :], chunks(0)).then_inc(loaded, 16)
                sp.dma_start(nxt[:, :], chunks(2)).then_inc(loaded, 16)
                sp.dma_start(eid[:, :], chunk_id).then_inc(loaded, 16)
                sp.dma_start(e.cst[:, :], consts).then_inc(loaded, 16)
                sp.dma_start(types[:, :], node_type).then_inc(types_in, 16)

                def body(st):
                    if st.on():
                        wait(sp, copied, st.n - (UT - 1), e.sp_passed)
                        sp.dma_start(xin[st.s][:, :, :], node_rows(e.x, st.n * GN)).then_inc(x_in[st.s], 16)
                run_groups(sp, body, UT, 0, 2)

            @block.scalar
            def _(act):
                act.wait_ge(weights_in, 16)
                act.activation(sig[0:D, :], e.W["skip"][0:D, :], ACT.Sigmoid).then_inc(sig_e, 1)

                def body(st):
                    if st.on():
                        act.wait_ge(copied, st.n + 1)
                        act.wait_ge(typed, st.n + 1)
                        act.dma_start(node_rows(e.T0, st.n * GN), row[st.s][:, :, :]).then_inc(row_out[st.s], 16)
                run_groups(act, body, UT, 0, 2)
                for i in range(UT):
                    act.wait_ge(row_out[i], 16 * (NG // UT))

            @block.vector
            def _(v):
                for i in range(UT):
                    v.memset(row[i][:, :, :], 0.0).then_inc(cleared, 1)
                n = [0]

                def link(ins):
                    n[0] += 1
                    ins.then_inc(chain, 1)
                    v.wait_ge(chain, n[0])

                v.wait_ge(loaded, 80)
                link(v.tensor_tensor(e.segc[:, :], dst[:, :], prv[:, :], ALU.is_equal))
                link(v.tensor_tensor(e.segn[:, :], dst[:, :], nxt[:, :], ALU.is_equal))
                link(v.tensor_tensor(tmp[:, :], eid[:, :], e.segc[:, :], ALU.mult))
                link(v.tensor_tensor(tmp[:, :], eid[:, :], tmp[:, :], ALU.subtract))
                v.tensor_tensor_scan(start[:, :], tmp[:, :], tmp[:, :], 0.0, ALU.max, ALU.max).then_inc(local_done, 1)
                link(v.memset(rows[0:1, :], 0.0))
                v.wait_ge(turned, 1)
                link(v.tensor_copy(ends[0:1, :], pt[0:1, :]))
                v.tensor_tensor_scan(rows[0:1, 1:P + 1], ends[0:1, :], ends[0:1, :], 0.0,
                                     ALU.max, ALU.max).then_inc(row_done, 1)
                v.wait_ge(carried, 1)
                link(v.tensor_copy(carry[:, :], pc[:, :]))
                v.tensor_scalar(start[:, :], start[:, :], carry[:, 0:1], None, ALU.max).then_inc(meta_done, 1)

                v.wait_ge(weights_in, 16)
                v.wait_ge(sig_e, 1)
                link(v.tensor_tensor(e.W["a"][0:D, :], e.W["a"][0:D, :], sig[0:D, :], ALU.mult))
                att = e.W["att"].rearrange("p (c m) -> p c m", c=4)
                pri = e.W["pri"].unsqueeze(2).broadcast_to([P, 4, D])
                link(v.tensor_tensor(att, att, pri, ALU.mult))
                link(v.tensor_scalar(e.W["att"], e.W["att"], 1.0 / 8.0, None, ALU.mult))
                link(v.tensor_scalar(e.relu_b[:, :], e.W["bffn_row"], 0.0, None, ALU.max))
                link(v.tensor_tensor(e.bfo[:, :], e.W["bf_row"], e.W["bo_row"], ALU.add))
                link(v.tensor_tensor(e.W["wob"], e.W["wob"], e.W["bf_64"], ALU.add))
                link(v.tensor_tensor(e.W["wob"][:, D:P], e.W["wob"][:, D:P], e.W["beta_64"], ALU.add))
                link(v.tensor_tensor(e.bfo_beta[:, :], e.bfo[:, :], e.W["beta"], ALU.add))
                for to, w in ((e.W["wfx"][:, 0:D], e.W["wfx"][:, 0:D]), (e.W["wob"][:, 0:D], e.W["wob"][:, 0:D]),
                              (e.W["wf2"][:, 0:D], e.W["wf2"][:, 0:D]), (e.W["wf2"][:, P:P + D], e.W["wf2"][:, P:P + D]),
                              (e.bfo_cent[:, :], e.bfo[:, :])):
                    link(v.tensor_reduce(row_sum[:, :], w, AX, ALU.add))
                    link(v.tensor_scalar(row_sum[:, :], row_sum[:, :], 1.0 / D, None, ALU.mult))
                    link(v.tensor_scalar(to, w, row_sum[:, 0:1], None, ALU.subtract))
                link(v.tensor_scalar(e.bq8[:, :], e.W["bq"], 1.0 / 8.0, None, ALU.mult))
                v.wait_ge(cleared, UT)
                v.wait_ge(types_in, 16)

                def body(st):
                    if st.on():
                        v.wait_ge(x_in[st.s], 16 * (st.k + 1))
                        wait(v, row_out[st.s], 16 * st.k)
                        v.tensor_copy(row[st.s][:, :, 0:D], xin[st.s][:, :, :]).then_inc(copied, 1)
                        v.tensor_copy(row[st.s][:, :, D], types[:, bass.ds(st.n * RN, RN)]).then_inc(typed, 1)
                run_groups(v, body, UT, 0, 2)

                by_group = lambda t: t.rearrange("p (g u) -> p g u", u=TU)
                v.wait_ge(idx_in, 48)
                v.wait_ge(majored, 1)
                v.tensor_copy(e.ptr_pay[:, :, 0], eid_major[:, :])
                v.tensor_copy(e.ptr_pay[:, :, 1], ps_major[2][:, :])
                link(v.tensor_copy(dstf[:, :, :], e.gather0[:, :, TU:2 * TU]))
                v.scalar_tensor_tensor(out=by_group(e.scat_out[:, :]), in0=by_group(ps_major[0][:, :]), scalar=FAR,
                                       in1=dstf[:, :, :], op0=ALU.mult, op1=ALU.add)
                link(v.tensor_scalar(by_group(tmp[:, :]), dstf[:, :, :], TW / 2.0, TW / 2.0 - 1.0, ALU.mult, ALU.add))
                link(v.scalar_tensor_tensor(out=e.scat_ptr[:, :], in0=ps_major[1][:, :], scalar=FAR, in1=tmp[:, :],
                                            op0=ALU.mult, op1=ALU.add))

            @block.tensor
            def _(pe):
                wait(pe, loaded, 80, e.pe_passed)
                wait(pe, local_done, 1, e.pe_passed)
                pe.transpose(pt[0:1, :], start[:, CH - 1:CH], e.C["ident"]).then_inc(turned, 1)
                wait(pe, row_done, 1, e.pe_passed)
                pe.matmul(pc[:, :], rows[0:1, 0:P], e.C["ones"][0:1, 0:1], start=True, stop=True).then_inc(carried, 1)
                wait(pe, back, 16 * 3 * NB, e.pe_passed)
                for a in range(3):
                    for b in range(NB):
                        n = min(P, CH - b * P)
                        m = pe.transpose(ps_major[a][:, b * P:b * P + n], blocks[0:n, a, b, :], e.C["ident"][0:n, 0:n])
                m.then_inc(majored, 1)


def dense(nc, e):
    with ExitStack() as ctx:
        s = Scope(nc, ctx, "den")
        slots = lambda name: [s.sb(f"{name}_{i}", [P, RN, D]) for i in range(U)]
        xin, x2, x2b, h2, x3, x3b, h3, x4 = [slots(n) for n in ("x", "x2", "x2b", "h2", "x3", "x3b", "h3", "x4")]
        hx = s.sb("hx", [P, RN, D])
        h2t = s.sb("h2t", [P, GE])
        h3t = s.sb("h3t", [P, GE])
        hid = s.sb("hid", [P, 2, GE])
        f1 = s.sb("f1", [P, RN, D])
        ps_t2, ps_t3 = s.ps("t2", [P, GE]), s.ps("t3", [P, GE])
        ps_hid = s.ps("hid", [P, 2, GE])
        ps_m, ps_h = s.ps("m", [P, RN, D]), s.ps("h", [P, RN, 2, D])
        n2, n3, n4 = s.norm("n2", RN), s.norm("n3", RN), s.norm("n4", RN)
        x_in, h2_out, h3_out, x4_out = s.sems("x_in"), s.sems("h2_out"), s.sems("h3_out"), s.sems("x4_out")
        x2_done, x2b_done, h2_done, x3_done, x3b_done, h3_done, hx_done, x4_done = [
            s.sem(n) for n in ("x2", "x2b", "h2", "x3", "x3b", "h3", "hx", "x4")]
        t2, t2_kept, hid_ready, hid_kept, m_ready = [s.sem(n) for n in ("t2", "t2k", "hidr", "hidk", "mr")]
        t3, t3_kept, h_ready = [s.sem(n) for n in ("t3", "t3k", "hr")]
        idx_c, ptr_out = s.sem("idx_c"), s.sems("ptr_out")
        sidx = [s.sb(f"sidx{i}", [P, TU], I32) for i in range(U)]
        spay = [s.sb(f"spay{i}", [P, TU, 2]) for i in range(U)]
        rows = lambda b: b.unsqueeze(1).broadcast_to([P, RN, D])

        with nc.Block() as block:
            @block.gpsimd
            def _(pool):
                pairs = e.T0.rearrange("n (a b) -> (n a) b", b=2)

                def body(st):
                    f = st.back(3)
                    if st.on():
                        i = st.s
                        wait(pool, x_in[i], 16 * (st.k + 1), e.pool_passed)
                        wait(pool, n2.centered, st.n - (U - 1), e.pool_passed)
                        pool.tensor_tensor(x2[i][:, :, :], xin[i][:, :, :], rows(e.relu_b[:, :]), ALU.add).then_inc(x2_done, 1)
                        wait(pool, x3_done, st.n - (U - 1), e.pool_passed)
                        wait(pool, x2_done, st.n + 1, e.pool_passed)
                        pool.tensor_tensor(x2b[i][:, :, :], x2[i][:, :, :], rows(e.W["b1_row"]), ALU.add).then_inc(x2b_done, 1)
                        wait(pool, ptr_out[i], 16 * TU * st.k, e.pool_passed)
                        pool.tensor_copy(sidx[i][:, :], e.scat_ptr[:, bass.ds(st.n * TU, TU)]).then_inc(idx_c, 1)
                        pool.tensor_copy(spay[i][:, :, :], e.ptr_pay[:, bass.ds(st.n * TU, TU), :]).then_inc(idx_c, 1)
                        wait(pool, idx_c, (st.n + 1) * 2, e.pool_passed)
                        for u in range(TU):
                            pool.indirect_dma_start(pairs, bass.IndirectOffsetOnAxis(ap=sidx[i][:, u:u + 1], axis=0),
                                                    spay[i][:, u, :], None, bounds_check=NP * TW // 2 - 1,
                                                    oob_is_err=False).then_inc(ptr_out[i], 16)
                    if f.on():
                        wait(pool, x3_done, f.n + 1, e.pool_passed)
                        wait(pool, hx_done, f.n - (U - 1), e.pool_passed)
                        pool.tensor_tensor(x3b[f.s][:, :, :], x3[f.s][:, :, :], rows(e.bfo_beta[:, :]), ALU.add).then_inc(x3b_done, 1)
                run_groups(pool, body, U, 3)
                for i in range(U):
                    wait(pool, ptr_out[i], 16 * TU * (NG // U), e.pool_passed)

            @block.sync
            def _(sp):
                def body(st):
                    if st.on():
                        wait(sp, x2_done, st.n - (U - 1), e.sp_passed)
                        sp.dma_start(xin[st.s][:, :, :], node_rows(e.x, st.n * GN)).then_inc(x_in[st.s], 16)
                    b = st.back(2)
                    if b.on():
                        wait(sp, h2_done, b.n + 1, e.sp_passed)
                        sp.dma_start(node_rows(e.U2, b.n * GN + EP), h2[b.s][:, :, :]).then_inc(h2_out[b.s], 16)
                    b = st.back(4)
                    if b.on():
                        wait(sp, h3_done, b.n + 1, e.sp_passed)
                        sp.dma_start(node_rows(e.U3, b.n * GN + EP), h3[b.s][:, :, :]).then_inc(h3_out[b.s], 16)
                    b = st.back(6)
                    if b.on():
                        wait(sp, x4_done, b.n + 1, e.sp_passed)
                        sp.dma_start(node_rows(e.out, b.n * GN), x4[b.s][:, :, :]).then_inc(x4_out[b.s], 16)
                run_groups(sp, body, U, 6)
                for sems in (h2_out, h3_out, x4_out):
                    for i in range(U):
                        wait(sp, sems[i], 16 * (NG // U), e.sp_passed)

            @block.vector
            def _(v):
                def body(st):
                    d, f, g = st, st.back(2), st.back(4)
                    cd, cf, cg = (Chain(v, n.chain, b, k) for n, b, k in ((n2, d, 2), (n3, f, 2), (n4, g, 3)))
                    if g.on():
                        v.wait_ge(h_ready, g.n + 1)
                        v.tensor_tensor(n4.cent[:, :, :], ps_h[:, :, 0, :], rows(e.bfo_cent[:, :]), ALU.add).then_inc(n4.centered, 1)
                    if d.on():
                        v.wait_ge(x2_done, d.n + 1)
                        cd.put(n2.total(v, x2[d.s][:, :, :]))
                    if g.on():
                        v.wait_ge(x3b_done, g.n + 1)
                        wait(v, x4_done, g.n)
                        v.tensor_tensor(hx[:, :, :], ps_h[:, :, 1, :], x3b[g.s][:, :, :], ALU.add).then_inc(hx_done, 1)
                    if d.on():
                        cd.join()
                        n2.shift(v, x2[d.s][:, :, :])
                    if g.on():
                        n4.sumsq(v, g)
                    if f.on():
                        v.wait_ge(m_ready, f.n + 1)
                        v.wait_ge(x2b_done, f.n + 1)
                        wait(v, x3b_done, f.n - (U - 1))
                        v.tensor_tensor(x3[f.s][:, :, :], ps_m[:, :, :], x2b[f.s][:, :, :], ALU.add).then_inc(x3_done, 1)
                    if f.on():
                        v.wait_ge(x3_done, f.n + 1)
                        cf.put(n3.total(v, x3[f.s][:, :, :]))
                    if f.on():
                        cf.join()
                        n3.shift(v, x3[f.s][:, :, :])
                    if g.on():
                        v.wait_ge(n4.rooted, g.n + 1)
                        cg.put(v.reciprocal(n4.rstd[:, :], n4.std[:, :]))
                        cg.join()
                        cg.put(v.tensor_tensor(f1[:, :, :], n4.cent[:, :, :], n4.over(n4.rstd), ALU.mult))
                        cg.join()
                        cg.put(v.tensor_tensor(f1[:, :, :], f1[:, :, :], rows(e.W["gamma"]), ALU.mult))
                    if d.on():
                        v.wait_ge(n2.rooted, d.n + 1)
                        cd.put(v.reciprocal(n2.rstd[:, :], n2.std[:, :]))
                    if f.on():
                        n3.sumsq(v, f)
                    if d.on():
                        cd.join()
                        wait(v, h2_out[d.s], 16 * d.k)
                        n2.relu_to(v, h2[d.s][:, :, :]).then_inc(h2_done, 1)
                        cd.end()
                    if f.on():
                        v.wait_ge(n3.rooted, f.n + 1)
                        cf.put(v.reciprocal(n3.rstd[:, :], n3.std[:, :]))
                    if g.on():
                        cg.join()
                        v.wait_ge(hx_done, g.n + 1)
                        wait(v, x4_out[g.s], 16 * g.k)
                        v.tensor_tensor(x4[g.s][:, :, :], f1[:, :, :], hx[:, :, :], ALU.add).then_inc(x4_done, 1)
                        cg.end()
                    if f.on():
                        cf.join()
                        wait(v, h3_out[f.s], 16 * f.k)
                        n3.relu_to(v, h3[f.s][:, :, :]).then_inc(h3_done, 1)
                        cf.end()
                run_groups(v, body, U, 4)

            @block.scalar
            def _(a):
                eps = e.C["eps"]

                def body(st):
                    d, f, g, d1, f1 = st, st.back(2), st.back(4), st.back(1), st.back(3)
                    if d1.on():
                        a.wait_ge(t2, d1.n + 1)
                        a.copy(h2t[:, :], ps_t2[:, :]).then_inc(t2_kept, 1)
                    if f1.on():
                        a.wait_ge(t3, f1.n + 1)
                        a.copy(h3t[:, :], ps_t3[:, :]).then_inc(t3_kept, 1)
                    if g.on():
                        n4.square(a, g)
                    if d.on():
                        n2.sum_squares(a, d)
                    if g.on():
                        n4.root(a, g, eps)
                    if d.on():
                        n2.root(a, d, eps)
                    if d1.on():
                        a.wait_ge(hid_ready, d1.n + 1)
                        a.activation(hid[:, :, :], ps_hid[:, :, :], ACT.Relu, bias=e.W["b0"]).then_inc(hid_kept, 1)
                    if f.on():
                        n3.square(a, f)
                    if f.on():
                        n3.root(a, f, eps)
                run_groups(a, body, U, 4)

            @block.tensor
            def _(pe):
                def turn(ps, rows):
                    for c in range(4):
                        m = pe.transpose(ps[:, c * P:(c + 1) * P], rows[:, 2 * c:2 * c + 2, :].rearrange("p a f -> p (a f)"),
                                         e.C["ident"])
                    return m

                def body(st):
                    d, f = st.back(1), st.back(3)
                    if d.on():
                        wait(pe, h2_done, d.n + 1, e.pe_passed)
                        wait(pe, t2_kept, d.n, e.pe_passed)
                        turn(ps_t2, h2[d.s]).then_inc(t2, 1)
                    if f.on():
                        wait(pe, h3_done, f.n + 1, e.pe_passed)
                        wait(pe, t3_kept, f.n, e.pe_passed)
                        turn(ps_t3, h3[f.s]).then_inc(t3, 1)
                    if d.on():
                        wait(pe, t2_kept, d.n + 1, e.pe_passed)
                        wait(pe, hid_kept, d.n, e.pe_passed)
                        for a in range(2):
                            m = pe.matmul(ps_hid[:, a, :], e.W["w0"][64 * a:64 * a + 64, :], h2t[64 * a:64 * a + 64, :],
                                          start=True, stop=True)
                        m.then_inc(hid_ready, 1)
                    if f.on():
                        wait(pe, t3_kept, f.n + 1, e.pe_passed)
                        wait(pe, hx_done, f.n, e.pe_passed)
                        for c in range(4):
                            m = pe.matmul(ps_h[:, 2 * c:2 * c + 2, :, :], h3t[:, c * P:(c + 1) * P],
                                          e.W["wf2"], start=(c % 2 == 0), stop=(c % 2 == 1), skip_group_check=True)
                        m.then_inc(h_ready, 1)
                    if d.on():
                        wait(pe, hid_kept, d.n + 1, e.pe_passed)
                        wait(pe, x3_done, d.n, e.pe_passed)
                        for j in range(RN):
                            a, c = j % 2, j // 2
                            m = pe.matmul(ps_m[:, j, :], hid[:, a, c * P:(c + 1) * P], e.W["w1"],
                                          start=(j == 0), stop=(j == RN - 1), skip_group_check=True)
                        m.then_inc(m_ready, 1)
                run_groups(pe, body, U, 4)


def scores(nc, e):
    with ExitStack() as ctx:
        s = Scope(nc, ctx, "sc")
        R = 2 * TU
        NB = -(-CH // P)
        idx = [s.sb(f"idx{i}", [P, R], I32) for i in range(U)]
        xg = [s.sb(f"xg{i}", [P, R, TW]) for i in range(U)]
        hid = [s.sb(f"h{i}", [P, R, D]) for i in range(U)]
        onehot = s.sb("onehot", [P, R, 4])
        hx = [s.sb(f"hx{i}", [P, R, 4, D]) for i in range(U)]
        ht = s.sb("ht", [P, 4, GE])
        et = [s.sb(f"et{i}", [P, GE], I32) for i in range(U)]
        qx = s.sb("qx", [P, 4, GE])
        kv = [s.sb(f"kv{i}", [P, GE]) for i in range(U)]
        prod = s.sb("prod", [D, GE])
        lmajor = s.sb("lmajor", [P, CH])
        lrows = s.sb("lrows", [P, NB, P])
        ps_t = s.ps("t", [P, 4, GE])
        ps_q, ps_kv, ps_r, ps_l = s.ps("q", [P, GE]), s.ps("kv", [P, GE]), s.ps("r", [D, GE]), s.ps("l", [P, TU])
        nrm = s.norm("n", R)
        gathered, et_in, h_out, xd_out, v_out = [s.sems(n) for n in ("g", "et", "ho", "xd", "vo")]
        l_turned, rows_kept, l_out = s.sem("lt"), s.sem("rk"), s.sem("lo")
        idx_c, h_done, hx_done, turned, ht_kept, q_ready, kv_ready = [
            s.sem(n) for n in ("ic", "h", "hx", "tu", "hk", "q", "kv")]
        q_used, r_ready, kv_kept, prod_done, l_ready, l_kept = [s.sem(n) for n in ("qu", "rr", "kvk", "pd", "lr", "lk")]
        ptr_c = s.sem("ptr")

        with nc.Block() as block:
            @block.gpsimd
            def _(pool):
                def body(st):
                    if st.on():
                        i = st.s
                        wait(pool, gathered[i], 16 * R * st.k, e.pool_passed)
                        pool.tensor_copy(idx[i][:, :], e.gather0[:, st.n, :] if isinstance(st.n, int) else
                                         e.gather0[:, bass.ds(st.n, 1), :].rearrange("p a r -> p (a r)")).then_inc(idx_c, 1)
                    b = st.back(1)
                    if not b.on():
                        return
                    i = b.s
                    wait(pool, idx_c, b.n + 1, e.pool_passed)
                    wait(pool, h_done, b.n - (U - 1), e.pool_passed)
                    wait(pool, ptr_c, b.n - (U - 1), e.pool_passed)
                    wait(pool, xd_out[i], 16 * b.k, e.pool_passed)
                    for u in range(R):
                        pool.indirect_dma_start(xg[i][:, u, :], None, e.T0,
                                                bass.IndirectOffsetOnAxis(ap=idx[i][:, u:u + 1], axis=0),
                                                bounds_check=NP - 1, oob_is_err=False).then_inc(gathered[i], 16)
                run_groups(pool, body, U, 1)

            @block.sync
            def _(sp):
                def body(st):
                    if st.on():
                        wait(sp, q_used, st.n - (U - 1), e.sp_passed)
                        sp.dma_start(et[st.s][:, :], over_parts(e.etype_row, st.n * GE, P)).then_inc(et_in[st.s], 16)
                        wait(sp, gathered[st.s], 16 * R * (st.k + 1), e.sp_passed)
                        sp.dma_start(edge_rows(e.XD, st.n * GE, TW), xg[st.s][:, TU:R, :]).then_inc(xd_out[st.s], 16)
                    b = st.back(1)
                    if b.on():
                        wait(sp, h_done, b.n + 1, e.sp_passed)
                        sp.dma_start(edge_rows(e.U1, b.n * GE + EP), hid[b.s][:, 0:TU, :]).then_inc(h_out[b.s], 16)
                    b = st.back(3)
                    if b.on():
                        wait(sp, kv_kept, b.n + 1, e.sp_passed)
                        sp.dma_start(e.VT[:, bass.ds(b.n * GE, GE)], kv[b.s][D:P, :]).then_inc(v_out[b.s], 16)
                run_groups(sp, body, U, 3)
                for b in range(NB):
                    n = min(P, CH - b * P)
                    wait(sp, rows_kept, b + 1, e.sp_passed)
                    sp.dma_start(e.logit[b * P * P:(b * P + n) * P].rearrange("(r p) -> r p", p=P), lrows[0:n, b, :]).then_inc(l_out, 16)
                wait(sp, l_out, 16 * NB, e.sp_passed)
                for sems in (xd_out, h_out, v_out):
                    for i in range(U):
                        wait(sp, sems[i], 16 * (NG // U), e.sp_passed)

            @block.vector
            def _(v):
                def body(st):
                    b, g = st.back(2), st.back(3)
                    c = Chain(v, nrm.chain, st, 3)

                    def mask(r):
                        return v.scalar_tensor_tensor(out=qx[:, r, :], in0=et[b.s][:, :], scalar=e.C["rels"][:, r:r + 1],
                                                      in1=ps_q[:, :], op0=ALU.is_equal, op1=ALU.mult)

                    if st.on():
                        v.wait_ge(gathered[st.s], 16 * R * (st.k + 1))
                        c.put(nrm.total(v, xg[st.s][:, :, 0:D]))
                    if b.on():
                        v.wait_ge(q_ready, b.n + 1)
                        v.wait_ge(et_in[b.s], 16 * (b.k + 1))
                        wait(v, r_ready, b.n)
                        mask(0)
                    if st.on():
                        c.join()
                        nrm.shift(v, xg[st.s][:, :, 0:D])
                    if b.on():
                        mask(1)
                        mask(2)
                        mask(3).then_inc(q_used, 1)
                    if g.on():
                        v.wait_ge(r_ready, g.n + 1)
                        v.wait_ge(kv_kept, g.n + 1)
                        wait(v, l_ready, g.n)
                        v.tensor_tensor(prod[:, :], ps_r[:, :], kv[g.s][0:D, :], ALU.mult).then_inc(prod_done, 1)
                    if st.on():
                        nrm.sumsq(v, st)
                        v.tensor_copy(e.ptrs[:, bass.ds(st.n * TU, TU), :], xg[st.s][:, 0:TU, TW - 2:TW]).then_inc(ptr_c, 1)
                        wait(v, hx_done, st.n)
                        c.put(v.tensor_tensor(onehot[:, :, :], e.C["types"].unsqueeze(1).broadcast_to([P, R, 4]),
                                              xg[st.s][:, :, D:D + 1].broadcast_to([P, R, 4]), ALU.is_equal))
                        nrm.recip(v, c, st)
                        wait(v, h_out[st.s], 16 * st.k)
                        nrm.relu_to(v, hid[st.s][:, :, :]).then_inc(h_done, 1)
                        v.wait_ge(h_done, st.n + 1)
                        wait(v, turned, 2 * (st.n - (U - 1)))
                        for r in range(2):
                            m = v.tensor_tensor(hx[st.s][:, r * TU:(r + 1) * TU, :, :],
                                                hid[st.s][:, r * TU:(r + 1) * TU, :].unsqueeze(2).broadcast_to([P, TU, 4, D]),
                                                onehot[:, r * TU:(r + 1) * TU, :].unsqueeze(3).broadcast_to([P, TU, 4, D]),
                                                ALU.mult)
                        m.then_inc(hx_done, 1)
                        c.end()
                run_groups(v, body, U, 3)

            @block.scalar
            def _(a):
                def body(st):
                    d, b, g = st.back(1), st.back(2), st.back(4)

                    def keep(side):
                        a.wait_ge(turned, 2 * d.n + side + 1)
                        a.copy(ht[:, 2 * side:2 * side + 2, :], ps_t[:, 2 * side:2 * side + 2, :]).then_inc(ht_kept, 1)

                    if b.on():
                        a.wait_ge(kv_ready, b.n + 1)
                        wait(a, prod_done, b.n - (U - 1))
                        wait(a, v_out[b.s], 16 * b.k)
                        a.copy(kv[b.s][:, :], ps_kv[:, :]).then_inc(kv_kept, 1)
                    if d.on():
                        keep(0)
                    if st.on():
                        nrm.square(a, st)
                    if d.on():
                        keep(1)
                    if g.on():
                        a.wait_ge(l_ready, g.n + 1)
                        a.copy(lmajor[:, bass.ds(g.n * TU, TU)], ps_l[:, :]).then_inc(l_kept, 1)
                    if st.on():
                        nrm.root(a, st, e.C["eps"])
                run_groups(a, body, U, 4)
                a.wait_ge(l_turned, 1)
                for b in range(NB):
                    n = min(P, CH - b * P)
                    a.copy(lrows[0:n, b, :], ps_t[0:n, b, 0:P]).then_inc(rows_kept, 1)

            @block.tensor
            def _(pe):
                def body(st):
                    d, b, g = st.back(1), st.back(2), st.back(4)
                    if d.on():
                        wait(pe, hx_done, d.n + 1, e.pe_passed)
                        wait(pe, ht_kept, 2 * d.n, e.pe_passed)
                        for side in range(2):
                            for u in range(TU):
                                for c in range(2):
                                    m = pe.transpose(ps_t[:, 2 * side + c, u * P:(u + 1) * P],
                                                     hx[d.s][:, (1 - side) * TU + u, 2 * c:2 * c + 2, :].rearrange("p a f -> p (a f)"),
                                                     e.C["ident"])
                            m.then_inc(turned, 1)
                    if g.on():
                        wait(pe, prod_done, g.n + 1, e.pe_passed)
                        wait(pe, l_kept, g.n, e.pe_passed)
                        for u in range(TU):
                            m = pe.matmul(ps_l[:, u:u + 1], prod[:, u * P:(u + 1) * P], e.C["ones"][0:D, 0:1],
                                          start=(u == 0), stop=(u == TU - 1), skip_group_check=True)
                        m.then_inc(l_ready, 1)
                    if d.on():
                        wait(pe, ht_kept, 2 * d.n + 1, e.pe_passed)
                        wait(pe, q_used, d.n, e.pe_passed)
                        for c in range(2):
                            m = pe.matmul(ps_q[:, :], e.W["q"][:, c * P:(c + 1) * P], ht[:, c, :], start=(c == 0), stop=(c == 1))
                        m.then_inc(q_ready, 1)
                    if b.on():
                        wait(pe, q_used, b.n + 1, e.pe_passed)
                        wait(pe, prod_done, b.n, e.pe_passed)
                        for r in range(4):
                            m = pe.matmul(ps_r[:, :], e.W["att"][:, r * D:(r + 1) * D], qx[:, r, :], start=(r == 0), stop=(r == 3))
                        m.then_inc(r_ready, 1)
                    if d.on():
                        wait(pe, ht_kept, 2 * d.n + 2, e.pe_passed)
                        wait(pe, kv_kept, d.n, e.pe_passed)
                        for c in range(2):
                            m = pe.matmul(ps_kv[:, :], e.W["kv"][:, c * P:(c + 1) * P], ht[:, 2 + c, :], start=(c == 0), stop=(c == 1))
                        m.then_inc(kv_ready, 1)
                run_groups(pe, body, U, 4)
                wait(pe, l_kept, NG)
                for b in range(NB):
                    n = min(P, CH - b * P)
                    m = pe.transpose(ps_t[0:n, b, 0:P], lmajor[:, b * P:b * P + n], e.C["ident"])
                m.then_inc(l_turned, 1)


def softmax(nc, e):
    with ExitStack() as ctx:
        s = Scope(nc, ctx, "sm")
        lg, a1, a2, a3, a4, m = [s.sb(n, [P, CH]) for n in ("lg", "a1", "a2", "a3", "a4", "m")]
        ones = s.sb("ones", [P, CH])
        ends = s.sb("ends", [1, 2, P])
        srcs = s.sb("srcs", [P, NG, TU])
        carried = s.sb("carried", [1, P + 1])
        carry = s.sb("carry", [P, 1])
        eid = s.sb("eid", [P, CH], I32)
        eidf = s.sb("eidf", [P, CH])
        ps_a, ps_b, ps_c = s.ps("a", [1, P]), s.ps("b", [1, P]), s.ps("c", [P, 1])
        loaded, stored, chain, p_ready, iot = s.sem("loaded"), s.sem("stored"), s.sem("chain"), s.sem("pr"), s.sem("iot")
        local, turned, row_done, back, alpha_done = [s.sem(n) for n in ("local", "turned", "row", "back", "alpha")]
        max_done = s.sem("maxd")

        with nc.Block() as block:
            @block.sync
            def _(sp):
                sp.dma_start(lg[:, :], e.logit.rearrange("(p j) -> p j", j=CH)).then_inc(loaded, 16)
                wait(sp, alpha_done, 1, e.sp_passed)
                sp.dma_start(e.alpha.rearrange("(p j) -> p j", j=CH), a1[:, :]).then_inc(stored, 16)
                wait(sp, stored, 16, e.sp_passed)

            @block.gpsimd
            def _(pool):
                pool.iota(eid[:, :], [[P, CH]], base=0, channel_multiplier=1).then_inc(iot, 1)

            @block.scalar
            def _(a):
                a.wait_ge(max_done, 1)
                a.activation(m[:, :], lg[:, :], ACT.Exp).then_inc(p_ready, 1)

            @block.tensor
            def _(pe):
                for i in range(4):
                    wait(pe, local, i + 1, e.pe_passed)
                    col = CH - 1 if i % 2 == 0 else 0
                    val = a1 if i % 2 == 0 else a3
                    pre = a2 if i % 2 == 0 else a4
                    pe.transpose(ps_a[:, :], val[:, col:col + 1], e.C["ident"])
                    pe.transpose(ps_b[:, :], pre[:, col:col + 1], e.C["ident"]).then_inc(turned, 1)
                    wait(pe, row_done, i + 1, e.pe_passed)
                    row = carried[0:1, 0:P] if i % 2 == 0 else carried[0:1, 1:P + 1]
                    pe.matmul(ps_c[:, :], row, e.C["ones"][0:1, 0:1], start=True, stop=True).then_inc(back, 1)

            @block.vector
            def _(v):
                n = [0]

                def link(ins):
                    n[0] += 1
                    ins.then_inc(chain, 1)
                    v.wait_ge(chain, n[0])

                def seg_scan(i, val, pre, x, is_max):
                    rev = slice(None, None, -1 if i % 2 else 1)
                    same = e.segn if i % 2 else e.segc
                    link(v.tensor_tensor_scan(pre[:, rev], same[:, rev], ones[:, :], 1.0, ALU.mult, ALU.mult))
                    if is_max:
                        link(v.tensor_scalar(val[:, :], same[:, :], -1.0, BIG, ALU.add, ALU.mult))
                        v.tensor_tensor_scan(val[:, rev], val[:, rev], x[:, rev], -BIG, ALU.add, ALU.max).then_inc(local, 1)
                    else:
                        v.tensor_tensor_scan(val[:, rev], same[:, rev], x[:, rev], 0.0, ALU.mult, ALU.add).then_inc(local, 1)
                    v.wait_ge(turned, i + 1)
                    none = -BIG if is_max else 0.0
                    link(v.memset(carried[0:1, :], none))
                    link(v.tensor_copy(ends[0:1, 0, :], ps_a[:, :]))
                    out = carried[0:1, 1:P + 1] if i % 2 == 0 else carried[0:1, 0:P]
                    if is_max:
                        link(v.tensor_scalar(ends[0:1, 1, :], ps_b[:, :], -1.0, BIG, ALU.add, ALU.mult))
                    else:
                        link(v.tensor_copy(ends[0:1, 1, :], ps_b[:, :]))
                    v.tensor_tensor_scan(out[:, rev], ends[0:1, 1, rev], ends[0:1, 0, rev], none,
                                         ALU.add if is_max else ALU.mult, ALU.max if is_max else ALU.add).then_inc(row_done, 1)
                    v.wait_ge(back, i + 1)
                    link(v.tensor_copy(carry[:, :], ps_c[:, :]))
                    if is_max:
                        link(v.tensor_scalar(pre[:, :], pre[:, :], -1.0, BIG, ALU.add, ALU.mult))
                        link(v.scalar_tensor_tensor(out=val[:, :], in0=pre[:, :], scalar=carry[:, 0:1], in1=val[:, :],
                                                    op0=ALU.add, op1=ALU.max))
                    else:
                        link(v.scalar_tensor_tensor(out=val[:, :], in0=pre[:, :], scalar=carry[:, 0:1], in1=val[:, :],
                                                    op0=ALU.mult, op1=ALU.add))

                link(v.memset(ones[:, :], 1.0))
                v.wait_ge(loaded, 16)
                seg_scan(0, a1, a2, lg, True)
                seg_scan(1, a3, a4, lg, True)
                link(v.tensor_tensor(a1[:, :], a1[:, :], a3[:, :], ALU.max))
                v.tensor_tensor(lg[:, :], lg[:, :], a1[:, :], ALU.subtract).then_inc(max_done, 1)
                v.wait_ge(p_ready, 1)
                seg_scan(2, a1, a2, m, False)
                seg_scan(3, a3, a4, m, False)
                link(v.tensor_tensor(a1[:, :], a1[:, :], a3[:, :], ALU.add))
                link(v.tensor_tensor(a1[:, :], a1[:, :], m[:, :], ALU.subtract))
                link(v.tensor_scalar(a2[:, :], a1[:, :], 0.0, None, ALU.is_equal))
                link(v.tensor_tensor(a1[:, :], a1[:, :], a2[:, :], ALU.add))
                link(v.reciprocal(a1[:, :], a1[:, :]))
                v.tensor_tensor(a1[:, :], a1[:, :], m[:, :], ALU.mult).then_inc(alpha_done, 1)

                v.wait_ge(iot, 1)
                link(v.tensor_copy(eidf[:, :], eid[:, :]))
                last, frst = e.ptrs[:, :, 0], e.ptrs[:, :, 1]
                link(v.tensor_scalar(e.has[:, :], last, 1.0, None, ALU.min))

                def choose(out, ptr, base, off):
                    link(v.tensor_scalar(a4[:, :], base, float(off), None, ALU.add))
                    link(v.tensor_tensor(a3[:, :], ptr, a4[:, :], ALU.subtract))
                    link(v.scalar_tensor_tensor(out=a3[:, :], in0=a3[:, :], scalar=-1.0, in1=e.has[:, :],
                                                op0=ALU.add, op1=ALU.mult))
                    link(v.tensor_tensor(out[:, :], a3[:, :], a4[:, :], ALU.add))

                choose(e.idx1, last, eidf[:, :], EP)
                choose(e.idxsd, frst, eidf[:, :], 0)
                link(v.tensor_copy(srcs[:, :, :], e.gather0[:, :, 0:TU]))
                choose(e.idx2, last, srcs[:, :, :].rearrange("p a b -> p (a b)"), EP)


def attend(nc, e):
    with ExitStack() as ctx:
        s = Scope(nc, ctx, "at")
        vin = [s.sb(f"v{i}", [P, GE]) for i in range(U)]
        et = [s.sb(f"et{i}", [P, GE], I32) for i in range(U)]
        al = [s.sb(f"al{i}", [D, GE]) for i in range(U)]
        same = [s.sb(f"same{i}", [D, GE]) for i in range(U)]
        xd = [s.sb(f"xd{i}", [P, TU, TW]) for i in range(U)]
        vx = [s.sb(f"vx{i}", [P, 4, GE]) for i in range(U)]
        eq = [s.sb(f"eq{i}", [P, 2, GE]) for i in range(U)]
        am = s.sb("am", [D, GE])
        agg = [s.sb(f"agg{i}", [D, GE]) for i in range(U)]
        onehot = s.sb("onehot", [P, TU, 4])
        ysel = [s.sb(f"ysel{i}", [P, TU, 4, D]) for i in range(U)]
        y2 = s.sb("y2", [P, TU, 2, D])
        y1 = s.sb("y1", [P, TU, D])
        hx = [s.sb(f"hx{i}", [P, TU, 2 * D]) for i in range(U)]
        xh = [s.sb(f"xh{i}", [P, GE]) for i in range(U)]
        ps_m, ps_y, ps_t = [s.ps(f"m{i}", [D, GE]) for i in range(U)], s.ps("y", [P, TU, 4, D]), s.ps("t", [P, GE])
        nrm = s.norm("n", TU)
        v_in, et_in, al_in, same_in, xd_in, h_out, xh_out = [s.sems(n) for n in ("v", "et", "al", "sa", "xd", "ho", "xho")]
        vx_low, vx_high, m_ready, am_done, agg_done, y_ready, y_sel, y2_done, y1_done, x1_done, h_done, turned, kept, oh_done, eq_off, eq_done = [
            s.sem(n) for n in ("vxl", "vxh", "mr", "am", "ag", "yr", "ys", "y2", "y1", "x1", "h", "tu", "kept", "oh", "eo", "ed")]

        with nc.Block() as block:
            @block.sync
            def _(sp):
                def body(st):
                    i, at = st.s, st.n * GE
                    if st.on():
                        wait(sp, vx_low, st.n - (U - 1), e.sp_passed)
                        wait(sp, vx_high, st.n - (U - 1), e.sp_passed)
                        for half in range(2):
                            sp.dma_start(vin[i][half * D:(half + 1) * D, :], e.VT[:, bass.ds(at, GE)]).then_inc(v_in[i], 16)
                        sp.dma_start(et[i][:, :], over_parts(e.etype_row, at, P)).then_inc(et_in[i], 16)
                    b = st.back(1)
                    if b.on():
                        wait(sp, agg_done, b.n - (U - 1), e.sp_passed)
                        sp.dma_start(al[b.s][:, :], over_parts(e.alpha, b.n * GE, D)).then_inc(al_in[b.s], 16)
                        sp.dma_start(same[b.s][:, :], over_parts(e.same_prev, b.n * GE, D)).then_inc(same_in[b.s], 16)
                    b = st.back(2)
                    if b.on():
                        wait(sp, x1_done, b.n - (U - 1), e.sp_passed)
                        sp.dma_start(xd[b.s][:, :, :], edge_rows(e.XD, b.n * GE, TW)).then_inc(xd_in[b.s], 16)
                run_groups(sp, body, U, 2)

            @block.gpsimd
            def _(pool):
                def body(st):
                    b = st.back(4)
                    if b.on():
                        i = b.s
                        wait(pool, y_sel, b.n + 1, e.pool_passed)
                        wait(pool, y1_done, b.n, e.pool_passed)
                        pool.tensor_tensor(y2[:, :, :, :], ysel[i][:, :, 0:2, :], ysel[i][:, :, 2:4, :], ALU.add).then_inc(y2_done, 1)
                        wait(pool, y2_done, b.n + 1, e.pool_passed)
                        wait(pool, x1_done, b.n, e.pool_passed)
                        pool.tensor_tensor(y1[:, :, :], y2[:, :, 0, :], y2[:, :, 1, :], ALU.add).then_inc(y1_done, 1)
                        wait(pool, y1_done, b.n + 1, e.pool_passed)
                        wait(pool, turned, b.n - (U - 1), e.pool_passed)
                        pool.tensor_tensor(hx[i][:, :, D:2 * D], y1[:, :, :], xd[i][:, :, 0:D], ALU.add).then_inc(x1_done, 1)
                    if st.on():
                        i = st.s
                        wait(pool, v_in[i], 32 * (st.k + 1), e.pool_passed)
                        wait(pool, eq_done, st.n + 1, e.pool_passed)
                        wait(pool, m_ready, st.n - (U - 1), e.pool_passed)
                        pool.tensor_tensor(vx[i][:, 2:4, :], eq[i][:, :, :],
                                           vin[i][:, :].unsqueeze(1).broadcast_to([P, 2, GE]), ALU.mult).then_inc(vx_high, 1)
                run_groups(pool, body, U, 4)

            @block.vector
            def _(v):
                def body(st):
                    b, f, g = st.back(2), st.back(4), st.back(5)
                    c = Chain(v, nrm.chain, g, 2)

                    def mask(r):
                        return v.scalar_tensor_tensor(out=vx[st.s][:, r, :], in0=et[st.s][:, :], scalar=e.C["rels"][:, r:r + 1],
                                                      in1=vin[st.s][:, :], op0=ALU.is_equal, op1=ALU.mult)

                    if f.on():
                        v.wait_ge(xd_in[f.s], 16 * (f.k + 1))
                        wait(v, y_sel, f.n)
                        v.tensor_tensor(onehot[:, :, :], e.C["types"].unsqueeze(1).broadcast_to([P, TU, 4]),
                                        xd[f.s][:, :, D:D + 1].broadcast_to([P, TU, 4]), ALU.is_equal).then_inc(oh_done, 1)
                    if g.on():
                        v.wait_ge(x1_done, g.n + 1)
                        c.put(nrm.total(v, hx[g.s][:, :, D:2 * D]))
                    if f.on():
                        v.wait_ge(y_ready, f.n + 1)
                        v.wait_ge(oh_done, f.n + 1)
                        wait(v, y2_done, f.n - (U - 1))
                        v.tensor_tensor(ysel[f.s][:, :, :, :], ps_y[:, :, :, :],
                                        onehot[:, :, :].unsqueeze(3).broadcast_to([P, TU, 4, D]), ALU.mult).then_inc(y_sel, 1)
                    if g.on():
                        c.join()
                        nrm.shift(v, hx[g.s][:, :, D:2 * D])
                    if g.on():
                        nrm.sumsq(v, g)
                    if st.on():
                        v.wait_ge(v_in[st.s], 32 * (st.k + 1))
                        v.wait_ge(et_in[st.s], 16 * (st.k + 1))
                        wait(v, m_ready, st.n - (U - 1))
                        mask(0)
                    if b.on():
                        i = b.s
                        v.wait_ge(m_ready, b.n + 1)
                        v.wait_ge(al_in[i], 16 * (b.k + 1))
                        wait(v, agg_done, b.n)
                        v.tensor_tensor(am[:, :], ps_m[i][:, :], al[i][:, :], ALU.mult).then_inc(am_done, 1)
                    if g.on():
                        nrm.recip(v, c, g)
                        wait(v, h_out[g.s], 16 * g.k)
                        nrm.relu_to(v, hx[g.s][:, :, 0:D]).then_inc(h_done, 1)
                        c.end()
                    if st.on():
                        mask(1).then_inc(vx_low, 1)
                    if b.on():
                        v.wait_ge(am_done, b.n + 1)
                        v.wait_ge(same_in[i], 16 * (b.k + 1))
                        wait(v, y_ready, b.n - (U - 1))
                        v.tensor_tensor_scan(agg[i][:, :], same[i][:, :], am[:, :],
                                             0.0 if b.first() else agg[(i - 1) % U][:, GE - 1:GE],
                                             ALU.mult, ALU.add).then_inc(agg_done, 1)
                run_groups(v, body, U, 5)

            @block.scalar
            def _(a):
                def body(st):
                    g, t = st.back(5), st.back(6)
                    if t.on():
                        a.dma_start(edge_rows(e.U1, t.n * GE), hx[t.s][:, :, 0:D]).then_inc(h_out[t.s], 16)
                        a.wait_ge(turned, t.n + 1)
                        wait(a, xh_out[t.s], 16 * t.k)
                        a.copy(xh[t.s][:, :], ps_t[:, :]).then_inc(kept, 1)
                    if g.on():
                        nrm.square(a, g)
                    if t.on():
                        a.wait_ge(kept, t.n + 1)
                        a.dma_start(e.XH1[:, bass.ds(t.n * GE, GE)], xh[t.s][:, :]).then_inc(xh_out[t.s], 16)
                    if g.on():
                        nrm.root(a, g, e.C["eps"])
                    if st.on():
                        i = st.s
                        a.wait_ge(et_in[i], 16 * (st.k + 1))
                        wait(a, vx_high, st.n - (U - 1))
                        for r in range(2):
                            m = a.activation(eq[i][:, r, :], et[i][:, :], ACT.Square, bias=e.C["less_rels"][:, 2 + r:3 + r])
                        m.then_inc(eq_off, 1)
                        a.wait_ge(eq_off, st.n + 1)
                        a.activation(eq[i][:, :, :], eq[i][:, :, :], ACT.Relu, bias=e.C["ones"][:, 0:1], scale=-1.0).then_inc(eq_done, 1)
                    if g.on():
                        a.wait_ge(h_done, g.n + 1)
                run_groups(a, body, U, 6)
                for sems in (h_out, xh_out):
                    for i in range(U):
                        a.wait_ge(sems[i], 16 * (NG // U))

            @block.tensor
            def _(pe):
                def body(st):
                    d, f, t = st.back(2), st.back(3), st.back(6)
                    if d.on():
                        wait(pe, vx_low, d.n + 1, e.pe_passed)
                        wait(pe, vx_high, d.n + 1, e.pe_passed)
                        wait(pe, am_done, d.n - (U - 1), e.pe_passed)
                        for r in range(4):
                            m = pe.matmul(ps_m[d.s][:, :], e.W["msg"][:, r * D:(r + 1) * D], vx[d.s][:, r, :], start=(r == 0), stop=(r == 3))
                        m.then_inc(m_ready, 1)
                    if t.on():
                        wait(pe, h_done, t.n + 1, e.pe_passed)
                        wait(pe, kept, t.n, e.pe_passed)
                        for u in range(TU):
                            m = pe.transpose(ps_t[:, u * P:(u + 1) * P], hx[t.s][:, u, :], e.C["ident"])
                        m.then_inc(turned, 1)
                    if f.on():
                        wait(pe, agg_done, f.n + 1, e.pe_passed)
                        wait(pe, y_sel, f.n, e.pe_passed)
                        for u in range(TU):
                            m = pe.matmul(ps_y[:, u, :, :], agg[f.s][:, u * P:(u + 1) * P],
                                          e.W["a"][0:D, :].rearrange("p (t f) -> p t f", t=4), start=(u % 2 == 0), stop=(u % 2 == 1),
                                          skip_group_check=True)
                        m.then_inc(y_ready, 1)
                run_groups(pe, body, U, 6)


def copy_index(e, pool, idx_all, idx, moved, copied, st, pos):
    i = st.s
    wait(pool, moved[i], 16 * TU * st.k, e.pool_passed)
    pool.tensor_copy(idx[i][:, :], idx_all[:, bass.ds(pos * TU, TU)]).then_inc(copied, 1)


def gather(e, pool, table, idx, gat, gathered, idx_c, st, rows):
    i = st.s
    wait(pool, idx_c, st.n + 1, e.pool_passed)
    for u in range(TU):
        pool.indirect_dma_start(gat[i][:, u, :], None, table,
                                bass.IndirectOffsetOnAxis(ap=idx[i][:, u:u + 1], axis=0),
                                bounds_check=rows - 1, oob_is_err=False).then_inc(gathered[i], 16)


def difference(nc, e):
    with ExitStack() as ctx:
        s = Scope(nc, ctx, "df")
        idx = [s.sb(f"idx{i}", [P, TU], I32) for i in range(U)]
        hs = [s.sb(f"hs{i}", [P, TU, D]) for i in range(U)]
        hd = [s.sb(f"hd{i}", [D, GE]) for i in range(U)]
        same = [s.sb(f"same{i}", [D, GE]) for i in range(U)]
        lastv = s.sb("lastv", [D, GE])
        hb = [s.sb(f"hb{i}", [D, GE]) for i in range(U)]
        prod = [s.sb(f"prod{i}", [D, GE]) for i in range(U)]
        diff = s.sb("diff", [D, GE])
        sd = [s.sb(f"sd{i}", [D, GE]) for i in range(U)]
        act = s.sb("act", [D, GE])
        junk_s, junk_d = s.sb("junk_s", [P, TU, D]), s.sb("junk_d", [D, GE])
        sdr = [s.sb(f"sdr{i}", [P, TU, D]) for i in range(U)]
        nacc = s.sb("nacc", [P, 2, NG])
        ntot = s.sb("ntot", [P, 2])
        nsq = s.sb("nsq", [P, 2])
        scale = s.sb("scale", [P, 1])
        ps_t = [s.ps(f"t{i}", [D, GE]) for i in range(U)]
        ps_p, ps_c, ps_b = s.ps("p", [D, GE]), s.ps("c", [P, TU]), s.ps("b", [P, TU, D])
        ps_n = s.ps("n", [P, 2])
        gathered, hd_in, same_in, sd_out = [s.sems(n) for n in ("g", "hd", "sa", "so")]
        idx_c, turned, last_done, hb_done, prod_done, diff_done, sd_done = [
            s.sem(n) for n in ("ic", "tu", "ld", "hb", "pd", "dd", "sdd")]
        p_ready, relu_done, c_ready, c_kept, b_ready, b_kept, sq1, sq2 = [
            s.sem(n) for n in ("pr", "rd", "cr", "ck", "br", "bk", "sq1", "sq2")]
        cleared, fin, tot_done, n_ready, gate_done, rooted, clip_done = [
            s.sem(n) for n in ("clr", "fin", "td", "nr", "gd", "rt", "cl")]
        pos = lambda st: st.n * -1 + (NG - 1)

        with nc.Block() as block:
            @block.gpsimd
            def _(pool):
                def body(st):
                    b = st.back(1)
                    if st.on():
                        copy_index(e, pool, e.idx1, idx, gathered, idx_c, st, pos(st))
                    if b.on():
                        wait(pool, turned, b.n - (U - 1), e.pool_passed)
                        wait(pool, sq1, b.n - (U - 1), e.pool_passed)
                        gather(e, pool, e.U1, idx, hs, gathered, idx_c, b, 2 * EP)
                run_groups(pool, body, U, 1)

            @block.sync
            def _(sp):
                def body(st):
                    if st.on():
                        i, at = st.s, pos(st) * GE
                        wait(sp, sd_done, st.n - (U - 1), e.sp_passed)
                        sp.dma_start(hd[i][:, :], e.XH1[0:D, bass.ds(at, GE)]).then_inc(hd_in[i], 16)
                        sp.dma_start(same[i][:, :], over_parts(e.same_next, at, D)).then_inc(same_in[i], 16)
                    b = st.back(4)
                    if b.on():
                        wait(sp, b_kept, b.n + 1, e.sp_passed)
                        sp.dma_start(edge_rows(e.SD, pos(b) * GE), sdr[b.s][:, :, :]).then_inc(sd_out[b.s], 16)
                run_groups(sp, body, U, 4)
                for i in range(U):
                    wait(sp, sd_out[i], 16 * (NG // U), e.sp_passed)

            @block.vector
            def _(v):
                v.memset(nacc[D:P, :, :], 0.0).then_inc(cleared, 1)

                def body(st):
                    b = st.back(1)
                    if b.on():
                        v.wait_ge(turned, b.n + 1)
                        wait(v, b_ready, b.n - (U - 1))
                        v.tensor_tensor(diff[:, :], ps_t[b.s][:, :], hb[b.s][:, :], ALU.subtract).then_inc(diff_done, 1)
                    if st.on():
                        i = st.s
                        v.wait_ge(hd_in[i], 16 * (st.k + 1))
                        v.wait_ge(same_in[i], 16 * (st.k + 1))
                        v.scalar_tensor_tensor(out=lastv[:, :], in0=same[i][:, :], scalar=-1.0, in1=hd[i][:, :],
                                               op0=ALU.add, op1=ALU.mult).then_inc(last_done, 1)
                    if b.on():
                        v.wait_ge(diff_done, b.n + 1)
                        v.tensor_tensor_scan(sd[b.s][:, ::-1], same[b.s][:, ::-1], diff[:, ::-1],
                                             0.0 if b.first() else sd[(b.s - 1) % U][:, 0:1],
                                             ALU.mult, ALU.add).then_inc(sd_done, 1)
                    if st.on():
                        v.wait_ge(last_done, st.n + 1)
                        wait(v, sq2, st.n - (U - 1))
                        v.tensor_tensor_scan(hb[i][:, ::-1], same[i][:, ::-1], lastv[:, ::-1],
                                             0.0 if st.first() else hb[(i - 1) % U][:, 0:1],
                                             ALU.mult, ALU.subtract).then_inc(hb_done, 1)
                    if b.on():
                        v.tensor_tensor(prod[b.s][:, :], ps_t[b.s][:, :], hb[b.s][:, :], ALU.mult).then_inc(prod_done, 1)
                    if st.on():
                        v.wait_ge(hb_done, st.n + 1)
                    if b.on():
                        v.wait_ge(sd_done, b.n + 1)
                run_groups(v, body, U, 1)
                n = [0]

                def link(ins):
                    n[0] += 1
                    ins.then_inc(fin, 1)
                    v.wait_ge(fin, n[0])

                v.wait_ge(sq1, NG)
                v.wait_ge(sq2, NG)
                v.tensor_reduce(ntot[:, :], nacc[:, :, :], AX, ALU.add).then_inc(tot_done, 1)
                v.wait_ge(rooted, 1)
                link(v.tensor_tensor(scale[:, :], nsq[:, 0:1], nsq[:, 1:2], ALU.mult))
                link(v.tensor_scalar(scale[:, :], scale[:, :], 1e-6, None, ALU.add))
                link(v.reciprocal(scale[:, :], scale[:, :]))
                v.wait_ge(c_kept, NG)
                link(v.tensor_scalar(e.gate[:, :], e.gate[:, :], scale[:, 0:1], -5.0, ALU.mult, ALU.max))
                v.tensor_scalar(e.gate[:, :], e.gate[:, :], 5.0, None, ALU.min).then_inc(clip_done, 1)
                v.wait_ge(gate_done, 1)
                v.tensor_tensor(e.gate[:, :], e.gate[:, :], e.has[:, :], ALU.mult)

            @block.scalar
            def _(a):
                def body(st):
                    b = st.back(2)
                    if b.on():
                        a.wait_ge(p_ready, b.n + 1)
                        a.activation(act[:, :], ps_p[:, :], ACT.Relu).then_inc(relu_done, 1)
                    if st.on():
                        a.wait_ge(gathered[st.s], 16 * TU * (st.k + 1))
                        wait(a, sq1, st.n)
                        a.activation(junk_s[:, :, :], hs[st.s][:, :, :], ACT.Square,
                                     accum_out=nacc[:, 0, bass.ds(st.n, 1)]).then_inc(sq1, 1)
                    if b.on():
                        a.wait_ge(b_ready, b.n + 1)
                        wait(a, sd_out[b.s], 16 * b.k)
                        a.copy(sdr[b.s][:, :, :], ps_b[:, :, :]).then_inc(b_kept, 1)
                    if st.on():
                        a.wait_ge(hb_done, st.n + 1)
                        wait(a, sq2, st.n)
                        a.activation(junk_d[:, :], hb[st.s][:, :], ACT.Square,
                                     accum_out=nacc[0:D, 1, bass.ds(st.n, 1)]).then_inc(sq2, 1)
                    if b.on():
                        a.wait_ge(c_ready, b.n + 1)
                        a.copy(e.gate[:, bass.ds(pos(b) * TU, TU)], ps_c[:, :]).then_inc(c_kept, 1)
                a.wait_ge(cleared, 1)
                run_groups(a, body)
                a.wait_ge(n_ready, 1)
                a.activation(nsq[:, :], ps_n[:, :], ACT.Sqrt).then_inc(rooted, 1)
                a.wait_ge(clip_done, 1)
                a.activation(e.gate[:, :], e.gate[:, :], ACT.Exp).then_inc(gate_done, 1)

            @block.tensor
            def _(pe):
                def body(st):
                    b = st.back(2)
                    if b.on():
                        wait(pe, prod_done, b.n + 1, e.pe_passed)
                        wait(pe, relu_done, b.n, e.pe_passed)
                        pe.matmul(ps_p[:, :], e.W["proj"][0:D, :], prod[b.s][:, :], start=True, stop=True).then_inc(p_ready, 1)
                        wait(pe, sd_done, b.n + 1, e.pe_passed)
                        wait(pe, b_kept, b.n, e.pe_passed)
                        for u in range(TU):
                            m = pe.transpose(ps_b[:, u, :], sd[b.s][:, u * P:(u + 1) * P], e.C["ident"][0:D, 0:D])
                        m.then_inc(b_ready, 1)
                    if st.on():
                        i = st.s
                        wait(pe, gathered[i], 16 * TU * (st.k + 1), e.pe_passed)
                        wait(pe, prod_done, st.n - (U - 1), e.pe_passed)
                        for u in range(TU):
                            m = pe.transpose(ps_t[i][:, u * P:(u + 1) * P], hs[i][:, u, :], e.C["ident"])
                        m.then_inc(turned, 1)
                    if b.on():
                        wait(pe, relu_done, b.n + 1, e.pe_passed)
                        wait(pe, c_kept, b.n, e.pe_passed)
                        for u in range(TU):
                            m = pe.matmul(ps_c[:, u:u + 1], act[:, u * P:(u + 1) * P], e.C["ones"][0:D, 0:1],
                                          start=(u == 0), stop=(u == TU - 1), skip_group_check=True)
                        m.then_inc(c_ready, 1)
                run_groups(pe, body)
                wait(pe, tot_done, 1, e.pe_passed)
                pe.matmul(ps_n[:, :], e.C["ones"], ntot[:, :], start=True, stop=True).then_inc(n_ready, 1)


def propagate(nc, e):
    with ExitStack() as ctx:
        s = Scope(nc, ctx, "pr")
        idx = [s.sb(f"idx{i}", [P, TU], I32) for i in range(U)]
        gat = [s.sb(f"gat{i}", [P, TU, D]) for i in range(U)]
        gm = [s.sb(f"gm{i}", [P, TU, D]) for i in range(U)]
        same = [s.sb(f"same{i}", [D, GE]) for i in range(U)]
        x1 = [s.sb(f"x1{i}", [D, GE]) for i in range(U)]
        agg = [s.sb(f"agg{i}", [D, GE]) for i in range(U)]
        ffn = [s.sb(f"ffn{i}", [D, GE]) for i in range(U)]
        x2 = [s.sb(f"x2{i}", [D, GE]) for i in range(U)]
        h2 = [s.sb(f"h2{i}", [P, TU, D]) for i in range(U)]
        ps_t, ps_x = [s.ps(f"t{i}", [D, GE]) for i in range(U)], [s.ps(f"x{i}", [P, TU, D]) for i in range(U)]
        ps_f = s.ps("f", [D, GE])
        nrm = s.norm("n", TU)
        gathered, same_in, x1_in, x2_out, h2_out = [s.sems(n) for n in ("g", "sa", "x1", "x2", "h2")]
        idx_c, gm_done, turned, agg_done, f_ready, relu_done, x2_done, x_ready, h_done = [
            s.sem(n) for n in ("ic", "gm", "tu", "ag", "fr", "rd", "xd", "xr", "hd")]

        with nc.Block() as block:
            @block.gpsimd
            def _(pool):
                def body(st):
                    b = st.back(1)
                    if st.on():
                        copy_index(e, pool, e.idxsd, idx, gathered, idx_c, st, st.n)
                    if b.on():
                        wait(pool, gm_done, b.n - (U - 1), e.pool_passed)
                        gather(e, pool, e.SD, idx, gat, gathered, idx_c, b, EP)
                run_groups(pool, body, U, 1)

            @block.sync
            def _(sp):
                def body(st):
                    b = st.back(1)
                    if b.on():
                        wait(sp, agg_done, b.n - (U - 1), e.sp_passed)
                        sp.dma_start(same[b.s][:, :], over_parts(e.same_prev, b.n * GE, D)).then_inc(same_in[b.s], 16)
                    b = st.back(3)
                    if b.on():
                        wait(sp, x2_done, b.n - (U - 1), e.sp_passed)
                        sp.dma_start(x1[b.s][:, :], e.XH1[D:P, bass.ds(b.n * GE, GE)]).then_inc(x1_in[b.s], 16)
                    b = st.back(5)
                    if b.on():
                        wait(sp, x2_done, b.n + 1, e.sp_passed)
                        sp.dma_start(e.X2T[:, bass.ds(b.n * GE, GE)], x2[b.s][:, :]).then_inc(x2_out[b.s], 16)
                run_groups(sp, body, U, 5)
                for i in range(U):
                    wait(sp, x2_out[i], 16 * (NG // U), e.sp_passed)

            @block.vector
            def _(v):
                def body(st):
                    b, f, g = st.back(2), st.back(4), st.back(6)
                    c = Chain(v, nrm.chain, g, 2)
                    if g.on():
                        v.wait_ge(x_ready, g.n + 1)
                        c.put(nrm.total(v, ps_x[g.s][:, :, :]))
                    if b.on():
                        i = b.s
                        v.wait_ge(turned, b.n + 1)
                        v.wait_ge(same_in[i], 16 * (b.k + 1))
                        wait(v, agg_done, b.n)
                        wait(v, f_ready, b.n - (U - 1))
                        v.tensor_tensor_scan(agg[i][:, :], same[i][:, :], ps_t[i][:, :],
                                             0.0 if b.first() else agg[(i - 1) % U][:, GE - 1:GE],
                                             ALU.mult, ALU.add).then_inc(agg_done, 1)
                    if g.on():
                        c.join()
                        nrm.shift(v, ps_x[g.s][:, :, :])
                    if f.on():
                        v.wait_ge(relu_done, f.n + 1)
                        v.wait_ge(x1_in[f.s], 16 * (f.k + 1))
                        wait(v, x2_out[f.s], 16 * f.k)
                        wait(v, x_ready, f.n - (U - 1))
                        v.tensor_tensor(x2[f.s][:, :], ffn[f.s][:, :], x1[f.s][:, :], ALU.add).then_inc(x2_done, 1)
                    if g.on():
                        nrm.sumsq(v, g)
                    if st.on():
                        i = st.s
                        v.wait_ge(gathered[i], 16 * TU * (st.k + 1))
                        wait(v, turned, st.n - (U - 1))
                        v.tensor_tensor(gm[i][:, :, :], gat[i][:, :, :],
                                        e.gate[:, bass.ds(st.n * TU, TU)].unsqueeze(2).broadcast_to([P, TU, D]),
                                        ALU.mult).then_inc(gm_done, 1)
                    if g.on():
                        nrm.recip(v, c, g)
                        wait(v, h2_out[g.s], 16 * g.k)
                        nrm.relu_to(v, h2[g.s][:, :, :]).then_inc(h_done, 1)
                        c.end()
                run_groups(v, body, U, 6)

            @block.scalar
            def _(a):
                def body(st):
                    b, g = st.back(3), st.back(6)
                    if g.on():
                        nrm.square(a, g)
                        nrm.root(a, g, e.C["eps"])
                    if b.on():
                        a.wait_ge(f_ready, b.n + 1)
                        wait(a, x2_done, b.n - (U - 1))
                        a.activation(ffn[b.s][:, :], ps_f[:, :], ACT.Relu, bias=e.W["bffn"][0:D, :]).then_inc(relu_done, 1)
                    if g.on():
                        a.wait_ge(h_done, g.n + 1)
                        a.dma_start(edge_rows(e.U2, g.n * GE), h2[g.s][:, :, :]).then_inc(h2_out[g.s], 16)
                run_groups(a, body, U, 6)
                for i in range(U):
                    a.wait_ge(h2_out[i], 16 * (NG // U))

            @block.tensor
            def _(pe):
                def body(st):
                    d, f, x = st.back(1), st.back(3), st.back(5)
                    if d.on():
                        i = d.s
                        wait(pe, gm_done, d.n + 1, e.pe_passed)
                        wait(pe, agg_done, d.n - (U - 1), e.pe_passed)
                        for u in range(TU):
                            m = pe.transpose(ps_t[i][:, u * P:(u + 1) * P], gm[i][:, u, :], e.C["ident"])
                        m.then_inc(turned, 1)
                    if f.on():
                        wait(pe, agg_done, f.n + 1, e.pe_passed)
                        wait(pe, relu_done, f.n, e.pe_passed)
                        pe.matmul(ps_f[:, :], e.W["ffnT"][0:D, :], agg[f.s][:, :], start=True, stop=True).then_inc(f_ready, 1)
                    if x.on():
                        wait(pe, x2_done, x.n + 1, e.pe_passed)
                        wait(pe, nrm.centered, x.n - (U - 1), e.pe_passed)
                        for u in range(TU):
                            m = pe.transpose(ps_x[x.s][:, u, :], x2[x.s][:, u * P:(u + 1) * P], e.C["ident"][0:D, 0:D])
                        m.then_inc(x_ready, 1)
                run_groups(pe, body, U, 5)


def mlp(nc, e):
    with ExitStack() as ctx:
        s = Scope(nc, ctx, "ml")
        idx = [s.sb(f"idx{i}", [P, TU], I32) for i in range(U)]
        gat = [s.sb(f"gat{i}", [P, TU, D]) for i in range(U)]
        own = [s.sb(f"own{i}", [P, TU, D]) for i in range(U)]
        same = [s.sb(f"same{i}", [D, GE]) for i in range(U)]
        x2 = [s.sb(f"x2{i}", [D, GE]) for i in range(U)]
        agg = [s.sb(f"agg{i}", [D, GE]) for i in range(U)]
        hh = [s.sb(f"hh{i}", [D, GE]) for i in range(U)]
        hid = s.sb("hid", [P, GE])
        x3 = [s.sb(f"x3{i}", [D, GE]) for i in range(U)]
        hx = [s.sb(f"hx{i}", [P, TU, 2 * D]) for i in range(U)]
        xh = [s.sb(f"xh{i}", [P, GE]) for i in range(U)]
        ps_t = [s.ps(f"t{i}", [D, GE]) for i in range(U)]
        ps_o, ps_1, ps_2, ps_x, ps_h = (s.ps("o", [D, GE]), s.ps("h1", [P, GE]), s.ps("h2", [D, GE]),
                                        s.ps("x", [P, TU, D]), s.ps("h", [P, GE]))
        last = s.sb("last", [P, CH])
        nrm = s.norm("n", TU)
        gathered, own_in, same_in, x2_in, h_out, xh_out = [s.sems(n) for n in ("g", "own", "sa", "x2", "ho", "xo")]
        idx_c, t_ready, o_ready, agg_done, hh_done, h1_ready, hid_done, h2_ready, x3_done = [
            s.sem(n) for n in ("ic", "tr", "or", "ag", "hh", "h1", "hid", "h2", "x3")]
        x_ready, x_kept, h_done, hx_turned, kept, last_done = [s.sem(n) for n in ("xr", "xk", "hd", "ht", "kp", "ld")]

        with nc.Block() as block:
            @block.gpsimd
            def _(pool):
                def body(st):
                    b = st.back(1)
                    if st.on():
                        copy_index(e, pool, e.idx2, idx, gathered, idx_c, st, st.n)
                    if b.on():
                        wait(pool, t_ready, b.n - (U - 1), e.pool_passed)
                        gather(e, pool, e.U2, idx, gat, gathered, idx_c, b, EP + NP)
                run_groups(pool, body, U, 1)

            @block.sync
            def _(sp):
                def body(st):
                    if st.on():
                        i, at = st.s, st.n * GE
                        wait(sp, o_ready, st.n - (U - 1), e.sp_passed)
                        sp.dma_start(own[i][:, :, :], edge_rows(e.U2, at)).then_inc(own_in[i], 16)
                        wait(sp, agg_done, st.n - (U - 1), e.sp_passed)
                        sp.dma_start(same[i][:, :], over_parts(e.same_prev, at, D)).then_inc(same_in[i], 16)
                    b = st.back(2)
                    if b.on():
                        wait(sp, x3_done, b.n - (U - 1), e.sp_passed)
                        sp.dma_start(x2[b.s][:, :], e.X2T[:, bass.ds(b.n * GE, GE)]).then_inc(x2_in[b.s], 16)
                run_groups(sp, body, U, 2)

            @block.vector
            def _(v):
                v.tensor_scalar(last[:, :], e.scat_ptr[:, :], FAR, None, ALU.is_lt).then_inc(last_done, 1)
                v.wait_ge(last_done, 1)

                def body(st):
                    b, f, g = st.back(1), st.back(3), st.back(5)
                    c = Chain(v, nrm.chain, g, 2)
                    if g.on():
                        v.wait_ge(x_ready, g.n + 1)
                        wait(v, hx_turned, g.n - (U - 1))
                        v.tensor_tensor(hx[g.s][:, :, D:2 * D], ps_x[:, :, :],
                                        last[:, bass.ds(g.n * TU, TU)].unsqueeze(2).broadcast_to([P, TU, D]),
                                        ALU.mult).then_inc(x_kept, 1)
                    if f.on():
                        v.wait_ge(h2_ready, f.n + 1)
                        v.wait_ge(x2_in[f.s], 16 * (f.k + 1))
                        wait(v, x_ready, f.n - (U - 1))
                        v.scalar_tensor_tensor(out=x3[f.s][:, :], in0=ps_2[:, :], scalar=e.W["b1"][0:D, :], in1=x2[f.s][:, :],
                                               op0=ALU.add, op1=ALU.add).then_inc(x3_done, 1)
                    if g.on():
                        v.wait_ge(x_kept, g.n + 1)
                        c.link(nrm.total(v, hx[g.s][:, :, D:2 * D]))
                        nrm.shift(v, hx[g.s][:, :, D:2 * D])
                    if b.on():
                        i = b.s
                        v.wait_ge(t_ready, b.n + 1)
                        v.wait_ge(same_in[i], 16 * (b.k + 1))
                        v.tensor_tensor_scan(agg[i][:, :], same[i][:, :], ps_t[i][:, :],
                                             0.0 if b.first() else agg[(i - 1) % U][:, GE - 1:GE],
                                             ALU.mult, ALU.add).then_inc(agg_done, 1)
                    if g.on():
                        nrm.sumsq(v, g)
                    if b.on():
                        v.wait_ge(agg_done, b.n + 1)
                        v.wait_ge(o_ready, b.n + 1)
                        wait(v, h1_ready, b.n - (U - 1))
                        v.tensor_tensor(hh[i][:, :], ps_o[:, :], agg[i][:, :], ALU.add).then_inc(hh_done, 1)
                    if g.on():
                        nrm.recip(v, c, g)
                        wait(v, h_out[g.s], 16 * g.k)
                        nrm.relu_to(v, hx[g.s][:, :, 0:D]).then_inc(h_done, 1)
                        c.end()
                run_groups(v, body, U, 5)

            @block.scalar
            def _(a):
                def body(st):
                    d, g, t = st.back(2), st.back(5), st.back(6)
                    if t.on():
                        a.dma_start(edge_rows(e.U3, t.n * GE), hx[t.s][:, :, 0:D]).then_inc(h_out[t.s], 16)
                    if d.on():
                        a.wait_ge(h1_ready, d.n + 1)
                        a.activation(hid[:, :], ps_1[:, :], ACT.Relu, bias=e.W["b0"]).then_inc(hid_done, 1)
                    if t.on():
                        a.wait_ge(hx_turned, t.n + 1)
                        wait(a, xh_out[t.s], 16 * t.k)
                        a.copy(xh[t.s][:, :], ps_h[:, :]).then_inc(kept, 1)
                    if g.on():
                        nrm.square(a, g)
                    if t.on():
                        a.wait_ge(kept, t.n + 1)
                        a.dma_start(e.XH3[:, bass.ds(t.n * GE, GE)], xh[t.s][:, :]).then_inc(xh_out[t.s], 16)
                    if g.on():
                        nrm.root(a, g, e.C["eps"])
                    if g.on():
                        a.wait_ge(h_done, g.n + 1)
                run_groups(a, body, U, 6)
                for sems in (h_out, xh_out):
                    for i in range(U):
                        a.wait_ge(sems[i], 16 * (NG // U))

            @block.tensor
            def _(pe):
                def body(st):
                    d, x, t = st.back(2), st.back(4), st.back(6)
                    if d.on():
                        wait(pe, hh_done, d.n + 1, e.pe_passed)
                        wait(pe, hid_done, d.n, e.pe_passed)
                        pe.matmul(ps_1[:, :], e.W["w0"][0:D, :], hh[d.s][:, :], start=True, stop=True).then_inc(h1_ready, 1)
                    if t.on():
                        wait(pe, h_done, t.n + 1, e.pe_passed)
                        wait(pe, kept, t.n, e.pe_passed)
                        for u in range(TU):
                            m = pe.transpose(ps_h[:, u * P:(u + 1) * P], hx[t.s][:, u, :], e.C["ident"])
                        m.then_inc(hx_turned, 1)
                    if st.on():
                        i = st.s
                        wait(pe, gathered[i], 16 * TU * (st.k + 1), e.pe_passed)
                        wait(pe, agg_done, st.n - (U - 1), e.pe_passed)
                        for u in range(TU):
                            m = pe.transpose(ps_t[i][:, u * P:(u + 1) * P], gat[i][:, u, :], e.C["ident"])
                        m.then_inc(t_ready, 1)
                    if d.on():
                        wait(pe, hid_done, d.n + 1, e.pe_passed)
                        wait(pe, x3_done, d.n, e.pe_passed)
                        pe.matmul(ps_2[:, :], e.W["w1"], hid[:, :], start=True, stop=True).then_inc(h2_ready, 1)
                    if x.on():
                        wait(pe, x3_done, x.n + 1, e.pe_passed)
                        wait(pe, x_kept, x.n, e.pe_passed)
                        for u in range(TU):
                            m = pe.transpose(ps_x[:, u, :], x3[x.s][:, u * P:(u + 1) * P], e.C["ident"][0:D, 0:D])
                        m.then_inc(x_ready, 1)
                    if st.on():
                        wait(pe, own_in[i], 16 * (st.k + 1), e.pe_passed)
                        wait(pe, hh_done, st.n, e.pe_passed)
                        for u in range(TU):
                            m = pe.transpose(ps_o[:, u * P:(u + 1) * P], own[i][:, u, :], e.C["ident"])
                        m.then_inc(o_ready, 1)
                run_groups(pe, body, U, 6)


def heads(nc, e):
    with ExitStack() as ctx:
        s = Scope(nc, ctx, "hd")
        idx = [s.sb(f"idx{i}", [P, TU], I32) for i in range(U)]
        oidx = [s.sb(f"oidx{i}", [P, TU], I32) for i in range(U)]
        gat = [s.sb(f"gat{i}", [P, TU, D]) for i in range(U)]
        xl = [s.sb(f"xl{i}", [P, GE]) for i in range(U)]
        same = [s.sb(f"same{i}", [P, GE]) for i in range(U)]
        xb = [s.sb(f"xb{i}", [P, GE]) for i in range(U)]
        ht = s.sb("ht", [D, GE])
        qt = [s.sb(f"qt{i}", [D, GE]) for i in range(U)]
        vt = [s.sb(f"vt{i}", [D, GE]) for i in range(U)]
        prod = s.sb("prod", [D, GE])
        clip = s.sb("clip", [P, GE])
        wz = [s.sb(f"wz{i}", [P, GE]) for i in range(U)]
        wv = [s.sb(f"wv{i}", [P, GE]) for i in range(U)]
        lnz = s.sb("lnz", [P, GE])
        rz = s.sb("rz", [P, GE])
        tz = s.sb("tz", [P, GE])
        rn = s.sb("rn", [D, GE])
        wn = [s.sb(f"wn{i}", [P, GE]) for i in range(U)]
        f1 = s.sb("f1", [P, TU, D])
        x4 = [s.sb(f"x4{i}", [P, TU, D]) for i in range(U)]
        ps_t, ps_q, ps_k, ps_v, ps_s = s.ps("t", [D, GE]), s.ps("q", [D, GE]), s.ps("k", [D, GE]), s.ps("v", [D, GE]), s.ps("s", [P, GE])
        ps_h = [s.ps(f"h{i}", [P, TU, 2 * D]) for i in range(U)]
        nrm = s.norm("n", TU)
        gathered, xl_in, same_in, x4_out = [s.sems(n) for n in ("g", "xl", "sa", "xo")]
        (idx_c, oidx_c, turned, ht_kept, xb_done, k_ready, q_ready, v_ready, q_kept, v_kept, prod_done, s_ready, clip_done,
         w_done, wz_done, wv_done, lnz_done, rz_done, tz_done, rn_done, wn_done, h_ready, x4_done, lnc, ones_in) = [
            s.sem(n) for n in ("ic", "oc", "tu", "htk", "xb", "kr", "qr", "vr", "qk", "vk", "pd", "sr", "cl", "wd",
                               "wzd", "wvd", "lz", "rz", "tz", "rn", "wn", "hr", "x4", "ln", "on")]
        pos = lambda st: st.n * -1 + (NG - 1)

        with nc.Block() as block:
            @block.gpsimd
            def _(pool):
                def body(st):
                    g, c = st.back(1), st.back(5)
                    if st.on():
                        copy_index(e, pool, e.idx2, idx, gathered, idx_c, st, pos(st))
                    if c.on():
                        copy_index(e, pool, e.scat_out, oidx, x4_out, oidx_c, c, pos(c))
                    if g.on():
                        wait(pool, turned, g.n - (U - 1), e.pool_passed)
                        gather(e, pool, e.U3, idx, gat, gathered, idx_c, g, EP + NP)
                    b = st.back(6)
                    if b.on():
                        i = b.s
                        wait(pool, oidx_c, b.n + 1, e.pool_passed)
                        wait(pool, x4_done, b.n + 1, e.pool_passed)
                        for u in range(TU):
                            pool.indirect_dma_start(e.out, bass.IndirectOffsetOnAxis(ap=oidx[i][:, u:u + 1], axis=0),
                                                    x4[i][:, u, :], None, bounds_check=NP - 1,
                                                    oob_is_err=False).then_inc(x4_out[i], 16)
                run_groups(pool, body, U, 6)
                for i in range(U):
                    wait(pool, x4_out[i], 16 * TU * (NG // U), e.pool_passed)

            @block.sync
            def _(sp):
                def body(st):
                    if st.on():
                        i, at = st.s, pos(st) * GE
                        wait(sp, xb_done, st.n - (U - 1), e.sp_passed)
                        sp.dma_start(xl[i][:, :], e.XH3[:, bass.ds(at, GE)]).then_inc(xl_in[i], 16)
                        wait(sp, wv_done, st.n - (U - 1), e.sp_passed)
                        sp.dma_start(same[i][:, :], over_parts(e.same_next, at, P)).then_inc(same_in[i], 16)
                run_groups(sp, body, U, 0)

            @block.vector
            def _(v):
                for i in range(U):
                    v.memset(wn[i][D:P, :], 1.0).then_inc(ones_in, 1)

                def body(st):
                    b, c, g = st.back(1), st.back(2), st.back(4)
                    ch = Chain(v, nrm.chain, g, 3)
                    if c.on():
                        i = c.s
                        v.wait_ge(w_done, c.n + 1)
                        v.wait_ge(v_kept, c.n + 1)
                        v.tensor_tensor(wz[i][0:D, :], vt[i][:, :], wz[i][0:D, :], ALU.mult).then_inc(wz_done, 1)
                    if b.on():
                        v.wait_ge(k_ready, b.n + 1)
                        v.wait_ge(q_kept, b.n + 1)
                        wait(v, s_ready, b.n)
                        v.scalar_tensor_tensor(out=prod[:, :], in0=ps_k[:, :], scalar=e.W["bk"][0:D, :], in1=qt[b.s][:, :],
                                               op0=ALU.add, op1=ALU.mult).then_inc(prod_done, 1)
                    if c.on():
                        v.wait_ge(wz_done, c.n + 1)
                        wait(v, wn_done, c.n - (U - 1))
                        v.tensor_tensor_scan(wv[i][:, ::-1], same[i][:, ::-1], wz[i][:, ::-1],
                                             0.0 if c.first() else wv[(i - 1) % U][:, 0:1],
                                             ALU.mult, ALU.add).then_inc(wv_done, 1)
                    if st.on():
                        j = st.s
                        v.wait_ge(xl_in[j], 16 * (st.k + 1))
                        v.wait_ge(same_in[j], 16 * (st.k + 1))
                        wait(v, h_ready, st.n - (U - 1))
                        wait(v, xb_done, st.n)
                        v.tensor_tensor_scan(xb[j][:, ::-1], same[j][:, ::-1], xl[j][:, ::-1],
                                             0.0 if st.first() else xb[(j - 1) % U][:, 0:1],
                                             ALU.mult, ALU.add).then_inc(xb_done, 1)
                    if g.on():
                        nrm.sumsq(v, g)
                    if b.on():
                        v.wait_ge(s_ready, b.n + 1)
                        wait(v, w_done, b.n)
                        v.tensor_scalar(clip[:, :], ps_s[:, :], 5.0, -5.0, ALU.min, ALU.max).then_inc(clip_done, 1)
                    if g.on():
                        nrm.recip(v, ch, g)
                        ch.put(v.tensor_tensor(f1[:, :, :], ps_h[g.s][:, :, 0:D], nrm.over(nrm.rstd), ALU.mult))
                    if c.on():
                        v.wait_ge(rz_done, c.n + 1)
                        wait(v, rn_done, c.n)
                        v.scalar_tensor_tensor(out=tz[D:P, :], in0=wv[i][D:P, :], scalar=1.0, in1=rz[D:P, :],
                                               op0=ALU.add, op1=ALU.mult).then_inc(tz_done, 1)
                    if g.on():
                        ch.join()
                        ch.put(v.tensor_tensor(f1[:, :, :], f1[:, :, :],
                                               e.W["gamma"].unsqueeze(1).broadcast_to([P, TU, D]), ALU.mult))
                    if c.on():
                        v.wait_ge(tz_done, c.n + 1)
                        v.scalar_tensor_tensor(out=rn[:, :], in0=tz[D:P, :], scalar=-2.0, in1=rz[D:P, :],
                                               op0=ALU.add, op1=ALU.mult).then_inc(rn_done, 1)
                    if g.on():
                        ch.join()
                        wait(v, x4_out[g.s], 16 * TU * g.k)
                        v.tensor_tensor(x4[g.s][:, :, :], f1[:, :, :], ps_h[g.s][:, :, D:2 * D], ALU.add).then_inc(x4_done, 1)
                        ch.end()
                    if c.on():
                        v.wait_ge(rn_done, c.n + 1)
                        wait(v, h_ready, c.n - (U - 1))
                        v.scalar_tensor_tensor(out=wn[i][0:D, :], in0=wv[i][0:D, :], scalar=-1.0, in1=rn[:, :],
                                               op0=ALU.mult, op1=ALU.mult).then_inc(wn_done, 1)
                run_groups(v, body, U, 4)

            @block.scalar
            def _(a):
                a.preload_act_table_set("natural_log_exp_and_others")

                def body(st):
                    b, c, g = st.back(1), st.back(2), st.back(4)
                    if g.on():
                        a.wait_ge(h_ready, g.n + 1)
                        wait(a, nrm.summed, g.n)
                        a.activation(nrm.sq[:, :, :], ps_h[g.s][:, :, 0:D], ACT.Square).then_inc(nrm.squared, 1)
                    if st.on():
                        a.wait_ge(turned, st.n + 1)
                        wait(a, v_ready, st.n)
                        a.copy(ht[:, :], ps_t[:, :]).then_inc(ht_kept, 1)
                    if c.on():
                        a.wait_ge(wv_done, c.n + 1)
                        a.activation(lnz[D:P, :], wv[c.s][D:P, :], ACT.Ln, bias=e.C["ones"][D:P, 0:1]).then_inc(lnz_done, 1)
                    if g.on():
                        a.wait_ge(nrm.summed, g.n + 1)
                        a.activation(nrm.std[:, :], nrm.ss[:, :], ACT.Ln, bias=e.C["eps"], scale=1.0 / D).then_inc(lnc, 1)
                    if c.on():
                        a.wait_ge(lnz_done, c.n + 1)
                        wait(a, rn_done, c.n)
                        a.activation(rz[D:P, :], lnz[D:P, :], ACT.Exp, scale=-1.0).then_inc(rz_done, 1)
                    if g.on():
                        a.wait_ge(lnc, g.n + 1)
                        a.activation(nrm.std[:, :], nrm.std[:, :], ACT.Exp, scale=0.5).then_inc(nrm.rooted, 1)
                    if st.on():
                        a.wait_ge(q_ready, st.n + 1)
                        wait(a, prod_done, st.n - (U - 1))
                        a.activation(qt[st.s][:, :], ps_q[:, :], ACT.Identity, bias=e.bq8[0:D, :], scale=1.0 / 8.0).then_inc(q_kept, 1)
                    if b.on():
                        a.wait_ge(clip_done, b.n + 1)
                        wait(a, wv_done, b.n - (U - 1))
                        a.activation(wz[b.s][:, :], clip[:, :], ACT.Exp).then_inc(w_done, 1)
                    if st.on():
                        a.wait_ge(v_ready, st.n + 1)
                        wait(a, wz_done, st.n - (U - 1))
                        a.activation(vt[st.s][:, :], ps_v[:, :], ACT.Identity, bias=e.W["bv"][0:D, :]).then_inc(v_kept, 1)
                run_groups(a, body, U, 4)

            @block.tensor
            def _(pe):
                wait(pe, ones_in, U)

                def body(st):
                    b, f = st.back(1), st.back(3)
                    if f.on():
                        i = f.s
                        wait(pe, wn_done, f.n + 1, e.pe_passed)
                        wait(pe, x4_done, f.n - (U - 1), e.pe_passed)
                        for u in range(TU):
                            pe.matmul(ps_h[i][:, u, :], xb[i][:, u * P:(u + 1) * P], e.W["wfx"], start=(u == 0),
                                      stop=False, skip_group_check=True)
                            m = pe.matmul(ps_h[i][:, u, :], wn[i][:, u * P:(u + 1) * P], e.W["wob"], start=False,
                                          stop=(u == TU - 1), skip_group_check=True)
                        m.then_inc(h_ready, 1)
                    if st.on():
                        i = st.s
                        wait(pe, gathered[i], 16 * TU * (st.k + 1), e.pe_passed)
                        wait(pe, ht_kept, st.n, e.pe_passed)
                        for u in range(TU):
                            m = pe.transpose(ps_t[:, u * P:(u + 1) * P], gat[i][:, u, :], e.C["ident"])
                        m.then_inc(turned, 1)
                    if b.on():
                        wait(pe, prod_done, b.n + 1, e.pe_passed)
                        wait(pe, clip_done, b.n, e.pe_passed)
                        pe.matmul(ps_s[:, :], e.C["heads"][0:D, :], prod[:, :], start=True, stop=True).then_inc(s_ready, 1)
                    if st.on():
                        wait(pe, xb_done, st.n + 1, e.pe_passed)
                        wait(pe, q_kept, st.n, e.pe_passed)
                        pe.matmul(ps_q[:, :], e.W["wq"][0:D, :], xb[i][0:D, :], start=True, stop=True).then_inc(q_ready, 1)
                        wait(pe, ht_kept, st.n + 1, e.pe_passed)
                        wait(pe, prod_done, st.n, e.pe_passed)
                        pe.matmul(ps_k[:, :], e.W["wk"][0:D, :], ht[:, :], start=True, stop=True).then_inc(k_ready, 1)
                        wait(pe, v_kept, st.n, e.pe_passed)
                        pe.matmul(ps_v[:, :], e.W["wv"][0:D, :], ht[:, :], start=True, stop=True).then_inc(v_ready, 1)
                run_groups(pe, body, U, 3)


def constants():
    c = np.zeros((P, CONST_W), np.float32)
    put = lambda name, a: c.__setitem__((slice(0, a.shape[0]), slice(*CONST_AT[name])), a)
    put("ident", np.eye(P, dtype=np.float32))
    put("ones", np.ones((P, P), np.float32))
    f, m = np.arange(D)[:, None], np.arange(P)[None, :]
    put("heads", (f // 16 == (m % D) // 16).astype(np.float32))
    put("types", np.tile(np.arange(4, dtype=np.float32), (P, 1)))
    put("rels", (2 * np.arange(4)[None, :] + (np.arange(P)[:, None] >= D)).astype(np.float32))
    put("less_rels", -(2 * np.arange(4)[None, :] + (np.arange(P)[:, None] >= D)).astype(np.float32))
    put("eps", np.full((P, 1), EPS, np.float32))
    return c


def pack_weights(i):
    w = np.zeros((P, WEIGHT_W), np.float32)

    def put(name, a, row=0, col=0):
        a = np.asarray(a)
        at = WEIGHT_AT[name][0] + col
        w[row:row + a.shape[0], at:at + a.shape[1]] = a

    def pairs(name, a, col, width):
        for c in range(a.shape[0] // 2):
            put(name, a[2 * c:2 * c + 2].reshape(P, D), 0, c * width + col)

    q, k, v = (np.asarray(i[f"L0_gnn_{n}_lin"]) for n in "qkv")
    for half in range(2):
        pairs("q", q, half * D, P)
    pairs("kv", k, 0, P)
    pairs("kv", v, D, P)
    pairs("att", np.asarray(i["L0_gnn_rel_att"]), 0, D)
    pairs("msg", np.asarray(i["L0_gnn_rel_msg"]), 0, D)
    pri = np.asarray(i["L0_gnn_rel_pri"]).reshape(4, 2)
    put("pri", np.repeat(pri.T, D, axis=0))
    put("a", np.asarray(i["L0_gnn_a_lin"]).transpose(1, 0, 2).reshape(D, 4 * D))
    put("skip", np.tile(np.repeat(np.asarray(i["L0_gnn_skip"]), D)[None], (D, 1)))
    put("proj", i["L1_gnn_proj_cosim"])
    put("ffnT", np.asarray(i["L1_gnn_W_ffn"]).T)
    put("bffn", np.asarray(i["L1_gnn_b_ffn"])[:, None])
    put("bffn_row", np.tile(np.asarray(i["L1_gnn_b_ffn"])[None], (P, 1)))
    for half in range(2):
        put("w0", i["L2_gnn_W0"], half * D)
        for copy in range(2):
            put("wf2", i["L3_gnn_Wf"], half * D, half * P + copy * D)
    put("b0", np.asarray(i["L2_gnn_b0"])[:, None])
    put("w1", i["L2_gnn_W1"])
    put("b1", np.asarray(i["L2_gnn_b1"])[:, None])
    put("b1_row", np.tile(np.asarray(i["L2_gnn_b1"])[None], (P, 1)))
    for n in "qkv":
        put("w" + n, i[f"L3_gnn_W{n}"])
        put("b" + n, np.asarray(i[f"L3_gnn_b{n}"])[:, None])
    put("wo", i["L3_gnn_Wo"])
    put("bo_row", np.tile(np.asarray(i["L3_gnn_bo"])[None], (P, 1)))
    put("bf_row", np.tile(np.asarray(i["L3_gnn_bf"])[None], (P, 1)))
    for half in range(2):
        put("wfx", i["L3_gnn_Wf"], 0, half * D)
        put("wob", i["L3_gnn_Wo"], 0, half * D)
        put("wob", np.asarray(i["L3_gnn_bo"])[None], D, half * D)
        put("bf_64", np.asarray(i["L3_gnn_bf"])[None], D, half * D)
    put("wfx", np.eye(D, dtype=np.float32), D, D)
    put("beta_64", np.asarray(i["L3_gnn_beta"])[None], D)
    put("gamma", np.tile(np.asarray(i["L3_gnn_gamma"])[None], (P, 1)))
    put("beta", np.tile(np.asarray(i["L3_gnn_beta"])[None], (P, 1)))
    return w


def lay_out(i):
    def padded(a, n, fill):
        a = np.asarray(a)
        p = np.full((n,) + a.shape[1:], fill, a.dtype)
        p[:a.shape[0]] = a
        return p

    src, dst = padded(i["src"], EP, PADN), padded(i["dst"], EP, PADN)
    etype = padded(i["edge_type_8"], EP, 0)
    major = lambda a: np.ascontiguousarray(a.reshape(NG, TU, P).transpose(2, 0, 1))
    ntype = padded(i["node_type_4"], NP, 0).reshape(NG, P, RN).transpose(1, 0, 2).reshape(P, NG * RN)
    return {
        "x": padded(i["x"], NP, 0.0), "node_type": np.ascontiguousarray(ntype),
        "src_idx": major(src), "dst_idx": major(dst), "etype_row": etype,
        "dst_row": np.concatenate([np.full(1, -1, dst.dtype), dst, np.full(1, -1, dst.dtype)]),
        "edge_id": np.ascontiguousarray(np.arange(1, EP + 1, dtype=np.float32).reshape(CH, P).T),
        "chunk_id": np.arange(1, EP + 1, dtype=np.float32).reshape(P, CH),
        "consts": constants(), "weights": pack_weights(i),
    }


def kernel(**inputs):
    import concourse.bacc as bacc
    from concourse.bass_utils import run_bass_kernel_spmd

    arrays = lay_out(inputs)
    nc = bacc.Bacc("TRN2", target_bir_lowering=False, num_devices=1)
    aps = {n: nc.dram_tensor("in_" + n, a.shape, mybir.dt.from_np(a.dtype), kind="ExternalInput").ap()
           for n, a in arrays.items()}
    out = nc.dram_tensor("out_x", (NP, D), F32, kind="ExternalOutput").ap()
    build(nc, out=out, **aps)
    r = run_bass_kernel_spmd(nc, [{"in_" + n: a for n, a in arrays.items()}], core_ids=[0])
    return r.results[0]["out_x"][:NODES]
```
